# Optimizing a Trainium2 kernel written in Bass

```python
import numpy as np
import jax
import jax.numpy as jnp

def _softmax(x, axis=-1):
    return jax.nn.softmax(x, axis=axis)

def _gelu(x):
    return jax.nn.gelu(x, approximate=True)

def _silu(x):
    return jax.nn.silu(x)

def _sigmoid(x):
    return jax.nn.sigmoid(x)

def _layernorm(x, axis=-1, eps=1e-05):
    m = jnp.mean(x, axis=axis, keepdims=True)
    v = jnp.var(x, axis=axis, keepdims=True)
    return (x - m) / jnp.sqrt(v + eps)

def _scatter_add(tgt, idx, src, axis=0):
    return tgt.at[idx].add(src)

def _segment_sum(src, seg, n):
    return jax.ops.segment_sum(src, seg, n)
kernel_name = 'mk_hybrid_d2_jaxref_r8_1039fb'

def setup_inputs(seed: int=0):
    np.random.seed(seed)
    _w = jnp.asarray

    def _L0_attn_a_setup():
        import jax, jax.numpy as jnp
        import numpy as np
        HID = 128
        HK, HV = (4, 8)
        DK, DV = (128, 128)
        KEY_DIM = HK * DK
        VAL_DIM = HV * DV
        CONV_DIM = 2 * KEY_DIM + VAL_DIM
        KCONV = 4
        NEXP, TOPK, INTER = (8, 2, 64)
        EPS = 1e-06

        def zrms(x, w):
            v = jnp.mean(x * x, axis=-1, keepdims=True)
            return x * jax.lax.rsqrt(v + EPS) * (1.0 + w)

        def causal_dwconv(x, w):
            xp = jnp.pad(x, ((0, 0), (KCONV - 1, 0), (0, 0)))
            kern = w.T[:, None, :]
            return jax.lax.conv_general_dilated(xp, kern, (1,), 'VALID', dimension_numbers=('NHC', 'HIO', 'NHC'), feature_group_count=CONV_DIM)

        def gated_delta_rule(q, k, v, g, beta):
            B = q.shape[0]
            S0 = jnp.zeros((B, HV, DK, DV), q.dtype)

            def step(S, inp):
                qt, kt, vt, gt, bt = inp
                S = S * jnp.exp(gt)[..., None, None]
                kv = jnp.einsum('bhk,bhkv->bhv', kt, S)
                delta = (vt - kv) * bt[..., None]
                S = S + jnp.einsum('bhk,bhv->bhkv', kt, delta)
                o = jnp.einsum('bhk,bhkv->bhv', qt, S)
                return (S, o)
            xs = tuple((jnp.moveaxis(a, 1, 0) for a in (q, k, v, g, beta)))
            _, o = jax.lax.scan(step, S0, xs)
            return jnp.moveaxis(o, 0, 1)

        def _reference_tuple_inner(hidden_states, w_ln1, w_ln2, W_qkvz, W_ba, conv_w, dt_bias, A_log, gate_norm_w, W_out, W_router, W_gate_e, W_up_e, W_down_e):
            B, S, _ = hidden_states.shape
            resid = hidden_states
            x = zrms(hidden_states, w_ln1)
            qkvz = x @ W_qkvz
            q, k, v, z = jnp.split(qkvz, [KEY_DIM, 2 * KEY_DIM, 2 * KEY_DIM + VAL_DIM], axis=-1)
            b, a = jnp.split(x @ W_ba, 2, axis=-1)
            beta = jax.nn.sigmoid(b)
            g = -jnp.exp(A_log) * jax.nn.softplus(a + dt_bias)
            mixed = jnp.concatenate([q, k, v], axis=-1)
            mixed = jax.nn.silu(causal_dwconv(mixed, conv_w))
            q, k, v = jnp.split(mixed, [KEY_DIM, 2 * KEY_DIM], axis=-1)
            q = q.reshape(B, S, HK, DK)
            k = k.reshape(B, S, HK, DK)
            v = v.reshape(B, S, HV, DV)
            rep = HV // HK
            q = jnp.repeat(q, rep, axis=2)
            k = jnp.repeat(k, rep, axis=2)
            q = q * jax.lax.rsqrt(jnp.sum(q * q, -1, keepdims=True) + EPS)
            k = k * jax.lax.rsqrt(jnp.sum(k * k, -1, keepdims=True) + EPS)
            q = q * DK ** (-0.5)
            core = gated_delta_rule(q, k, v, g, beta)
            core = core * jax.lax.rsqrt(jnp.mean(core * core, -1, keepdims=True) + EPS) * gate_norm_w
            core = core * jax.nn.silu(z.reshape(B, S, HV, DV))
            h = resid + core.reshape(B, S, VAL_DIM) @ W_out
            resid = h
            x = zrms(h, w_ln2)
            probs = jax.nn.softmax(x @ W_router, axis=-1)
            topv, topi = jax.lax.top_k(probs, TOPK)
            topv = topv / jnp.sum(topv, -1, keepdims=True)
            route = jnp.sum(jax.nn.one_hot(topi, NEXP, dtype=x.dtype) * topv[..., None], axis=-2)
            gate_h = jnp.einsum('bsh,ehi->bsei', x, W_gate_e)
            up_h = jnp.einsum('bsh,ehi->bsei', x, W_up_e)
            exp_out = jnp.einsum('bsei,eih->bseh', jax.nn.silu(gate_h) * up_h, W_down_e)
            moe_out = jnp.einsum('bseh,bse->bsh', exp_out, route)
            return (resid + moe_out, topi)
        key = jax.random.key(seed)
        ks = jax.random.split(key, 12)

        def lin(k, shape, fan_in):
            return jax.random.normal(k, shape, jnp.float32) * fan_in ** (-0.5)
        return {'hidden_states': jax.random.normal(ks[0], (1, 256, HID), jnp.float32), 'w_ln1': jnp.zeros((HID,), jnp.float32), 'w_ln2': jnp.zeros((HID,), jnp.float32), 'W_qkvz': lin(ks[1], (HID, 2 * KEY_DIM + 2 * VAL_DIM), HID), 'W_ba': lin(ks[2], (HID, 2 * HV), HID), 'conv_w': jax.random.normal(ks[3], (CONV_DIM, KCONV), jnp.float32) * KCONV ** (-0.5), 'dt_bias': jax.random.normal(ks[4], (HV,), jnp.float32) * 0.1, 'A_log': jnp.log(jax.random.uniform(ks[5], (HV,), jnp.float32, 1.0, 16.0)), 'gate_norm_w': jnp.ones((DV,), jnp.float32), 'W_out': lin(ks[6], (VAL_DIM, HID), VAL_DIM), 'W_router': lin(ks[7], (HID, NEXP), HID), 'W_gate_e': lin(ks[8], (NEXP, HID, INTER), HID), 'W_up_e': lin(ks[9], (NEXP, HID, INTER), HID), 'W_down_e': lin(ks[10], (NEXP, INTER, HID), INTER)}
    _L0_attn_a_in = _L0_attn_a_setup()

    def _L0_attn_b_setup():
        import jax, jax.numpy as jnp
        import numpy as np
        EMBED_DIM = 128
        NUM_HEADS = 16
        CHUNK = 32

        def _mha_residual(x, Wq, Wk, Wv, Wo, num_heads):
            *lead, S, D = x.shape
            hd = D // num_heads
            scale = 1.0 / jnp.sqrt(jnp.asarray(hd, x.dtype))
            q = (x @ Wq).reshape(*lead, S, num_heads, hd)
            k = (x @ Wk).reshape(*lead, S, num_heads, hd)
            v = (x @ Wv).reshape(*lead, S, num_heads, hd)
            scores = jnp.einsum('...qhe,...khe->...hqk', q, k) * scale
            attn = jax.nn.softmax(scores, axis=-1)
            ctx = jnp.einsum('...hqk,...khe->...qhe', attn, v)
            ctx = ctx.reshape(*lead, S, D)
            return x + ctx @ Wo
        key = jax.random.key(seed)
        ks = jax.random.split(key, 9)
        B, S, D = (4, 1024, EMBED_DIM)
        w = lambda k: jax.random.normal(k, (D, D), dtype=jnp.float32) * (1.0 / np.sqrt(D))
        return {'x': jax.random.normal(ks[0], (B, S, D), dtype=jnp.float32), 'Wq_l': w(ks[1]), 'Wk_l': w(ks[2]), 'Wv_l': w(ks[3]), 'Wo_l': w(ks[4]), 'Wq_g': w(ks[5]), 'Wk_g': w(ks[6]), 'Wv_g': w(ks[7]), 'Wo_g': w(ks[8])}
    _L0_attn_b_in = _L0_attn_b_setup()

    def _L0_ffn_setup():
        import jax, jax.numpy as jnp
        import numpy as np
        THRESH_FACTOR = 0.7

        def ternary_quantize(w):
            delta = THRESH_FACTOR * jnp.mean(jnp.abs(w))
            return jnp.where(w > delta, 1.0, jnp.where(w < -delta, -1.0, 0.0)).astype(w.dtype)
        key = jax.random.key(seed)
        k1, k2, k3 = jax.random.split(key, 3)
        B, S, D_IN, D_OUT = (8, 512, 128, 128)
        inp = {'input': jax.random.normal(k1, (B, S, D_IN), dtype=jnp.float32), 'weight': jax.random.normal(k2, (D_OUT, D_IN), dtype=jnp.float32) * (1.0 / np.sqrt(D_IN)), 'alpha': jnp.ones((1,), dtype=jnp.float32), 'bias': jax.random.normal(k3, (D_OUT,), dtype=jnp.float32) * (1.0 / np.sqrt(D_IN))}
        return inp
    _L0_ffn_in = _L0_ffn_setup()

    def _L1_attn_a_setup():
        import jax, jax.numpy as jnp
        import numpy as np
        B, L, D = (8, 512, 128)
        H = 16
        DK = D // H
        MIN_FACTOR, MAX_FACTOR = (3, 10)

        def _attn(x, Wq, bq, Wk, bk, Wv, bv, Wo, bo):
            Bx, Lx, Dx = x.shape

            def proj(W, b):
                return (x @ W.T + b).reshape(Bx, Lx, H, DK).transpose(0, 2, 1, 3)
            Q, K, V = (proj(Wq, bq), proj(Wk, bk), proj(Wv, bv))
            l2 = jnp.linalg.norm(Q, axis=-1)
            logp = jax.nn.log_softmax(Q, axis=-1)
            prob = jnp.exp(logp)
            entropy = -jnp.sum(prob * jnp.log(prob + 1e-09), axis=-1)
            var = jnp.var(Q, axis=-1, ddof=1)
            q_scores = 0.5 * l2 + 0.3 * entropy + 0.2 * var
            q_std = jnp.std(q_scores, axis=2, ddof=1)
            q_mean = jnp.mean(q_scores, axis=2)
            factor = jnp.clip(jnp.round(q_std / (q_mean + 1e-06) * MAX_FACTOR), MIN_FACTOR, MAX_FACTOR).astype(jnp.int32)
            u = factor[:, 0]
            _, top_idx = jax.lax.top_k(q_scores, MAX_FACTOR)
            Q_sparse = jnp.take_along_axis(Q, top_idx[..., None], axis=2)
            scores = jnp.einsum('bhud,bhld->bhul', Q_sparse, K) / np.sqrt(DK)
            attn = jax.nn.softmax(scores, axis=-1)
            out = jnp.einsum('bhul,bhld->bhud', attn, V)
            valid = jnp.arange(MAX_FACTOR)[None, None, :] < u[:, None, None]
            scatter_idx = jnp.where(valid, top_idx, Lx)
            bidx = jnp.arange(Bx)[:, None, None]
            hidx = jnp.arange(H)[None, :, None]
            full = jnp.zeros((Bx, H, Lx, DK), dtype=x.dtype).at[bidx, hidx, scatter_idx].set(out, mode='drop')
            output = full.transpose(0, 2, 1, 3).reshape(Bx, Lx, Dx)
            return output @ Wo.T + bo
        key = jax.random.key(seed)
        ks = jax.random.split(key, 9)
        s = 1.0 / np.sqrt(D)
        return {'x': jax.random.normal(ks[0], (B, L, D), dtype=jnp.float32), 'Wq': jax.random.normal(ks[1], (D, D), dtype=jnp.float32) * s, 'bq': jax.random.normal(ks[2], (D,), dtype=jnp.float32) * s, 'Wk': jax.random.normal(ks[3], (D, D), dtype=jnp.float32) * s, 'bk': jax.random.normal(ks[4], (D,), dtype=jnp.float32) * s, 'Wv': jax.random.normal(ks[5], (D, D), dtype=jnp.float32) * s, 'bv': jax.random.normal(ks[6], (D,), dtype=jnp.float32) * s, 'Wo': jax.random.normal(ks[7], (D, D), dtype=jnp.float32) * s, 'bo': jax.random.normal(ks[8], (D,), dtype=jnp.float32) * s}
    _L1_attn_a_in = _L1_attn_a_setup()

    def _L1_attn_b_setup():
        import jax, jax.numpy as jnp
        import numpy as np
        HEADS = 16
        KV_HEADS = 4
        DIM_HEAD = 64
        SCALE = DIM_HEAD ** (-0.5)

        def _rotate_half(x):
            x1, x2 = jnp.split(x, 2, axis=-1)
            return jnp.concatenate((-x2, x1), axis=-1)

        def _rope_freqs(n, d):
            inv_freq = 1.0 / 10000.0 ** (jnp.arange(0, d, 2, dtype=jnp.float32) / d)
            freqs = jnp.einsum('i,j->ij', jnp.arange(n, dtype=jnp.float32), inv_freq)
            return jnp.concatenate((freqs, freqs), axis=-1)
        key = jax.random.key(seed)
        ks = jax.random.split(key, 4)
        b, n, dim = (2, 256, 128)
        inner = HEADS * DIM_HEAD
        s = dim ** (-0.5)
        return {'x': jax.random.normal(ks[0], (b, n, dim), jnp.float32), 'Wq': jax.random.normal(ks[1], (dim, inner), jnp.float32) * s, 'Wkv': jax.random.normal(ks[2], (dim, DIM_HEAD * KV_HEADS * 2), jnp.float32) * s, 'Wo': jax.random.normal(ks[3], (inner, dim), jnp.float32) * s, 'bo': jnp.zeros((dim,), jnp.float32)}
    _L1_attn_b_in = _L1_attn_b_setup()

    def _L1_ffn_setup():
        import jax, jax.numpy as jnp
        import numpy as np
        DIM = 128
        DEPTH = 2
        HEADS = 8
        DIM_HEAD = 64
        WINDOW = 64
        INNER = HEADS * DIM_HEAD
        HID = int(DIM * 4 * 2 / 3)
        B, N = (2, 1024)
        QK_SCALE = 8.0

        def shift_token(t):
            t1, t2 = jnp.split(t, 2, axis=-1)
            t2 = jnp.pad(t2, ((0, 0), (1, 0), (0, 0)))[:, :-1]
            return jnp.concatenate([t1, t2], axis=-1)

        def l2norm(t):
            return t / jnp.clip(jnp.linalg.norm(t, axis=-1, keepdims=True), 1e-12)

        def rotate_half(x):
            x1, x2 = jnp.split(x, 2, axis=-1)
            return jnp.concatenate([-x2, x1], axis=-1)

        def rotary_xpos(q, k):
            n = q.shape[-2]
            half_idx = jnp.arange(0, DIM_HEAD, 2, dtype=jnp.float32)
            inv_freq = 1.0 / 10000.0 ** (half_idx / DIM_HEAD)
            t = jnp.arange(n, dtype=jnp.float32)
            freqs = t[:, None] * inv_freq[None, :]
            freqs = jnp.concatenate([freqs, freqs], axis=-1)
            base = (half_idx + 0.4 * DIM_HEAD) / (1.4 * DIM_HEAD)
            power = (t - n // 2) / float(WINDOW // 2)
            scale = base[None, :] ** power[:, None]
            scale = jnp.concatenate([scale, scale], axis=-1)
            cos, sin = (jnp.cos(freqs), jnp.sin(freqs))
            q = q * cos * scale + rotate_half(q) * sin * scale
            k = k * cos / scale + rotate_half(k) * sin / scale
            return (q, k)

        def local_attention(q, k, v):
            b, h, n, d = q.shape
            w = n // WINDOW
            bq = q.reshape(b, h, w, WINDOW, d) * QK_SCALE
            bk = k.reshape(b, h, w, WINDOW, d)
            bv = v.reshape(b, h, w, WINDOW, d)

            def look_around(t):
                p = jnp.pad(t, ((0, 0), (0, 0), (1, 0), (0, 0), (0, 0)))
                return jnp.concatenate([p[:, :, :w], p[:, :, 1:]], axis=3)
            bk, bv = (look_around(bk), look_around(bv))
            bt = jnp.arange(n).reshape(w, WINDOW)
            btp = jnp.pad(bt, ((1, 0), (0, 0)), constant_values=-1)
            btk = jnp.concatenate([btp[:w], btp[1:]], axis=1)
            sim = jnp.einsum('bhwid,bhwjd->bhwij', bq, bk)
            i = bt[:, :, None]
            j = btk[:, None, :]
            mask = (i < j) | (i > j + WINDOW) | (j == -1)
            sim = jnp.where(mask, -jnp.finfo(sim.dtype).max, sim)
            attn = jax.nn.softmax(sim, axis=-1)
            out = jnp.einsum('bhwij,bhwjd->bhwid', attn, bv)
            return out.reshape(b, h, n, d)

        def _layer(x, wqkv, qs, ksc, wo, lg, lb, w1, b1, w2, b2):
            b, n, _ = x.shape
            h = shift_token(x)
            qkv = h @ wqkv
            q, k, v = jnp.split(qkv, 3, axis=-1)
            to_heads = lambda t: t.reshape(b, n, HEADS, DIM_HEAD).transpose(0, 2, 1, 3)
            q, k, v = (to_heads(q), to_heads(k), to_heads(v))
            q = l2norm(q) * qs
            k = l2norm(k) * ksc
            q, k = rotary_xpos(q, k)
            o = local_attention(q, k, v)
            o = o.transpose(0, 2, 1, 3).reshape(b, n, INNER)
            x = x + o @ wo
            h = shift_token(x)
            mu = h.mean(-1, keepdims=True)
            var = h.var(-1, keepdims=True)
            h = (h - mu) / jnp.sqrt(var + 1e-05) * lg + lb
            h = h @ w1 + b1
            a, g = jnp.split(h, 2, axis=-1)
            h = a * jax.nn.gelu(g, approximate=False)
            x = x + h @ w2 + b2
            return x
        key = jax.random.key(seed)
        ks = jax.random.split(key, 6)
        return {'x': jax.random.normal(ks[0], (B, N, DIM), jnp.float32), 'wqkv': jax.random.normal(ks[1], (DEPTH, DIM, 3 * INNER), jnp.float32) * 0.02, 'q_scale': jnp.ones((DEPTH, DIM_HEAD), jnp.float32), 'k_scale': jnp.ones((DEPTH, DIM_HEAD), jnp.float32), 'wo': jax.random.normal(ks[2], (DEPTH, INNER, DIM), jnp.float32) * 0.02, 'ln_g': jnp.ones((DEPTH, DIM), jnp.float32), 'ln_b': jnp.zeros((DEPTH, DIM), jnp.float32), 'w1': jax.random.normal(ks[3], (DEPTH, DIM, 2 * HID), jnp.float32) * 0.02, 'b1': jnp.zeros((DEPTH, 2 * HID), jnp.float32), 'w2': jax.random.normal(ks[4], (DEPTH, HID, DIM), jnp.float32) * 0.02, 'b2': jnp.zeros((DEPTH, DIM), jnp.float32)}
    _L1_ffn_in = _L1_ffn_setup()
    _d = {'L0_attn_a_hidden_states': _L0_attn_a_in['hidden_states'], 'L0_attn_a_w_ln1': _L0_attn_a_in['w_ln1'], 'L0_attn_a_w_ln2': _L0_attn_a_in['w_ln2'], 'L0_attn_a_W_qkvz': _L0_attn_a_in['W_qkvz'], 'L0_attn_a_W_ba': _L0_attn_a_in['W_ba'], 'L0_attn_a_conv_w': _L0_attn_a_in['conv_w'], 'L0_attn_a_dt_bias': _L0_attn_a_in['dt_bias'], 'L0_attn_a_A_log': _L0_attn_a_in['A_log'], 'L0_attn_a_gate_norm_w': _L0_attn_a_in['gate_norm_w'], 'L0_attn_a_W_out': _L0_attn_a_in['W_out'], 'L0_attn_a_W_router': _L0_attn_a_in['W_router'], 'L0_attn_a_W_gate_e': _L0_attn_a_in['W_gate_e'], 'L0_attn_a_W_up_e': _L0_attn_a_in['W_up_e'], 'L0_attn_a_W_down_e': _L0_attn_a_in['W_down_e'], 'L0_attn_b_Wq_l': _L0_attn_b_in['Wq_l'], 'L0_attn_b_Wk_l': _L0_attn_b_in['Wk_l'], 'L0_attn_b_Wv_l': _L0_attn_b_in['Wv_l'], 'L0_attn_b_Wo_l': _L0_attn_b_in['Wo_l'], 'L0_attn_b_Wq_g': _L0_attn_b_in['Wq_g'], 'L0_attn_b_Wk_g': _L0_attn_b_in['Wk_g'], 'L0_attn_b_Wv_g': _L0_attn_b_in['Wv_g'], 'L0_attn_b_Wo_g': _L0_attn_b_in['Wo_g'], 'L0_ffn_weight': _L0_ffn_in['weight'], 'L0_ffn_alpha': _L0_ffn_in['alpha'], 'L0_ffn_bias': _L0_ffn_in['bias'], 'L1_attn_a_Wq': _L1_attn_a_in['Wq'], 'L1_attn_a_bq': _L1_attn_a_in['bq'], 'L1_attn_a_Wk': _L1_attn_a_in['Wk'], 'L1_attn_a_bk': _L1_attn_a_in['bk'], 'L1_attn_a_Wv': _L1_attn_a_in['Wv'], 'L1_attn_a_bv': _L1_attn_a_in['bv'], 'L1_attn_a_Wo': _L1_attn_a_in['Wo'], 'L1_attn_a_bo': _L1_attn_a_in['bo'], 'L1_attn_b_Wq': _L1_attn_b_in['Wq'], 'L1_attn_b_Wkv': _L1_attn_b_in['Wkv'], 'L1_attn_b_Wo': _L1_attn_b_in['Wo'], 'L1_attn_b_bo': _L1_attn_b_in['bo'], 'L1_ffn_wqkv': _L1_ffn_in['wqkv'], 'L1_ffn_q_scale': _L1_ffn_in['q_scale'], 'L1_ffn_k_scale': _L1_ffn_in['k_scale'], 'L1_ffn_wo': _L1_ffn_in['wo'], 'L1_ffn_ln_g': _L1_ffn_in['ln_g'], 'L1_ffn_ln_b': _L1_ffn_in['ln_b'], 'L1_ffn_w1': _L1_ffn_in['w1'], 'L1_ffn_b1': _L1_ffn_in['b1'], 'L1_ffn_w2': _L1_ffn_in['w2'], 'L1_ffn_b2': _L1_ffn_in['b2']}
    _x0 = _d['L0_attn_a_hidden_states']
    _d['L0_attn_a_hidden_states'] = jax.random.normal(jax.random.fold_in(jax.random.key(seed), 1), (1, 2048, 128), dtype=_x0.dtype)
    del _x0
    return _d

def reference(L0_attn_a_hidden_states, L0_attn_a_w_ln1, L0_attn_a_w_ln2, L0_attn_a_W_qkvz, L0_attn_a_W_ba, L0_attn_a_conv_w, L0_attn_a_dt_bias, L0_attn_a_A_log, L0_attn_a_gate_norm_w, L0_attn_a_W_out, L0_attn_a_W_router, L0_attn_a_W_gate_e, L0_attn_a_W_up_e, L0_attn_a_W_down_e, L0_attn_b_Wq_l, L0_attn_b_Wk_l, L0_attn_b_Wv_l, L0_attn_b_Wo_l, L0_attn_b_Wq_g, L0_attn_b_Wk_g, L0_attn_b_Wv_g, L0_attn_b_Wo_g, L0_ffn_weight, L0_ffn_alpha, L0_ffn_bias, L1_attn_a_Wq, L1_attn_a_bq, L1_attn_a_Wk, L1_attn_a_bk, L1_attn_a_Wv, L1_attn_a_bv, L1_attn_a_Wo, L1_attn_a_bo, L1_attn_b_Wq, L1_attn_b_Wkv, L1_attn_b_Wo, L1_attn_b_bo, L1_ffn_wqkv, L1_ffn_q_scale, L1_ffn_k_scale, L1_ffn_wo, L1_ffn_ln_g, L1_ffn_ln_b, L1_ffn_w1, L1_ffn_b1, L1_ffn_w2, L1_ffn_b2):

    def _L0_attn_a_ref(hidden_states, w_ln1, w_ln2, W_qkvz, W_ba, conv_w, dt_bias, A_log, gate_norm_w, W_out, W_router, W_gate_e, W_up_e, W_down_e):
        import jax, jax.numpy as jnp
        import numpy as np
        HID = 128
        HK, HV = (4, 8)
        DK, DV = (128, 128)
        KEY_DIM = HK * DK
        VAL_DIM = HV * DV
        CONV_DIM = 2 * KEY_DIM + VAL_DIM
        KCONV = 4
        NEXP, TOPK, INTER = (8, 2, 64)
        EPS = 1e-06

        def zrms(x, w):
            v = jnp.mean(x * x, axis=-1, keepdims=True)
            return x * jax.lax.rsqrt(v + EPS) * (1.0 + w)

        def causal_dwconv(x, w):
            xp = jnp.pad(x, ((0, 0), (KCONV - 1, 0), (0, 0)))
            kern = w.T[:, None, :]
            return jax.lax.conv_general_dilated(xp, kern, (1,), 'VALID', dimension_numbers=('NHC', 'HIO', 'NHC'), feature_group_count=CONV_DIM)

        def gated_delta_rule(q, k, v, g, beta):
            B = q.shape[0]
            S0 = jnp.zeros((B, HV, DK, DV), q.dtype)

            def step(S, inp):
                qt, kt, vt, gt, bt = inp
                S = S * jnp.exp(gt)[..., None, None]
                kv = jnp.einsum('bhk,bhkv->bhv', kt, S)
                delta = (vt - kv) * bt[..., None]
                S = S + jnp.einsum('bhk,bhv->bhkv', kt, delta)
                o = jnp.einsum('bhk,bhkv->bhv', qt, S)
                return (S, o)
            xs = tuple((jnp.moveaxis(a, 1, 0) for a in (q, k, v, g, beta)))
            _, o = jax.lax.scan(step, S0, xs)
            return jnp.moveaxis(o, 0, 1)

        def _reference_tuple_inner(hidden_states, w_ln1, w_ln2, W_qkvz, W_ba, conv_w, dt_bias, A_log, gate_norm_w, W_out, W_router, W_gate_e, W_up_e, W_down_e):
            B, S, _ = hidden_states.shape
            resid = hidden_states
            x = zrms(hidden_states, w_ln1)
            qkvz = x @ W_qkvz
            q, k, v, z = jnp.split(qkvz, [KEY_DIM, 2 * KEY_DIM, 2 * KEY_DIM + VAL_DIM], axis=-1)
            b, a = jnp.split(x @ W_ba, 2, axis=-1)
            beta = jax.nn.sigmoid(b)
            g = -jnp.exp(A_log) * jax.nn.softplus(a + dt_bias)
            mixed = jnp.concatenate([q, k, v], axis=-1)
            mixed = jax.nn.silu(causal_dwconv(mixed, conv_w))
            q, k, v = jnp.split(mixed, [KEY_DIM, 2 * KEY_DIM], axis=-1)
            q = q.reshape(B, S, HK, DK)
            k = k.reshape(B, S, HK, DK)
            v = v.reshape(B, S, HV, DV)
            rep = HV // HK
            q = jnp.repeat(q, rep, axis=2)
            k = jnp.repeat(k, rep, axis=2)
            q = q * jax.lax.rsqrt(jnp.sum(q * q, -1, keepdims=True) + EPS)
            k = k * jax.lax.rsqrt(jnp.sum(k * k, -1, keepdims=True) + EPS)
            q = q * DK ** (-0.5)
            core = gated_delta_rule(q, k, v, g, beta)
            core = core * jax.lax.rsqrt(jnp.mean(core * core, -1, keepdims=True) + EPS) * gate_norm_w
            core = core * jax.nn.silu(z.reshape(B, S, HV, DV))
            h = resid + core.reshape(B, S, VAL_DIM) @ W_out
            resid = h
            x = zrms(h, w_ln2)
            probs = jax.nn.softmax(x @ W_router, axis=-1)
            topv, topi = jax.lax.top_k(probs, TOPK)
            topv = topv / jnp.sum(topv, -1, keepdims=True)
            route = jnp.sum(jax.nn.one_hot(topi, NEXP, dtype=x.dtype) * topv[..., None], axis=-2)
            gate_h = jnp.einsum('bsh,ehi->bsei', x, W_gate_e)
            up_h = jnp.einsum('bsh,ehi->bsei', x, W_up_e)
            exp_out = jnp.einsum('bsei,eih->bseh', jax.nn.silu(gate_h) * up_h, W_down_e)
            moe_out = jnp.einsum('bseh,bse->bsh', exp_out, route)
            return (resid + moe_out, topi)
        return _reference_tuple_inner(hidden_states, w_ln1, w_ln2, W_qkvz, W_ba, conv_w, dt_bias, A_log, gate_norm_w, W_out, W_router, W_gate_e, W_up_e, W_down_e)[0]

    def _L0_attn_b_ref(x, Wq_l, Wk_l, Wv_l, Wo_l, Wq_g, Wk_g, Wv_g, Wo_g):
        import jax, jax.numpy as jnp
        import numpy as np
        EMBED_DIM = 128
        NUM_HEADS = 16
        CHUNK = 32

        def _mha_residual(x, Wq, Wk, Wv, Wo, num_heads):
            *lead, S, D = x.shape
            hd = D // num_heads
            scale = 1.0 / jnp.sqrt(jnp.asarray(hd, x.dtype))
            q = (x @ Wq).reshape(*lead, S, num_heads, hd)
            k = (x @ Wk).reshape(*lead, S, num_heads, hd)
            v = (x @ Wv).reshape(*lead, S, num_heads, hd)
            scores = jnp.einsum('...qhe,...khe->...hqk', q, k) * scale
            attn = jax.nn.softmax(scores, axis=-1)
            ctx = jnp.einsum('...hqk,...khe->...qhe', attn, v)
            ctx = ctx.reshape(*lead, S, D)
            return x + ctx @ Wo
        B, S, D = x.shape
        nC = S // CHUNK
        chunks = x.reshape(B, nC, CHUNK, D)
        chunks = _mha_residual(chunks, Wq_l, Wk_l, Wv_l, Wo_l, NUM_HEADS)
        summaries = chunks.mean(axis=2)
        global_ctx = _mha_residual(summaries, Wq_g, Wk_g, Wv_g, Wo_g, NUM_HEADS)
        enhanced = chunks + global_ctx[:, :, None, :]
        return enhanced.reshape(B, S, D)

    def _L0_ffn_ref(input, weight, alpha, bias):
        import jax, jax.numpy as jnp
        import numpy as np
        THRESH_FACTOR = 0.7

        def ternary_quantize(w):
            delta = THRESH_FACTOR * jnp.mean(jnp.abs(w))
            return jnp.where(w > delta, 1.0, jnp.where(w < -delta, -1.0, 0.0)).astype(w.dtype)
        w_ternary = ternary_quantize(weight)
        w_eff = w_ternary * alpha
        out = jnp.einsum('bsd,od->bso', input, w_eff) + bias
        return out

    def _L1_attn_a_ref(x, Wq, bq, Wk, bk, Wv, bv, Wo, bo):
        import jax, jax.numpy as jnp
        import numpy as np
        B, L, D = (8, 512, 128)
        H = 16
        DK = D // H
        MIN_FACTOR, MAX_FACTOR = (3, 10)

        def _attn(x, Wq, bq, Wk, bk, Wv, bv, Wo, bo):
            Bx, Lx, Dx = x.shape

            def proj(W, b):
                return (x @ W.T + b).reshape(Bx, Lx, H, DK).transpose(0, 2, 1, 3)
            Q, K, V = (proj(Wq, bq), proj(Wk, bk), proj(Wv, bv))
            l2 = jnp.linalg.norm(Q, axis=-1)
            logp = jax.nn.log_softmax(Q, axis=-1)
            prob = jnp.exp(logp)
            entropy = -jnp.sum(prob * jnp.log(prob + 1e-09), axis=-1)
            var = jnp.var(Q, axis=-1, ddof=1)
            q_scores = 0.5 * l2 + 0.3 * entropy + 0.2 * var
            q_std = jnp.std(q_scores, axis=2, ddof=1)
            q_mean = jnp.mean(q_scores, axis=2)
            factor = jnp.clip(jnp.round(q_std / (q_mean + 1e-06) * MAX_FACTOR), MIN_FACTOR, MAX_FACTOR).astype(jnp.int32)
            u = factor[:, 0]
            _, top_idx = jax.lax.top_k(q_scores, MAX_FACTOR)
            Q_sparse = jnp.take_along_axis(Q, top_idx[..., None], axis=2)
            scores = jnp.einsum('bhud,bhld->bhul', Q_sparse, K) / np.sqrt(DK)
            attn = jax.nn.softmax(scores, axis=-1)
            out = jnp.einsum('bhul,bhld->bhud', attn, V)
            valid = jnp.arange(MAX_FACTOR)[None, None, :] < u[:, None, None]
            scatter_idx = jnp.where(valid, top_idx, Lx)
            bidx = jnp.arange(Bx)[:, None, None]
            hidx = jnp.arange(H)[None, :, None]
            full = jnp.zeros((Bx, H, Lx, DK), dtype=x.dtype).at[bidx, hidx, scatter_idx].set(out, mode='drop')
            output = full.transpose(0, 2, 1, 3).reshape(Bx, Lx, Dx)
            return output @ Wo.T + bo
        return _attn(x, Wq, bq, Wk, bk, Wv, bv, Wo, bo)

    def _L1_attn_b_ref(x, Wq, Wkv, Wo, bo):
        import jax, jax.numpy as jnp
        import numpy as np
        HEADS = 16
        KV_HEADS = 4
        DIM_HEAD = 64
        SCALE = DIM_HEAD ** (-0.5)

        def _rotate_half(x):
            x1, x2 = jnp.split(x, 2, axis=-1)
            return jnp.concatenate((-x2, x1), axis=-1)

        def _rope_freqs(n, d):
            inv_freq = 1.0 / 10000.0 ** (jnp.arange(0, d, 2, dtype=jnp.float32) / d)
            freqs = jnp.einsum('i,j->ij', jnp.arange(n, dtype=jnp.float32), inv_freq)
            return jnp.concatenate((freqs, freqs), axis=-1)
        b, n, dim = x.shape
        g = HEADS // KV_HEADS
        q = (x @ Wq).reshape(b, n, HEADS, DIM_HEAD).transpose(0, 2, 1, 3)
        kv = (x @ Wkv).reshape(b, n, 2 * KV_HEADS, DIM_HEAD)
        k = kv[:, :, :KV_HEADS].transpose(0, 2, 1, 3)
        v = kv[:, :, KV_HEADS:].transpose(0, 2, 1, 3)
        freqs = _rope_freqs(n, DIM_HEAD)
        cos, sin = (jnp.cos(freqs), jnp.sin(freqs))
        q = q * cos + _rotate_half(q) * sin
        k = k * cos + _rotate_half(k) * sin
        k = jnp.repeat(k, g, axis=1)
        v = jnp.repeat(v, g, axis=1)
        dots = jnp.einsum('bhid,bhjd->bhij', q, k) * SCALE
        attn = jax.nn.softmax(dots, axis=-1)
        out = jnp.einsum('bhij,bhjd->bhid', attn, v)
        out = out.transpose(0, 2, 1, 3).reshape(b, n, HEADS * DIM_HEAD)
        return out @ Wo + bo

    def _L1_ffn_ref(x, wqkv, q_scale, k_scale, wo, ln_g, ln_b, w1, b1, w2, b2):
        import jax, jax.numpy as jnp
        import numpy as np
        DIM = 128
        DEPTH = 2
        HEADS = 8
        DIM_HEAD = 64
        WINDOW = 64
        INNER = HEADS * DIM_HEAD
        HID = int(DIM * 4 * 2 / 3)
        B, N = (2, 1024)
        QK_SCALE = 8.0

        def shift_token(t):
            t1, t2 = jnp.split(t, 2, axis=-1)
            t2 = jnp.pad(t2, ((0, 0), (1, 0), (0, 0)))[:, :-1]
            return jnp.concatenate([t1, t2], axis=-1)

        def l2norm(t):
            return t / jnp.clip(jnp.linalg.norm(t, axis=-1, keepdims=True), 1e-12)

        def rotate_half(x):
            x1, x2 = jnp.split(x, 2, axis=-1)
            return jnp.concatenate([-x2, x1], axis=-1)

        def rotary_xpos(q, k):
            n = q.shape[-2]
            half_idx = jnp.arange(0, DIM_HEAD, 2, dtype=jnp.float32)
            inv_freq = 1.0 / 10000.0 ** (half_idx / DIM_HEAD)
            t = jnp.arange(n, dtype=jnp.float32)
            freqs = t[:, None] * inv_freq[None, :]
            freqs = jnp.concatenate([freqs, freqs], axis=-1)
            base = (half_idx + 0.4 * DIM_HEAD) / (1.4 * DIM_HEAD)
            power = (t - n // 2) / float(WINDOW // 2)
            scale = base[None, :] ** power[:, None]
            scale = jnp.concatenate([scale, scale], axis=-1)
            cos, sin = (jnp.cos(freqs), jnp.sin(freqs))
            q = q * cos * scale + rotate_half(q) * sin * scale
            k = k * cos / scale + rotate_half(k) * sin / scale
            return (q, k)

        def local_attention(q, k, v):
            b, h, n, d = q.shape
            w = n // WINDOW
            bq = q.reshape(b, h, w, WINDOW, d) * QK_SCALE
            bk = k.reshape(b, h, w, WINDOW, d)
            bv = v.reshape(b, h, w, WINDOW, d)

            def look_around(t):
                p = jnp.pad(t, ((0, 0), (0, 0), (1, 0), (0, 0), (0, 0)))
                return jnp.concatenate([p[:, :, :w], p[:, :, 1:]], axis=3)
            bk, bv = (look_around(bk), look_around(bv))
            bt = jnp.arange(n).reshape(w, WINDOW)
            btp = jnp.pad(bt, ((1, 0), (0, 0)), constant_values=-1)
            btk = jnp.concatenate([btp[:w], btp[1:]], axis=1)
            sim = jnp.einsum('bhwid,bhwjd->bhwij', bq, bk)
            i = bt[:, :, None]
            j = btk[:, None, :]
            mask = (i < j) | (i > j + WINDOW) | (j == -1)
            sim = jnp.where(mask, -jnp.finfo(sim.dtype).max, sim)
            attn = jax.nn.softmax(sim, axis=-1)
            out = jnp.einsum('bhwij,bhwjd->bhwid', attn, bv)
            return out.reshape(b, h, n, d)

        def _layer(x, wqkv, qs, ksc, wo, lg, lb, w1, b1, w2, b2):
            b, n, _ = x.shape
            h = shift_token(x)
            qkv = h @ wqkv
            q, k, v = jnp.split(qkv, 3, axis=-1)
            to_heads = lambda t: t.reshape(b, n, HEADS, DIM_HEAD).transpose(0, 2, 1, 3)
            q, k, v = (to_heads(q), to_heads(k), to_heads(v))
            q = l2norm(q) * qs
            k = l2norm(k) * ksc
            q, k = rotary_xpos(q, k)
            o = local_attention(q, k, v)
            o = o.transpose(0, 2, 1, 3).reshape(b, n, INNER)
            x = x + o @ wo
            h = shift_token(x)
            mu = h.mean(-1, keepdims=True)
            var = h.var(-1, keepdims=True)
            h = (h - mu) / jnp.sqrt(var + 1e-05) * lg + lb
            h = h @ w1 + b1
            a, g = jnp.split(h, 2, axis=-1)
            h = a * jax.nn.gelu(g, approximate=False)
            x = x + h @ w2 + b2
            return x
        for l in range(DEPTH):
            x = _layer(x, wqkv[l], q_scale[l], k_scale[l], wo[l], ln_g[l], ln_b[l], w1[l], b1[l], w2[l], b2[l])
        return x
    x = L0_attn_a_hidden_states
    x = x + _L0_attn_a_ref(_layernorm(x, axis=-1), L0_attn_a_w_ln1, L0_attn_a_w_ln2, L0_attn_a_W_qkvz, L0_attn_a_W_ba, L0_attn_a_conv_w, L0_attn_a_dt_bias, L0_attn_a_A_log, L0_attn_a_gate_norm_w, L0_attn_a_W_out, L0_attn_a_W_router, L0_attn_a_W_gate_e, L0_attn_a_W_up_e, L0_attn_a_W_down_e)
    x = x + _L0_ffn_ref(_layernorm(x, axis=-1), L0_ffn_weight, L0_ffn_alpha, L0_ffn_bias)
    x = x + _L0_attn_b_ref(_layernorm(x, axis=-1), L0_attn_b_Wq_l, L0_attn_b_Wk_l, L0_attn_b_Wv_l, L0_attn_b_Wo_l, L0_attn_b_Wq_g, L0_attn_b_Wk_g, L0_attn_b_Wv_g, L0_attn_b_Wo_g)
    x = x + _L0_ffn_ref(_layernorm(x, axis=-1), L0_ffn_weight, L0_ffn_alpha, L0_ffn_bias)
    x = x + _L1_attn_a_ref(_layernorm(x, axis=-1), L1_attn_a_Wq, L1_attn_a_bq, L1_attn_a_Wk, L1_attn_a_bk, L1_attn_a_Wv, L1_attn_a_bv, L1_attn_a_Wo, L1_attn_a_bo)
    x = x + _L1_ffn_ref(_layernorm(x, axis=-1), L1_ffn_wqkv, L1_ffn_q_scale, L1_ffn_k_scale, L1_ffn_wo, L1_ffn_ln_g, L1_ffn_ln_b, L1_ffn_w1, L1_ffn_b1, L1_ffn_w2, L1_ffn_b2)
    x = x + _L1_attn_b_ref(_layernorm(x, axis=-1), L1_attn_b_Wq, L1_attn_b_Wkv, L1_attn_b_Wo, L1_attn_b_bo)
    x = x + _L1_ffn_ref(_layernorm(x, axis=-1), L1_ffn_wqkv, L1_ffn_q_scale, L1_ffn_k_scale, L1_ffn_wo, L1_ffn_ln_g, L1_ffn_ln_b, L1_ffn_w1, L1_ffn_b1, L1_ffn_w2, L1_ffn_b2)
    return x

_drawn_inputs = setup_inputs


def setup_inputs(seed=0):
    import zlib

    import numpy as np

    out = dict(_drawn_inputs(seed))
    spreads = {'L0_attn_a_w_ln1': (0.0, 0.1),
     'L0_attn_a_w_ln2': (0.0, 0.1),
     'L0_attn_a_gate_norm_w': (1.0, 0.2),
     'L1_attn_b_bo': (0.0, 2.0),
     'L1_ffn_q_scale': (1.0, 0.6),
     'L1_ffn_k_scale': (1.0, 0.6),
     'L1_ffn_ln_g': (1.0, 0.6),
     'L1_ffn_ln_b': (0.0, 0.8),
     'L1_ffn_b1': (0.0, 0.8),
     'L1_ffn_b2': (0.0, 0.423)}
    factors = {'L0_attn_a_dt_bias': 3.796,
     'L0_attn_b_Wq_g': 8.0,
     'L0_attn_b_Wk_g': 8.0,
     'L0_attn_b_Wv_g': 8.0,
     'L0_attn_b_Wo_g': 8.0,
     'L0_ffn_bias': 3.845,
     'L1_attn_a_Wq': 8.0,
     'L1_attn_a_bq': 8.0,
     'L1_attn_a_Wk': 8.0,
     'L1_attn_a_bk': 64.0,
     'L1_attn_a_Wv': 8.0,
     'L1_attn_a_bv': 64.0,
     'L1_attn_a_Wo': 8.0,
     'L1_attn_a_bo': 8.0,
     'L1_attn_b_Wq': 3.775,
     'L1_attn_b_Wkv': 3.177,
     'L1_attn_b_Wo': 3.262,
     'L1_ffn_wqkv': 8.0,
     'L1_ffn_wo': 8.0,
     'L1_ffn_w1': 8.0,
     'L1_ffn_w2': 8.0}
    for name, (base, spread) in spreads.items():
        noise = np.random.default_rng([zlib.crc32(name.encode()), seed]).standard_normal(out[name].shape)
        drawn = base * np.exp(spread * noise) if base else spread * noise
        out[name] = jnp.asarray(drawn.astype(out[name].dtype))
    for name, factor in factors.items():
        out[name] = (out[name] * factor).astype(out[name].dtype)
    return out
```

```python
from contextlib import ExitStack

import numpy as np
import concourse.bass as bass
from concourse import mybir

F32 = mybir.dt.float32
BF16 = mybir.dt.bfloat16
U32 = mybir.dt.uint32
I32 = mybir.dt.int32
ALU = mybir.AluOpType
ACT = mybir.ActivationFunctionType
X_AXIS = mybir.AxisListType.X

P = 128
TOKENS = 2048
TILES = TOKENS // P
DIM = 128
LN_EPS = 1e-5



def signals(nc, ctx, names):
    return {name: ctx.enter_context(nc.semaphore(name)) for name in names.split()}


def clear_signals(nc, S):
    for sem in S.values():
        nc.sync.sem_clear(sem)
    nc.all_engine_barrier()


def counted(eng, sem):
    count = [0]

    def link(ins):
        count[0] += 1
        ins.then_inc(sem, 1)
        eng.wait_ge(sem, count[0])

    return link


def over_inner(ap, n):
    return ap.unsqueeze(2).broadcast_to([ap.shape[0], ap.shape[1], n])


def over_middle(ap, n):
    return ap.unsqueeze(1).broadcast_to([ap.shape[0], n, ap.shape[1]])


def heads(ap, n):
    return ap.rearrange("p (h d) -> p h d", h=n)


def tile_of(ap3, t):
    return ap3[:, bass.ds(t, 1), :].rearrange("p a d -> p (a d)")


def inv_sqrt(dve, link, x, y, tmp):
    link(dve.tensor_scalar(y.bitcast(U32), x.bitcast(U32), 1, None, ALU.logical_shift_right))
    link(dve.tensor_scalar(y.bitcast(I32), y.bitcast(I32), -1.0, float(0x5F3759DF), ALU.mult, ALU.add))
    for _ in range(3):
        link(dve.tensor_tensor(tmp, y, y, ALU.mult))
        link(dve.tensor_tensor(tmp, tmp, x, ALU.mult))
        link(dve.tensor_scalar(tmp, tmp, -0.5, 1.5, ALU.mult, ALU.add))
        link(dve.tensor_tensor(y, y, tmp, ALU.mult))


def normalize_rows(dve, link, x, out, stats, mv, rstd):
    link(dve.bn_stats(stats, x))
    link(dve.bn_aggr(mv, stats))
    link(dve.tensor_scalar(mv[:, 1:2], mv[:, 1:2], LN_EPS, None, ALU.add))
    inv_sqrt(dve, link, mv[:, 1:2], rstd, stats[:, 0:1])
    return dve.tensor_scalar(out, x, mv[:, 0:1], rstd, ALU.subtract, ALU.mult)



def shape_constants():
    j, t = np.arange(P)[:, None], np.arange(P)[None, :]
    f32 = {
        "ident": j == t,
        "upto": j <= t,
        "after": j > t,
        "ones": np.ones((P, P)),
    }
    levels = []
    for l in range(7):
        a, b = j >> l, t >> l
        levels.append((a % 2 == 1) & (b == a - 1))
    masks = np.stack(levels + [m.T for m in levels], 1)
    return (np.concatenate([v.astype(np.float32) for v in f32.values()], 1),
            np.ascontiguousarray(masks.astype(np.uint32)))



def delta_block(nc, W, C, X, tag):
    HK, HV, D, TAPS, NEXP, INTER = 4, 8, 128, 4, 8, 64
    REP = HV // HK
    QK, VAL = 2 * HK * D, HV * D
    CONV = QK + VAL
    EPS = 1e-6
    LEVELS = 7
    ident, upto, after, ones = C["ident"], C["upto"], C["after"], C["ones"]

    with ExitStack() as ctx:
        def sb(name, shape, dt=F32):
            return ctx.enter_context(nc.sbuf_tensor(f"{tag}_{name}", shape, dt))

        wconv = sb("wconv", [P, TAPS, CONV])
        wz = sb("wz", [P, VAL])
        wba = sb("wba", [P, 2 * HV])
        wout = sb("wout", [P, HV, DIM])
        wrouter = sb("wrouter", [P, NEXP])
        wgate = sb("wgate", [P, NEXP, INTER])
        wup = sb("wup", [P, NEXP, INTER])
        wdown = sb("wdown", [P, 4, DIM])
        ln1 = sb("ln1", [P, 1])
        ln2 = sb("ln2", [P, 1])
        dtb = sb("dtb", [P, HV])
        nega = sb("nega", [P, HV])
        gnw = sb("gnw", [P, D])
        tri = sb("tri", [P, 2 * LEVELS, P], U32)
        iota8 = sb("iota8", [P, NEXP])
        state = sb("state", [P, HV, D])
        x1T = sb("x1T", [P, TAPS - 1 + P])
        ps = ctx.enter_context(nc.psum_tensor(tag + "_ps", [P, 8, 512], F32))

        with ExitStack() as c2:
            cw = c2.enter_context(nc.sbuf_tensor(tag + "_cw", [P, CONV, TAPS], F32))
            wqkvz = c2.enter_context(nc.sbuf_tensor(tag + "_wqkvz", [P, CONV], F32))
            S = signals(nc, c2, "weights_loaded alog_exp dve_step pool_step")
            with nc.Block() as block:
                loads = [
                    (cw[:], W["L0_attn_a_conv_w"].partition_broadcast(P)),
                    (wqkvz[:], W["L0_attn_a_W_qkvz"][:, 0:CONV]),
                    (wz[:], W["L0_attn_a_W_qkvz"][:, CONV:CONV + VAL]),
                    (wba[:], W["L0_attn_a_W_ba"]),
                    (wout[:], W["L0_attn_a_W_out"].rearrange("(h d) n -> d h n", h=HV)),
                    (wrouter[:], W["L0_attn_a_W_router"]),
                    (wgate[:], W["L0_attn_a_W_gate_e"].rearrange("e h i -> h e i")),
                    (wup[:], W["L0_attn_a_W_up_e"].rearrange("e h i -> h e i")),
                    (wdown[:], W["L0_attn_a_W_down_e"].rearrange("(c e) i h -> (e i) c h", e=2)),
                    (ln1[:], W["L0_attn_a_w_ln1"].unsqueeze(1)),
                    (ln2[:], W["L0_attn_a_w_ln2"].unsqueeze(1)),
                    (dtb[:], W["L0_attn_a_dt_bias"].partition_broadcast(P)),
                    (nega[:], W["L0_attn_a_A_log"].partition_broadcast(P)),
                    (gnw[:], W["L0_attn_a_gate_norm_w"].partition_broadcast(P)),
                    (tri[:], W["tri_masks"]),
                ]

                @block.sync
                def _(sp):
                    for dst, src in loads:
                        sp.dma_start(dst, src).then_inc(S["weights_loaded"], 16)

                @block.gpsimd
                def _(pool):
                    pool.memset(x1T[:], 0.0)
                    pool.memset(state[:], 0.0)
                    pool.iota(iota8[:], [[1, NEXP]], base=0, channel_multiplier=0,
                              allow_small_or_imprecise_dtypes=True)

                @block.scalar
                def _(act):
                    act.wait_ge(S["weights_loaded"], 16 * len(loads))
                    act.activation(nega[:], nega[:], ACT.Exp).then_inc(S["alog_exp"], 1)

                @block.vector
                def _(dve):
                    dve.wait_ge(S["weights_loaded"], 16 * len(loads))
                    for j in range(TAPS):
                        dve.tensor_tensor(wconv[:, j, :], wqkvz[:], cw[:, :, j], ALU.mult)
                    dve.tensor_scalar(ln1[:], ln1[:], 1.0, None, ALU.add)
                    dve.tensor_scalar(ln2[:], ln2[:], 1.0, None, ALU.add)
                    dve.wait_ge(S["alog_exp"], 1)
                    dve.tensor_scalar(nega[:], nega[:], -1.0, None, ALU.mult)
            clear_signals(nc, S)

        xt = sb("xt", [P, DIM])
        stats, mv, rstd = sb("stats", [P, 6]), sb("mv", [P, 2]), sb("rstd", [P, 1])
        h0 = sb("h0", [P, DIM])
        sq = sb("sq", [P, 1024])
        ms = sb("ms", [P, 1])
        x1 = sb("x1", [P, DIM])
        qk = sb("qk", [P, 2 * HK, D])
        val = sb("val", [P, HV, D])
        zs = sb("zs", [P, HV, D])
        ya, ny, eb, ea, la, beta, nbeta, g = (sb(n, [P, HV]) for n in "ya ny eb ea la beta nbeta g".split())
        qkss = sb("qkss", [P, 2 * HK])
        rn, rtmp = sb("rn", [P, 8]), sb("rtmp", [P, 8])
        qkn = sb("qkn", [P, 2 * HK, D])
        qkT = sb("qkT", [P, 2 * HK, P])
        gm = sb("gm", [P, HV, P])
        et = sb("et", [P, HV, P])
        etm = sb("etm", [P, HV, P])
        etb = sb("etb", [P, HV, P])
        eg = sb("eg", [P, 3, HV])
        probsT = sb("probsT", [P, HV, P])
        NT = sb("NT", [P, HV, P])
        Y = sb("Y", [P, HV, P])
        T = sb("T", [P, HV, P])
        NTp = sb("NTp", [P, HV, P])
        R = sb("R", [P, HV, D])
        U = sb("U", [P, HV, D])
        UD = sb("UD", [P, HV, D])
        qs = sb("qs", [P, HV, D])
        core = sb("core", [P, HV, D])
        oss = sb("oss", [P, HV])
        coreT = sb("coreT", [P, HV, P])
        h1 = sb("h1", [P, DIM])
        x2 = sb("x2", [P, DIM])
        x2T = sb("x2T", [P, P])
        lmax, rl, el, esum = sb("lmax", [P, 8]), sb("rl", [P, NEXP]), sb("el", [P, NEXP]), sb("esum", [P, 1])
        nmax = sb("nmax", [P, 1])
        eidx, eidf = sb("eidx", [P, 8], U32), sb("eidf", [P, 8])
        pick = sb("pick", [P, 3, NEXP])
        route = sb("route", [P, NEXP])
        sg = sb("sg", [P, NEXP, INTER])
        hid = sb("hid", [P, NEXP, INTER])
        hidT = sb("hidT", [P, 4, P])

        def banks(a, n=1):
            return ps[:, a:a + n, :].rearrange("p b n -> p (b n)")

        def bank_heads(a, n):
            return heads(banks(a, n), 4 * n)

        S = signals(nc, ctx, """x1_ready x1T_ps halo x1T_ready ba_ps qk_ps v_ps z_ps v_silu z_silu qk_silu
            gate_in gate_exp gate_ln g_ready gm_ready gsum_ps decay_ps decay_exp eg_ready qkn_ready qkT_ps qkT_ready
            gram_ps et_masked probs_ready NT_ready Y_ready T_ps T_ready NTp_ps NTp_ready delta_ps TY_ready
            kS_ps R_ready W_ps U_ready qS_ps qs_ready intra_ps state_ps state_ready core_ready coreT_ps coreT_ready
            out_ps x2_ready x2T_ps x2T_ready router_ps gateup_ps nmax_ready el_ready sg_ready hid_ready hidT_ps
            hidT_ready down_ps dve_step pool_step""")

        with nc.Fori(0, TILES) as t:
            with nc.Block() as block:

                @block.tensor
                def _(pe):
                    pe.wait_ge(S["x1_ready"], 1)
                    pe.transpose(banks(7)[:, 0:P], x1[:], ident).then_inc(S["x1T_ps"], 1)
                    pe.wait_ge(S["x1T_ready"], 1)
                    pe.matmul(banks(6)[:, 0:2 * HV], x1T[:, 3:3 + P], wba[:], start=True, stop=True)\
                        .then_inc(S["ba_ps"], 1)
                    for b, sig in ((0, None), (1, "qk_ps"), (2, None), (3, "v_ps")):
                        for j in range(TAPS):
                            mm = pe.matmul(banks(b), x1T[:, j:j + P], wconv[:, j, b * 512:b * 512 + 512],
                                           start=(j == 0), stop=(j == TAPS - 1))
                        if sig:
                            mm.then_inc(S[sig], 1)
                    for b in range(2):
                        mm = pe.matmul(banks(4 + b), x1T[:, 3:3 + P], wz[:, b * 512:b * 512 + 512],
                                       start=True, stop=True)
                    mm.then_inc(S["z_ps"], 1)
                    pe.wait_ge(S["g_ready"], 1)
                    pe.matmul(banks(6)[:, 32:40], upto, g[:], start=True, stop=True)
                    pe.matmul(banks(6)[:, 40:48], after, g[:], start=True, stop=True)
                    pe.matmul(banks(6)[:, 48:56], ones, g[:], start=True, stop=True).then_inc(S["gsum_ps"], 1)
                    pe.wait_ge(S["qkn_ready"], 1)
                    for h in range(2 * HK):
                        mm = pe.transpose(bank_heads(0, 2)[:, h, :], qkn[:, h, :], ident)
                    mm.then_inc(S["qkT_ps"], 1)
                    pe.wait_ge(S["gm_ready"], 1)
                    pe.wait_ge(S["z_silu"], 1)
                    for h in range(HV):
                        mm = pe.matmul(bank_heads(4, 2)[:, h, :], gm[:, h, :], upto, start=True, stop=True)
                    mm.then_inc(S["decay_ps"], 1)
                    pe.wait_ge(S["qkT_ready"], 1)
                    pe.wait_ge(S["v_silu"], 1)
                    for h in range(HK):
                        kT = qkT[:, HK + h, :]
                        pe.matmul(bank_heads(2, 1)[:, h, :], kT, kT, start=True, stop=True)
                        mm = pe.matmul(bank_heads(3, 1)[:, h, :], kT, qkT[:, h, :], start=True, stop=True)
                    mm.then_inc(S["gram_ps"], 1)
                    pe.wait_ge(S["Y_ready"], 1)
                    for h in range(HV):
                        mm = pe.transpose(bank_heads(0, 2)[:, h, :], Y[:, h, :], ident)
                    mm.then_inc(S["T_ps"], 1)
                    pe.wait_ge(S["T_ready"], 1)
                    pe.wait_ge(S["decay_exp"], 1)
                    for l in range(1, LEVELS):
                        if l > 1:
                            pe.wait_ge(S["TY_ready"], l - 1)
                        for h in range(HV):
                            mm = pe.matmul(bank_heads(4, 2)[:, h, :], NT[:, h, :], T[:, h, :], start=True, stop=True)
                        mm.then_inc(S["NTp_ps"], 1)
                        pe.wait_ge(S["NTp_ready"], l)
                        if l == 1:
                            pe.wait_ge(S["eg_ready"], 1)
                        for h in range(HV):
                            if l < LEVELS - 1:
                                pe.matmul(bank_heads(0, 2)[:, h, :], Y[:, h, :], NTp[:, h, :], start=True, stop=True)
                            mm = pe.matmul(bank_heads(6, 2)[:, h, :], NTp[:, h, :], Y[:, h, :], start=True, stop=True)
                        mm.then_inc(S["delta_ps"], 1)
                    for h in range(HK):
                        pair = slice(REP * h, REP * h + REP)
                        mm = pe.matmul(bank_heads(0, 2)[:, pair, :], qkT[:, HK + h, :], state[:, pair, :],
                                       start=True, stop=True)
                    mm.then_inc(S["kS_ps"], 1)
                    pe.wait_ge(S["TY_ready"], LEVELS - 1)
                    for h in range(HK):
                        pair = slice(REP * h, REP * h + REP)
                        mm = pe.matmul(bank_heads(6, 2)[:, pair, :], qkT[:, h, :], state[:, pair, :],
                                       start=True, stop=True)
                    mm.then_inc(S["qS_ps"], 1)
                    pe.wait_ge(S["R_ready"], 1)
                    pe.wait_ge(S["NT_ready"], 1)
                    for h in range(HV):
                        mm = pe.matmul(bank_heads(2, 2)[:, h, :], Y[:, h, :], R[:, h, :], start=True, stop=True)
                    mm.then_inc(S["W_ps"], 1)
                    pe.wait_ge(S["U_ready"], 1)
                    for h in range(HV):
                        mm = pe.matmul(bank_heads(4, 2)[:, h, :], probsT[:, h, :], U[:, h, :], start=True, stop=True)
                    mm.then_inc(S["intra_ps"], 1)
                    for h in range(HK):
                        pair = slice(REP * h, REP * h + REP)
                        mm = pe.matmul(bank_heads(0, 2)[:, pair, :], qkn[:, HK + h, :], UD[:, pair, :],
                                       start=True, stop=True)
                    mm.then_inc(S["state_ps"], 1)
                    pe.wait_ge(S["core_ready"], 1)
                    for h in range(HV):
                        mm = pe.transpose(bank_heads(2, 2)[:, h, :], core[:, h, :], ident)
                    mm.then_inc(S["coreT_ps"], 1)
                    pe.wait_ge(S["coreT_ready"], 1)
                    for h in range(HV):
                        mm = pe.matmul(banks(4)[:, 0:DIM], coreT[:, h, :], wout[:, h, :],
                                       start=(h == 0), stop=(h == HV - 1))
                    mm.then_inc(S["out_ps"], 1)
                    pe.wait_ge(S["x2_ready"], 1)
                    pe.transpose(banks(5)[:, 0:P], x2[:], ident).then_inc(S["x2T_ps"], 1)
                    pe.wait_ge(S["x2T_ready"], 1)
                    pe.matmul(banks(5)[:, 0:NEXP], x2T[:], wrouter[:], start=True, stop=True)\
                        .then_inc(S["router_ps"], 1)
                    pe.matmul(banks(6), x2T[:], wgate[:].rearrange("p e i -> p (e i)"), start=True, stop=True)
                    pe.matmul(banks(7), x2T[:], wup[:].rearrange("p e i -> p (e i)"), start=True, stop=True)\
                        .then_inc(S["gateup_ps"], 1)
                    pe.wait_ge(S["hid_ready"], 1)
                    for c in range(4):
                        mm = pe.transpose(bank_heads(2, 1)[:, c, :],
                                          hid[:, 2 * c:2 * c + 2, :].rearrange("p e i -> p (e i)"), ident)
                    mm.then_inc(S["hidT_ps"], 1)
                    pe.wait_ge(S["hidT_ready"], 1)
                    for c in range(4):
                        mm = pe.matmul(banks(3)[:, 0:DIM], hidT[:, c, :], wdown[:, c, :], start=(c == 0), stop=(c == 3))
                    mm.then_inc(S["down_ps"], 1)

                @block.scalar
                def _(act):
                    act.activation(x1T[:, 0:3], x1T[:, P:P + 3], ACT.Copy).then_inc(S["halo"], 1)
                    act.wait_ge(S["halo"], 1)
                    act.wait_ge(S["x1T_ps"], 1)
                    act.activation(x1T[:, 3:3 + P], banks(7)[:, 0:P], ACT.Copy, scale=ln1[:])\
                        .then_inc(S["x1T_ready"], 1)
                    act.wait_ge(S["gate_in"], 1)
                    act.activation(ea[:], ny[:], ACT.Exp)
                    act.activation(eb[:], banks(6)[:, 0:HV], ACT.Exp, scale=-1.0).then_inc(S["gate_exp"], 1)
                    act.wait_ge(S["gate_exp"], 1)
                    act.activation(la[:], ea[:], ACT.Ln, bias=1.0).then_inc(S["gate_ln"], 1)
                    act.wait_ge(S["qk_ps"], 1)
                    act.activation(qk[:].rearrange("p h d -> p (h d)"), banks(0, 2), ACT.Silu)\
                        .then_inc(S["qk_silu"], 1)
                    act.wait_ge(S["v_ps"], 1)
                    act.activation(val[:].rearrange("p h d -> p (h d)"), banks(2, 2), ACT.Silu)\
                        .then_inc(S["v_silu"], 1)
                    act.wait_ge(S["z_ps"], 1)
                    act.activation(zs[:].rearrange("p h d -> p (h d)"), banks(4, 2), ACT.Silu)\
                        .then_inc(S["z_silu"], 1)
                    act.wait_ge(S["qkT_ps"], 1)
                    act.activation(qkT[:].rearrange("p h d -> p (h d)"), banks(0, 2), ACT.Copy)\
                        .then_inc(S["qkT_ready"], 1)
                    act.wait_ge(S["gsum_ps"], 1)
                    act.activation(eg[:].rearrange("p a h -> p (a h)"), banks(6)[:, 32:56], ACT.Exp)\
                        .then_inc(S["eg_ready"], 1)
                    act.wait_ge(S["decay_ps"], 1)
                    act.activation(et[:].rearrange("p h d -> p (h d)"), banks(4, 2), ACT.Exp)\
                        .then_inc(S["decay_exp"], 1)
                    act.wait_ge(S["T_ps"], 1)
                    act.activation(T[:].rearrange("p h d -> p (h d)"), banks(0, 2), ACT.Copy)\
                        .then_inc(S["T_ready"], 1)
                    for l in range(1, LEVELS):
                        act.wait_ge(S["NTp_ps"], l)
                        act.activation(NTp[:].rearrange("p h d -> p (h d)"), banks(4, 2), ACT.Copy)\
                            .then_inc(S["NTp_ready"], 1)
                    act.wait_ge(S["coreT_ps"], 1)
                    act.activation(coreT[:].rearrange("p h d -> p (h d)"), banks(2, 2), ACT.Copy)\
                        .then_inc(S["coreT_ready"], 1)
                    act.wait_ge(S["x2T_ps"], 1)
                    act.activation(x2T[:], banks(5)[:, 0:P], ACT.Copy, scale=ln2[:]).then_inc(S["x2T_ready"], 1)
                    act.wait_ge(S["nmax_ready"], 1)
                    act.activation(el[:], rl[:], ACT.Exp, bias=nmax[:], accum_out=esum[:]).then_inc(S["el_ready"], 1)
                    act.wait_ge(S["gateup_ps"], 1)
                    act.activation(sg[:].rearrange("p e i -> p (e i)"), banks(6), ACT.Silu).then_inc(S["sg_ready"], 1)
                    act.wait_ge(S["hidT_ps"], 1)
                    act.activation(hidT[:].rearrange("p c n -> p (c n)"), banks(2), ACT.Copy)\
                        .then_inc(S["hidT_ready"], 1)

                @block.gpsimd
                def _(pool):
                    pool.wait_ge(S["g_ready"], 1)
                    pool.tensor_tensor(gm[:], over_middle(after, HV), over_inner(g[:], P), ALU.mult)\
                        .then_inc(S["gm_ready"], 1)
                    pool.wait_ge(S["decay_exp"], 1)
                    pool.tensor_tensor(etm[:], et[:], over_middle(upto, HV), ALU.mult).then_inc(S["et_masked"], 1)

                @block.vector
                def _(dve):
                    link = counted(dve, S["dve_step"])
                    link(dve.tensor_copy(xt[:], tile_of(X, t)))
                    link(normalize_rows(dve, link, xt[:], h0[:], stats[:], mv[:], rstd[:]))
                    link(dve.tensor_tensor_reduce(sq[:, 0:DIM], h0[:], h0[:], 1.0, 0.0, ALU.mult, ALU.add, ms[:]))
                    link(dve.tensor_scalar(ms[:], ms[:], 1.0 / DIM, EPS, ALU.mult, ALU.add))
                    inv_sqrt(dve, link, ms[:], rstd[:], stats[:, 0:1])
                    dve.tensor_scalar(x1[:], h0[:], rstd[:], None, ALU.mult).then_inc(S["x1_ready"], 1)
                    dve.wait_ge(S["ba_ps"], 1)
                    link(dve.tensor_tensor(ya[:], banks(6)[:, HV:2 * HV], dtb[:], ALU.add))
                    dve.scalar_tensor_tensor(out=ny[:], in0=ya[:], scalar=-1.0, in1=ya[:],
                                             op0=ALU.mult, op1=ALU.min).then_inc(S["gate_in"], 1)
                    dve.wait_ge(S["gate_ln"], 1)
                    link(dve.scalar_tensor_tensor(out=la[:], in0=ya[:], scalar=0.0, in1=la[:],
                                                  op0=ALU.max, op1=ALU.add))
                    dve.tensor_tensor(g[:], la[:], nega[:], ALU.mult).then_inc(S["g_ready"], 1)
                    link(dve.tensor_scalar(eb[:], eb[:], 1.0, None, ALU.add))
                    link(dve.reciprocal(beta[:], eb[:]))
                    link(dve.tensor_scalar(nbeta[:], beta[:], -1.0, None, ALU.mult))
                    dve.wait_ge(S["qk_silu"], 1)
                    link(dve.tensor_tensor(heads(sq[:], 8), qk[:], qk[:], ALU.mult))
                    link(dve.tensor_reduce(qkss[:], heads(sq[:], 8), X_AXIS, ALU.add))
                    link(dve.tensor_scalar(qkss[:], qkss[:], EPS, None, ALU.add))
                    inv_sqrt(dve, link, qkss[:], rn[:], rtmp[:])
                    link(dve.tensor_scalar(rn[:, 0:HK], rn[:, 0:HK], D ** -0.5, None, ALU.mult))
                    dve.tensor_tensor(qkn[:], qk[:], over_inner(rn[:], D), ALU.mult).then_inc(S["qkn_ready"], 1)
                    dve.wait_ge(S["decay_exp"], 1)
                    link(dve.tensor_tensor(etb[:], et[:], over_inner(nbeta[:], P), ALU.mult))
                    dve.wait_ge(S["gram_ps"], 1)
                    for r in range(REP):
                        link(dve.tensor_tensor(NT[:, r::REP, :], bank_heads(2, 1), etb[:, r::REP, :], ALU.mult))
                    link(dve.tensor_copy(Y[:], over_middle(ident, HV)))
                    dve.copy_predicated(Y[:], over_middle(tri[:, LEVELS, :], HV), NT[:]).then_inc(S["Y_ready"], 1)
                    dve.wait_ge(S["et_masked"], 1)
                    for r in range(REP):
                        ins = dve.tensor_tensor(probsT[:, r::REP, :], bank_heads(3, 1), etm[:, r::REP, :], ALU.mult)
                    ins.then_inc(S["NT_ready"], 1)
                    dve.wait_ge(S["T_ready"], 1)
                    dve.wait_ge(S["Y_ready"], 1)
                    for l in range(1, LEVELS):
                        dve.wait_ge(S["delta_ps"], l)
                        if l > 1:
                            dve.wait_ge(S["TY_ready"], l - 1)
                        if l < LEVELS - 1:
                            link(dve.copy_predicated(T[:], over_middle(tri[:, l, :], HV), bank_heads(0, 2)))
                        dve.copy_predicated(Y[:], over_middle(tri[:, LEVELS + l, :], HV), bank_heads(6, 2))\
                            .then_inc(S["TY_ready"], 1)
                    dve.wait_ge(S["kS_ps"], 1)
                    dve.wait_ge(S["eg_ready"], 1)
                    link(dve.tensor_tensor(R[:], bank_heads(0, 2), over_inner(eg[:, 0, :], D), ALU.mult))
                    dve.tensor_tensor(R[:], val[:], R[:], ALU.subtract).then_inc(S["R_ready"], 1)
                    dve.wait_ge(S["qS_ps"], 1)
                    link(dve.tensor_tensor(qs[:], bank_heads(6, 2), over_inner(eg[:, 0, :], D), ALU.mult))
                    dve.wait_ge(S["W_ps"], 1)
                    link(dve.tensor_tensor(U[:], bank_heads(2, 2), over_inner(beta[:], D), ALU.mult))
                    dve.tensor_tensor(UD[:], U[:], over_inner(eg[:, 1, :], D), ALU.mult).then_inc(S["U_ready"], 1)
                    dve.wait_ge(S["intra_ps"], 1)
                    link(dve.tensor_tensor(core[:], bank_heads(4, 2), qs[:], ALU.add))
                    link(dve.tensor_tensor(heads(sq[:], 8), core[:], core[:], ALU.mult))
                    link(dve.tensor_reduce(oss[:], heads(sq[:], 8), X_AXIS, ALU.add))
                    link(dve.tensor_scalar(oss[:], oss[:], 1.0 / D, EPS, ALU.mult, ALU.add))
                    inv_sqrt(dve, link, oss[:], rn[:], rtmp[:])
                    link(dve.tensor_tensor(core[:], core[:], over_inner(rn[:], D), ALU.mult))
                    link(dve.tensor_tensor(core[:], core[:], over_middle(gnw[:], HV), ALU.mult))
                    dve.wait_ge(S["z_silu"], 1)
                    dve.tensor_tensor(core[:], core[:], zs[:], ALU.mult).then_inc(S["core_ready"], 1)
                    dve.wait_ge(S["state_ps"], 1)
                    link(dve.tensor_tensor(state[:], state[:], over_inner(eg[:, 2, :], D), ALU.mult))
                    link(dve.tensor_tensor(state[:], bank_heads(0, 2), state[:], ALU.add))
                    dve.wait_ge(S["out_ps"], 1)
                    link(dve.tensor_tensor(h1[:], banks(4)[:, 0:DIM], h0[:], ALU.add))
                    link(dve.tensor_tensor_reduce(sq[:, 0:DIM], h1[:], h1[:], 1.0, 0.0, ALU.mult, ALU.add, ms[:]))
                    link(dve.tensor_scalar(ms[:], ms[:], 1.0 / DIM, EPS, ALU.mult, ALU.add))
                    inv_sqrt(dve, link, ms[:], rstd[:], stats[:, 0:1])
                    dve.tensor_scalar(x2[:], h1[:], rstd[:], None, ALU.mult).then_inc(S["x2_ready"], 1)
                    dve.wait_ge(S["router_ps"], 1)
                    link(dve.tensor_copy(rl[:], banks(5)[:, 0:NEXP]))
                    link(dve.max(lmax[:], rl[:]))
                    dve.tensor_scalar(nmax[:], lmax[:, 0:1], -1.0, None, ALU.mult).then_inc(S["nmax_ready"], 1)
                    link(dve.max_index(eidx[:], lmax[:], rl[:]))
                    link(dve.tensor_copy(eidf[:], eidx[:]))
                    dve.tensor_scalar(pick[:, 0, :], iota8[:], eidf[:, 0:1], None, ALU.is_equal)
                    link(dve.tensor_scalar(pick[:, 1, :], iota8[:], eidf[:, 1:2], None, ALU.is_equal))
                    link(dve.tensor_tensor(pick[:, 0, :], pick[:, 0, :], pick[:, 1, :], ALU.add))
                    dve.wait_ge(S["el_ready"], 1)
                    link(dve.tensor_tensor_reduce(pick[:, 2, :], el[:], pick[:, 0, :], 1.0, 0.0,
                                                  ALU.mult, ALU.add, ms[:]))
                    link(dve.reciprocal(ms[:], ms[:]))
                    link(dve.tensor_scalar(route[:], pick[:, 2, :], ms[:], None, ALU.mult))
                    dve.wait_ge(S["sg_ready"], 1)
                    link(dve.tensor_tensor(hid[:], heads(banks(7), NEXP), sg[:], ALU.mult))
                    dve.tensor_tensor(hid[:], hid[:], over_inner(route[:], INTER), ALU.mult)\
                        .then_inc(S["hid_ready"], 1)
                    dve.wait_ge(S["down_ps"], 1)
                    link(dve.tensor_tensor(h1[:], banks(3)[:, 0:DIM], h1[:], ALU.add))
                    dve.tensor_tensor(tile_of(X, t), h1[:], xt[:], ALU.add)
            clear_signals(nc, S)



GROUP = 4


def group_buffers(sb):
    return {"stats": sb("gstats", [P, GROUP, 6]), "mv": sb("gmv", [P, GROUP, 2]),
            "var": sb("gvar", [P, GROUP]), "rstd": sb("grstd", [P, GROUP]), "tmp": sb("gtmp", [P, GROUP])}


def normalize_group(dve, link, x, out, B):
    for i in range(GROUP):
        link(dve.bn_stats(B["stats"][:, i, :], x[:, i, :]))
    for i in range(GROUP):
        link(dve.bn_aggr(B["mv"][:, i, :], B["stats"][:, i, :]))
    link(dve.tensor_scalar(B["var"][:], B["mv"][:, :, 1], LN_EPS, None, ALU.add))
    inv_sqrt(dve, link, B["var"][:], B["rstd"][:], B["tmp"][:])
    for i in range(GROUP - 1):
        link(dve.tensor_scalar(out[:, i, :], x[:, i, :], B["mv"][:, i, 0:1], B["rstd"][:, i:i + 1],
                               ALU.subtract, ALU.mult))
    i = GROUP - 1
    return dve.tensor_scalar(out[:, i, :], x[:, i, :], B["mv"][:, i, 0:1], B["rstd"][:, i:i + 1],
                             ALU.subtract, ALU.mult)



def ternary_layer(nc, W, C, X, tag):
    ident, ones = C["ident"], C["ones"]
    with ExitStack() as ctx:
        def sb(name, shape, dt=F32):
            return ctx.enter_context(nc.sbuf_tensor(f"{tag}_{name}", shape, dt))

        w, wabs, wpos, wneg = (sb(n, [P, DIM]) for n in ("w", "wabs", "wpos", "wneg"))
        wT = sb("wT", [P, DIM])
        rowsum, delta, ndelta, alpha = (sb(n, [P, 1]) for n in ("rowsum", "delta", "ndelta", "alpha"))
        bias = sb("bias", [P, DIM])
        xg, xn, xnT = sb("xg", [P, GROUP, DIM]), sb("xn", [P, GROUP, DIM]), sb("xnT", [P, GROUP, P])
        B = group_buffers(sb)
        ps = ctx.enter_context(nc.psum_tensor(tag + "_ps", [P, 2, GROUP, 128], F32))

        S = signals(nc, ctx, "loaded rowsum_ready total_ps w_ready wT_ps xn_ready xnT_ps xnT_ready y_ps dve_step")
        with nc.Block() as block:

            @block.sync
            def _(sp):
                sp.dma_start(w[:], W["L0_ffn_weight"]).then_inc(S["loaded"], 16)
                sp.dma_start(alpha[:], W["L0_ffn_alpha"].partition_broadcast(P)).then_inc(S["loaded"], 16)
                sp.dma_start(bias[:], W["L0_ffn_bias"].partition_broadcast(P)).then_inc(S["loaded"], 16)

            @block.vector
            def _(dve):
                link = counted(dve, S["dve_step"])
                dve.wait_ge(S["loaded"], 48)
                link(dve.scalar_tensor_tensor(out=wabs[:], in0=w[:], scalar=-1.0, in1=w[:], op0=ALU.mult, op1=ALU.max))
                dve.tensor_reduce(rowsum[:], wabs[:], X_AXIS, ALU.add).then_inc(S["rowsum_ready"], 1)
                dve.wait_ge(S["total_ps"], 1)
                link(dve.tensor_scalar(delta[:], ps[:, 0, 0, 0:1], 1.0 / (DIM * DIM), 0.7, ALU.mult, ALU.mult))
                link(dve.tensor_scalar(ndelta[:], delta[:], -1.0, None, ALU.mult))
                link(dve.tensor_scalar(wpos[:], w[:], delta[:], None, ALU.is_gt))
                link(dve.tensor_scalar(wneg[:], w[:], ndelta[:], None, ALU.is_lt))
                link(dve.tensor_tensor(wpos[:], wpos[:], wneg[:], ALU.subtract))
                dve.tensor_scalar(wpos[:], wpos[:], alpha[:], None, ALU.mult).then_inc(S["w_ready"], 1)
                dve.wait_ge(S["wT_ps"], 1)
                dve.tensor_copy(wT[:], ps[:, 1, 0, :])

            @block.tensor
            def _(pe):
                pe.wait_ge(S["rowsum_ready"], 1)
                pe.matmul(ps[:, 0, 0, 0:1], ones, rowsum[:], start=True, stop=True).then_inc(S["total_ps"], 1)
                pe.wait_ge(S["w_ready"], 1)
                pe.transpose(ps[:, 1, 0, :], wpos[:], ident).then_inc(S["wT_ps"], 1)
        clear_signals(nc, S)

        with nc.Fori(0, TILES // GROUP) as t:
            with nc.Block() as block:

                @block.tensor
                def _(pe):
                    pe.wait_ge(S["xn_ready"], 1)
                    for i in range(GROUP):
                        mm = pe.transpose(ps[:, 0, i, :], xn[:, i, :], ident)
                    mm.then_inc(S["xnT_ps"], 1)
                    pe.wait_ge(S["xnT_ready"], 1)
                    for i in range(GROUP):
                        mm = pe.matmul(ps[:, 1, i, :], xnT[:, i, :], wT[:], start=True, stop=True)
                    mm.then_inc(S["y_ps"], 1)

                @block.scalar
                def _(act):
                    act.wait_ge(S["xnT_ps"], 1)
                    act.activation(xnT[:], ps[:, 0], ACT.Copy).then_inc(S["xnT_ready"], 1)

                @block.vector
                def _(dve):
                    link = counted(dve, S["dve_step"])
                    link(dve.tensor_copy(xg[:], X[:, bass.ds(t * GROUP, GROUP), :]))
                    normalize_group(dve, link, xg, xn, B).then_inc(S["xn_ready"], 1)
                    dve.wait_ge(S["xn_ready"], 1)
                    link(dve.tensor_tensor(xg[:], xg[:], over_middle(bias[:], GROUP), ALU.add))
                    dve.wait_ge(S["y_ps"], 1)
                    dve.tensor_tensor(X[:, bass.ds(t * GROUP, GROUP), :], ps[:, 1], xg[:], ALU.add)
            clear_signals(nc, S)



def chunk_attention(nc, W, C, X, tag):
    H, HD, CH = 16, 8, 32
    QUADS = P // CH
    NCH = TOKENS // CH
    SCALE = float(1.0 / np.sqrt(np.float32(HD)))
    ident = C["ident"]
    with ExitStack() as ctx:
        def sb(name, shape, dt=F32):
            return ctx.enter_context(nc.sbuf_tensor(f"{tag}_{name}", shape, dt))

        wl = sb("wl", [P, 4, DIM])
        wg = sb("wg", [P, 4, DIM])
        hm = sb("hm", [P, H])
        mean4 = sb("mean4", [P, QUADS])
        spread = sb("spread", [NCH, TOKENS])
        sumT = sb("sumT", [P, NCH])
        ps = ctx.enter_context(nc.psum_tensor(tag + "_ps", [P, 8, 512], F32))

        xt, xl, xlT = sb("xt", [P, DIM]), sb("xl", [P, DIM]), sb("xlT", [P, P])
        stats, mv, rstd = sb("stats", [P, 6]), sb("mv", [P, 2]), sb("rstd", [P, 1])
        qT, v = sb("qT", [P, P]), sb("v", [P, DIM])
        kexp = sb("kexp", [P, H, P])
        mx, den = sb("mx", [P, H]), sb("den", [P, H])
        e, eT = sb("e", [P, H, CH]), sb("eT", [P, H, CH])
        ctxm = sb("ctxm", [P, QUADS, H, CH])
        ctxT = sb("ctxT", [P, P])
        chunk = sb("chunk", [P, DIM])
        xout = sb("xout", [P, DIM])
        S = signals(nc, ctx, """loaded xl_ready xlT_ps xlT_ready qkv_ps qTv_ready kexp_ready scores_ps shifted_ready
            exp_ready eT_ready ctx_ps ctxT_ready y_ps chunk_ready sum_ps dve_step""")
        with nc.Block() as block:

            @block.sync
            def _(sp):
                for i, n in enumerate(("Wq", "Wk", "Wv", "Wo")):
                    sp.dma_start(wl[:, i, :], W[f"L0_attn_b_{n}_l"]).then_inc(S["loaded"], 16)
                    sp.dma_start(wg[:, i, :], W[f"L0_attn_b_{n}_g"]).then_inc(S["loaded"], 16)
                sp.dma_start(hm[:], W["head8_mask"]).then_inc(S["loaded"], 16)
                sp.dma_start(mean4[:], W["mean4"]).then_inc(S["loaded"], 16)
                sp.dma_start(spread[:], W["spread"]).then_inc(S["loaded"], 16)
                sp.wait_ge(S["loaded"], 11 * 16)
        clear_signals(nc, S)

        with nc.Fori(0, TILES) as t:
            with nc.Block() as block:

                @block.tensor
                def _(pe):
                    pe.wait_ge(S["xl_ready"], 1)
                    pe.transpose(ps[:, 0, 0:P], xl[:], ident).then_inc(S["xlT_ps"], 1)
                    pe.wait_ge(S["xlT_ready"], 1)
                    pe.matmul(ps[:, 0, 128:256], wl[:, 0, :], xlT[:], start=True, stop=True)
                    pe.matmul(ps[:, 7, 128:256], wl[:, 1, :], xlT[:], start=True, stop=True)
                    pe.matmul(ps[:, 0, 384:512], xlT[:], wl[:, 2, :], start=True, stop=True).then_inc(S["qkv_ps"], 1)
                    pe.wait_ge(S["qTv_ready"], 1)
                    pe.wait_ge(S["kexp_ready"], 1)
                    for j in range(QUADS):
                        own = slice(CH * j, CH * j + CH)
                        mm = pe.matmul(ps[own, 1, :], qT[:, own], kexp[:, :, own], start=True, stop=True)
                    mm.then_inc(S["scores_ps"], 1)
                    pe.wait_ge(S["eT_ready"], 1)
                    for j in range(QUADS):
                        own = slice(CH * j, CH * j + CH)
                        mm = pe.matmul(ps[:, 2 + j, :], v[own, :], eT[own].rearrange("p h q -> p (h q)"),
                                       start=True, stop=True)
                    mm.then_inc(S["ctx_ps"], 1)
                    pe.wait_ge(S["ctxT_ready"], 1)
                    pe.matmul(ps[:, 6, 0:DIM], ctxT[:], wl[:, 3, :], start=True, stop=True).then_inc(S["y_ps"], 1)
                    pe.wait_ge(S["chunk_ready"], 1)
                    pe.matmul(ps[:, 7, 0:QUADS], chunk[:], mean4[:], start=True, stop=True).then_inc(S["sum_ps"], 1)

                @block.scalar
                def _(act):
                    act.wait_ge(S["xlT_ps"], 1)
                    act.activation(xlT[:], ps[:, 0, 0:P], ACT.Copy).then_inc(S["xlT_ready"], 1)
                    act.wait_ge(S["qkv_ps"], 1)
                    act.activation(qT[:], ps[:, 0, 128:256], ACT.Copy, scale=SCALE)
                    act.activation(v[:], ps[:, 0, 384:512], ACT.Copy).then_inc(S["qTv_ready"], 1)
                    act.wait_ge(S["shifted_ready"], 1)
                    act.activation(e[:], e[:], ACT.Exp).then_inc(S["exp_ready"], 1)

                @block.vector
                def _(dve):
                    link = counted(dve, S["dve_step"])
                    link(dve.tensor_copy(xt[:], tile_of(X, t)))
                    normalize_rows(dve, link, xt[:], xl[:], stats[:], mv[:], rstd[:]).then_inc(S["xl_ready"], 1)
                    dve.wait_ge(S["qkv_ps"], 1)
                    dve.tensor_tensor(kexp[:], over_middle(ps[:, 7, 128:256], H), over_inner(hm[:], P), ALU.mult)\
                        .then_inc(S["kexp_ready"], 1)
                    dve.wait_ge(S["scores_ps"], 1)
                    scores = heads(ps[:, 1, :], H)
                    link(dve.tensor_reduce(mx[:], scores, X_AXIS, ALU.max))
                    dve.tensor_tensor(e[:], scores, over_inner(mx[:], CH), ALU.subtract).then_inc(S["shifted_ready"], 1)
                    dve.wait_ge(S["exp_ready"], 1)
                    link(dve.tensor_reduce(den[:], e[:], X_AXIS, ALU.add))
                    link(dve.reciprocal(den[:], den[:]))
                    link(dve.tensor_tensor(e[:], e[:], over_inner(den[:], CH), ALU.mult))
                    dve.transpose(eT[:].rearrange("p h q -> p (h q)"), e[:].rearrange("p h k -> p (h k)"))\
                        .then_inc(S["eT_ready"], 1)
                    dve.wait_ge(S["ctx_ps"], 1)
                    own_head = hm[:].unsqueeze(1).unsqueeze(3).broadcast_to([P, QUADS, H, CH])
                    link(dve.tensor_tensor(ctxm[:], ps[:, 2:6, :].rearrange("p j (h q) -> p j h q", h=H),
                                           own_head, ALU.mult))
                    dve.tensor_reduce(ctxT[:].rearrange("p (j q) -> p j q", j=QUADS),
                                      ctxm[:].rearrange("p j h q -> p j q h"), X_AXIS, ALU.add)\
                        .then_inc(S["ctxT_ready"], 1)
                    dve.wait_ge(S["y_ps"], 1)
                    dve.wait_ge(S["xl_ready"], 1)
                    dve.tensor_tensor(chunk[:], ps[:, 6, 0:DIM], xl[:], ALU.add).then_inc(S["chunk_ready"], 1)
                    dve.wait_ge(S["chunk_ready"], 1)
                    dve.tensor_tensor(tile_of(X, t), chunk[:], xt[:], ALU.add)
                    dve.wait_ge(S["sum_ps"], 1)
                    dve.tensor_copy(sumT[:, bass.ds(t * QUADS, QUADS)], ps[:, 7, 0:QUADS])
            clear_signals(nc, S)

        summ, gqT, gv = sb("summ", [NCH, DIM]), sb("gqT", [P, NCH]), sb("gv", [NCH, DIM])
        gk = sb("gk", [P, H, NCH])
        ge, geT = sb("ge", [NCH, H, NCH]), sb("geT", [NCH, H, NCH])
        gm = sb("gm", [P, H, NCH])
        gctxT = sb("gctxT", [P, NCH])
        gout = sb("gout", [NCH, DIM])
        S2 = signals(nc, ctx, """proj_ps g_evac gk_ready gscores_ps gshifted gexp gnorm geT_ps geT_ready gctx_ps
            gctxT_ready gout_ps gout_ready spread_ps g_step""")
        with nc.Block() as block:

            @block.tensor
            def _(pe):
                pe.transpose(ps[0:NCH, 0, 0:P], sumT[:], ident)
                pe.matmul(ps[:, 0, 128:192], wg[:, 0, :], sumT[:], start=True, stop=True)
                pe.matmul(ps[:, 7, 128:192], wg[:, 1, :], sumT[:], start=True, stop=True)
                pe.matmul(ps[0:NCH, 0, 256:384], sumT[:], wg[:, 2, :], start=True, stop=True).then_inc(S2["proj_ps"], 1)
                pe.wait_ge(S2["g_evac"], 1)
                pe.wait_ge(S2["gk_ready"], 1)
                gkf = gk[:].rearrange("p h k -> p (h k)")
                for b in range(2):
                    mm = pe.matmul(ps[0:NCH, 1 + b, :], gqT[:], gkf[:, 512 * b:512 * b + 512], start=True, stop=True)
                mm.then_inc(S2["gscores_ps"], 1)
                pe.wait_ge(S2["gnorm"], 1)
                for h in range(H):
                    mm = pe.transpose(ps[0:NCH, 3 + h // 8, NCH * (h % 8):NCH * (h % 8) + NCH], ge[:, h, :],
                                      ident[0:NCH, 0:NCH])
                mm.then_inc(S2["geT_ps"], 1)
                pe.wait_ge(S2["geT_ready"], 1)
                geTf = geT[:].rearrange("p h q -> p (h q)")
                for b in range(2):
                    mm = pe.matmul(ps[:, 5 + b, :], gv[:], geTf[:, 512 * b:512 * b + 512], start=True, stop=True)
                mm.then_inc(S2["gctx_ps"], 1)
                pe.wait_ge(S2["gctxT_ready"], 1)
                pe.matmul(ps[0:NCH, 7, 0:DIM], gctxT[:], wg[:, 3, :], start=True, stop=True).then_inc(S2["gout_ps"], 1)
                pe.wait_ge(S2["gout_ready"], 1)
                for i in range(TILES):
                    mm = pe.matmul(ps[:, i // 4, 128 * (i % 4):128 * (i % 4) + DIM], spread[:, P * i:P * i + P],
                                   gout[:], start=True, stop=True)
                mm.then_inc(S2["spread_ps"], 1)

            @block.scalar
            def _(act):
                act.wait_ge(S2["proj_ps"], 1)
                act.activation(summ[:], ps[0:NCH, 0, 0:P], ACT.Copy)
                act.activation(gqT[:], ps[:, 0, 128:192], ACT.Copy, scale=SCALE)
                act.activation(gv[:], ps[0:NCH, 0, 256:384], ACT.Copy).then_inc(S2["g_evac"], 1)
                act.wait_ge(S2["gshifted"], 1)
                act.activation(ge[:], ge[:], ACT.Exp).then_inc(S2["gexp"], 1)
                act.wait_ge(S2["geT_ps"], 1)
                act.activation(geT[:].rearrange("p h q -> p (h q)"), ps[0:NCH, 3:5, :].rearrange("p b n -> p (b n)"),
                               ACT.Copy).then_inc(S2["geT_ready"], 1)

            @block.vector
            def _(dve):
                link = counted(dve, S2["g_step"])
                dve.wait_ge(S2["proj_ps"], 1)
                dve.tensor_tensor(gk[:], over_middle(ps[:, 7, 128:192], H), over_inner(hm[:], NCH), ALU.mult)\
                    .then_inc(S2["gk_ready"], 1)
                dve.wait_ge(S2["gscores_ps"], 1)
                scores = heads(ps[0:NCH, 1:3, :].rearrange("p b n -> p (b n)"), H)
                link(dve.tensor_reduce(mx[0:NCH], scores, X_AXIS, ALU.max))
                dve.tensor_tensor(ge[:], scores, over_inner(mx[0:NCH], NCH), ALU.subtract).then_inc(S2["gshifted"], 1)
                dve.wait_ge(S2["gexp"], 1)
                link(dve.tensor_reduce(den[0:NCH], ge[:], X_AXIS, ALU.add))
                link(dve.reciprocal(den[0:NCH], den[0:NCH]))
                dve.tensor_tensor(ge[:], ge[:], over_inner(den[0:NCH], NCH), ALU.mult).then_inc(S2["gnorm"], 1)
                dve.wait_ge(S2["gctx_ps"], 1)
                link(dve.tensor_tensor(gm[:], heads(ps[:, 5:7, :].rearrange("p b n -> p (b n)"), H),
                                       over_inner(hm[:], NCH), ALU.mult))
                dve.tensor_reduce(gctxT[:], gm[:].rearrange("p h q -> p q h"), X_AXIS, ALU.add)\
                    .then_inc(S2["gctxT_ready"], 1)
                dve.wait_ge(S2["gout_ps"], 1)
                dve.wait_ge(S2["g_evac"], 1)
                dve.tensor_tensor(gout[:], ps[0:NCH, 7, 0:DIM], summ[:], ALU.add).then_inc(S2["gout_ready"], 1)
                dve.wait_ge(S2["spread_ps"], 1)
                dve.tensor_tensor(X[:].rearrange("p t d -> p (t d)"), ps[:, 0:4, :].rearrange("p b n -> p (b n)"),
                                  X[:].rearrange("p t d -> p (t d)"), ALU.add)
        clear_signals(nc, S2)



def rotary_tables():
    half = np.arange(0, 64, 2, dtype=np.float32)
    inv_freq = (np.float32(1.0) / np.power(np.float32(10000.0), half / np.float32(64))).astype(np.float32)
    t = np.arange(TOKENS, dtype=np.float32)
    freqs = np.tile(t[:, None] * inv_freq[None, :], (1, 2)).astype(np.float32)
    base = ((half + np.float32(0.4 * 64)) / np.float32(1.4 * 64)).astype(np.float32)
    power = ((t - TOKENS // 2) / np.float32(32.0)).astype(np.float32)
    scale = np.tile(np.power(base[None, :], power[:, None]), (1, 2)).astype(np.float32)
    cos, sin = np.cos(freqs).astype(np.float32), np.sin(freqs).astype(np.float32)
    sin = np.concatenate([-sin[:, :32], sin[:, 32:]], 1)
    both = [np.stack([a * scale, a / scale], 1) for a in (cos, sin)]
    return [np.ascontiguousarray(a.reshape(TILES, P, 2, 64).transpose(1, 0, 2, 3).astype(np.float32)) for a in both]


def rope_tables():
    d = np.arange(0, 64, 2, dtype=np.float32) / np.float32(64)
    inv_freq = (np.float32(1.0) / np.power(np.float32(10000.0), d)).astype(np.float32)
    freqs = (np.arange(TOKENS, dtype=np.float32)[:, None] * inv_freq[None, :]).astype(np.float32)
    freqs = np.concatenate([freqs, freqs], 1).T
    return np.cos(freqs).astype(np.float32).copy(), np.sin(freqs).astype(np.float32).copy()


def band_masks():
    q, c = np.arange(P)[:, None], np.arange(P + 64)[None, :]
    near = (c - q >= 0) & (c - q <= 64)
    return np.stack([np.where(m, 0, -1e30) for m in (near & (c >= 64), near)], 1).astype(np.float32)


def shift_matrices():
    s = np.zeros((P, 2, P), np.float32)
    s[np.arange(P - 1), 0, np.arange(1, P)] = 1
    s[P - 1, 1, 0] = 1
    return s


def table_constants():
    rot_cos, rot_sin = rotary_tables()
    f = np.arange(P)
    c = np.arange(TOKENS // 32)
    rope_cos, rope_sin = rope_tables()
    return {
        "rope_cos": rope_cos,
        "rope_sin": rope_sin,
        "rot_cos": rot_cos,
        "rot_sin": rot_sin,
        "bands": band_masks(),
        "shift": shift_matrices(),
        "token_ids": (f[:, None] + P * np.arange(TILES)[None, :]).astype(np.float32),
        "rank_ids": (np.arange(80)[:, None] % 10).astype(np.float32),
        "head8_mask": (f[:, None] // 8 == np.arange(16)[None, :]).astype(np.float32),
        "mean4": np.where(f[:, None] // 32 == np.arange(4)[None, :], 1 / 32, 0).astype(np.float32),
        "spread": (c[:, None] == np.arange(TOKENS)[None, :] // 32).astype(np.float32),
    }



def sparse_attention(nc, W, C, X, tag):
    H, HD, TOP, LEAST = 16, 8, 10, 3
    HALF = H // 2 * TOP
    SCALE = float(1.0 / np.sqrt(np.float32(HD)))
    ROUND = float(3 << 22)
    LOWEST = -3.0e38
    GT = GROUP * P
    ident, ones = C["ident"], C["ones"]
    with ExitStack() as ctx:
        def sb(name, shape, dt=F32):
            return ctx.enter_context(nc.sbuf_tensor(f"{tag}_{name}", shape, dt))

        w = sb("w", [P, 4, DIM])
        wT = sb("wT", [P, 4, DIM])
        bq, bv, bo = sb("bq", [P, DIM]), sb("bv", [P, DIM]), sb("bo", [P, DIM])
        bk = sb("bk", [P, 1])
        hm, tokid = sb("hm", [P, H]), sb("tokid", [P, TILES])
        q_all, v_all = sb("q_all", [P, TILES, DIM]), sb("v_all", [P, TILES, DIM])
        kT_all = sb("kT_all", [P, TOKENS])
        qs = sb("qs", [H, TOKENS])
        tokrow = sb("tokrow", [HALF, TOKENS])
        ps = ctx.enter_context(nc.psum_tensor(tag + "_ps", [P, 8, 512], F32))

        xg, xn, xnT = sb("xg", [P, GROUP, DIM]), sb("xn", [P, GROUP, DIM]), sb("xnT", [P, GT])
        B = group_buffers(sb)
        qg = sb("qg", [P, GROUP, DIM])
        NH = GROUP * H
        e8, t8, lp = sb("e8", [P, NH, HD]), sb("t8", [P, NH, HD]), sb("lp", [P, NH, HD])
        m8, s8, l2, r8, ent, var8 = (sb(n, [P, NH]) for n in "m8 s8 l2 r8 ent var8".split())
        score = sb("score", [P, GROUP, H])
        tiny = sb("tiny", [P, 1])

        S = signals(nc, ctx, """loaded wT_ps wT_ready xn_ready xnT_ps xnT_ready qv_ps kT_ps kT_done shifted8 exp8
            prob_ready log_ready score_ready scoreT_ps dve_step pool_step""")
        with nc.Block() as block:

            @block.sync
            def _(sp):
                for i, n in enumerate("qkvo"):
                    sp.dma_start(w[:, i, :], W["L1_attn_a_W" + n]).then_inc(S["loaded"], 16)
                for dst, n in ((bq, "q"), (bv, "v"), (bo, "o")):
                    sp.dma_start(dst[:], W["L1_attn_a_b" + n].partition_broadcast(P)).then_inc(S["loaded"], 16)
                sp.dma_start(bk[:], W["L1_attn_a_bk"].unsqueeze(1)).then_inc(S["loaded"], 16)
                sp.dma_start(hm[:], W["head8_mask"]).then_inc(S["loaded"], 16)
                sp.dma_start(tokid[:], W["token_ids"]).then_inc(S["loaded"], 16)
                sp.wait_ge(S["loaded"], 10 * 16)

            @block.gpsimd
            def _(pool):
                pool.iota(tokrow[:], [[1, TOKENS]], base=0, channel_multiplier=0,
                          allow_small_or_imprecise_dtypes=True)
                pool.memset(tiny[:], 1e-9)

            @block.tensor
            def _(pe):
                pe.wait_ge(S["loaded"], 10 * 16)
                for i in range(4):
                    mm = pe.transpose(ps[:, 0, P * i:P * i + P], w[:, i, :], ident)
                mm.then_inc(S["wT_ps"], 1)

            @block.scalar
            def _(act):
                act.wait_ge(S["wT_ps"], 1)
                act.activation(wT[:].rearrange("p a n -> p (a n)"), ps[:, 0, :], ACT.Copy)
        clear_signals(nc, S)

        with nc.Fori(0, TILES // GROUP) as t:
            with nc.Block() as block:

                @block.tensor
                def _(pe):
                    pe.wait_ge(S["xn_ready"], 1)
                    for i in range(GROUP):
                        mm = pe.transpose(ps[:, 0, P * i:P * i + P], xn[:, i, :], ident)
                    mm.then_inc(S["xnT_ps"], 1)
                    pe.wait_ge(S["xnT_ready"], 1)
                    for i in range(GROUP):
                        pe.matmul(ps[:, 1, P * i:P * i + P], xnT[:, P * i:P * i + P], wT[:, 0, :], start=True, stop=True)
                        mm = pe.matmul(ps[:, 2, P * i:P * i + P], xnT[:, P * i:P * i + P], wT[:, 2, :],
                                       start=True, stop=True)
                    mm.then_inc(S["qv_ps"], 1)
                    pe.matmul(ps[:, 3, :], wT[:, 1, :], xnT[:], start=True, stop=True).then_inc(S["kT_ps"], 1)
                    pe.wait_ge(S["score_ready"], 1)
                    for i in range(GROUP):
                        mm = pe.transpose(ps[0:H, 4, P * i:P * i + P], score[:, i, :], ident)
                    mm.then_inc(S["scoreT_ps"], 1)

                @block.scalar
                def _(act):
                    act.wait_ge(S["xnT_ps"], 1)
                    act.activation(xnT[:], ps[:, 0, :], ACT.Copy).then_inc(S["xnT_ready"], 1)
                    act.wait_ge(S["kT_ps"], 1)
                    act.activation(kT_all[:, bass.ds(t * GT, GT)], ps[:, 3, :], ACT.Identity, bias=bk[:])
                    act.wait_ge(S["shifted8"], 1)
                    act.activation(e8[:], e8[:], ACT.Exp).then_inc(S["exp8"], 1)
                    act.wait_ge(S["prob_ready"], 1)
                    act.activation(lp[:], e8[:], ACT.Ln, bias=tiny[:]).then_inc(S["log_ready"], 1)

                @block.vector
                def _(dve):
                    link = counted(dve, S["dve_step"])
                    link(dve.tensor_copy(xg[:], X[:, bass.ds(t * GROUP, GROUP), :]))
                    normalize_group(dve, link, xg, xn, B).then_inc(S["xn_ready"], 1)
                    dve.wait_ge(S["qv_ps"], 1)
                    psq = ps[:, 1, :].rearrange("p (g d) -> p g d", g=GROUP)
                    psv = ps[:, 2, :].rearrange("p (g d) -> p g d", g=GROUP)
                    link(dve.tensor_tensor(qg[:], psq, over_middle(bq[:], GROUP), ALU.add))
                    dve.tensor_tensor(v_all[:, bass.ds(t * GROUP, GROUP), :], psv, over_middle(bv[:], GROUP), ALU.add)
                    dve.tensor_copy(q_all[:, bass.ds(t * GROUP, GROUP), :], qg[:])
                    q8 = qg[:].rearrange("p g (h e) -> p (g h) e", e=HD)
                    link(dve.tensor_reduce(m8[:], q8, X_AXIS, ALU.max))
                    dve.tensor_tensor(e8[:], q8, over_inner(m8[:], HD), ALU.subtract).then_inc(S["shifted8"], 1)
                    link(dve.tensor_tensor(t8[:], q8, q8, ALU.mult))
                    link(dve.tensor_reduce(s8[:], t8[:], X_AXIS, ALU.add))
                    inv_sqrt(dve, link, s8[:], l2[:], r8[:])
                    link(dve.tensor_tensor(l2[:], l2[:], s8[:], ALU.mult))
                    link(dve.tensor_reduce(s8[:], q8, X_AXIS, ALU.add))
                    link(dve.tensor_scalar(s8[:], s8[:], 1.0 / HD, None, ALU.mult))
                    link(dve.tensor_tensor(t8[:], q8, over_inner(s8[:], HD), ALU.subtract))
                    link(dve.tensor_tensor(t8[:], t8[:], t8[:], ALU.mult))
                    link(dve.tensor_reduce(var8[:], t8[:], X_AXIS, ALU.add))
                    dve.wait_ge(S["exp8"], 1)
                    link(dve.tensor_reduce(s8[:], e8[:], X_AXIS, ALU.add))
                    link(dve.reciprocal(s8[:], s8[:]))
                    dve.tensor_tensor(e8[:], e8[:], over_inner(s8[:], HD), ALU.mult).then_inc(S["prob_ready"], 1)
                    dve.wait_ge(S["log_ready"], 1)
                    link(dve.tensor_tensor(t8[:], e8[:], lp[:], ALU.mult))
                    link(dve.tensor_reduce(ent[:], t8[:], X_AXIS, ALU.add))
                    link(dve.tensor_scalar(ent[:], ent[:], -0.3, None, ALU.mult))
                    link(dve.scalar_tensor_tensor(out=ent[:], in0=l2[:], scalar=0.5, in1=ent[:],
                                                  op0=ALU.mult, op1=ALU.add))
                    dve.scalar_tensor_tensor(out=score[:].rearrange("p g h -> p (g h)"), in0=var8[:],
                                             scalar=0.2 / (HD - 1), in1=ent[:], op0=ALU.mult, op1=ALU.add)\
                        .then_inc(S["score_ready"], 1)
                    dve.wait_ge(S["scoreT_ps"], 1)
                    dve.tensor_copy(qs[:, bass.ds(t * GT, GT)], ps[0:H, 4, :])
            clear_signals(nc, S)

        qs2, dev = sb("qs2", [H, TOKENS]), sb("dev", [H, TOKENS])
        top = sb("top", [H, 2, 8])
        topi, topf = sb("topi", [H, 2, 8], U32), sb("topf", [H, 16])
        st, u, ut, ur = (sb(n, [H, 1]) for n in ("st", "u", "ut", "ur"))
        zexp = sb("zexp", [H, H, TOP])
        idx = sb("idx", [P, H * TOP])
        idxcol, ucol, valid = sb("idxcol", [HALF, 2]), sb("ucol", [HALF, 1]), sb("valid", [HALF, 1])
        rank = sb("rank", [HALF, 1])
        sel = sb("sel", [P, TILES, H * TOP])
        qexp = sb("qexp", [P, H, TOP])
        mrow, srow = sb("mrow", [HALF, 1]), sb("srow", [HALF, 1])
        probs = sb("probs", [HALF, TOKENS])
        probsT = sb("probsT", [P, TILES, H * TOP])
        oT = sb("oT", [P, H, TOP])
        ow = sb("ow", [HALF, 2, DIM])
        selT = sb("selT", [HALF, 2, TOKENS])
        A = signals(nc, ctx, """rank_loaded stats_ready z_ready idx_ps idx_ready cols_ps sel_ready q_ps qexp_ready
            top_scores_ps rowmax_ready probs_exp probs_ready probsT_ps probsT_ready o_ps oT_ready ow_ps ow_ready
            selT_ready y_ps top_step""")
        with nc.Block() as block:

            @block.sync
            def _(sp):
                sp.dma_start(rank[:], W["rank_ids"]).then_inc(A["rank_loaded"], 16)
                sp.wait_ge(A["rank_loaded"], 16)

            @block.tensor
            def _(pe):
                pe.wait_ge(A["z_ready"], 1)
                pe.matmul(ps[:, 0, 0:H * TOP], ones[0:H, :], zexp[:].rearrange("p h r -> p (h r)"),
                          start=True, stop=True).then_inc(A["idx_ps"], 1)
                pe.wait_ge(A["idx_ready"], 1)
                for g in range(2):
                    pe.matmul(ps[0:HALF, 1, g:g + 1], idx[0:1, HALF * g:HALF * g + HALF], ones[0:1, 0:1],
                              start=True, stop=True)
                pe.matmul(ps[0:HALF, 1, 2:3], ones[0:1, 0:HALF], u[0:1, :], start=True, stop=True)\
                    .then_inc(A["cols_ps"], 1)
                pe.wait_ge(A["sel_ready"], 1)
                for i in range(TILES):
                    mm = pe.matmul(ps[:, 7, 0:H * TOP], q_all[:, i, :], sel[:, i, :],
                                   start=(i == 0), stop=(i == TILES - 1))
                mm.then_inc(A["q_ps"], 1)
                pe.wait_ge(A["qexp_ready"], 1)
                for g in range(2):
                    if g:
                        pe.wait_ge(A["probs_exp"], 1)
                    for b in range(4):
                        mm = pe.matmul(ps[0:HALF, b, :], qexp[:, 8 * g:8 * g + 8, :].rearrange("p h r -> p (h r)"),
                                       kT_all[:, 512 * b:512 * b + 512], start=True, stop=True)
                    mm.then_inc(A["top_scores_ps"], 1)
                    pe.wait_ge(A["probs_ready"], g + 1)
                    if g:
                        pe.wait_ge(A["probsT_ready"], 1)
                    for i in range(TILES):
                        mm = pe.transpose(ps[:, 4 + i // 6, HALF * (i % 6):HALF * (i % 6) + HALF],
                                          probs[:, P * i:P * i + P], ident[0:HALF, 0:HALF])
                    mm.then_inc(A["probsT_ps"], 1)
                pe.wait_ge(A["probsT_ready"], 2)
                for i in range(TILES):
                    mm = pe.matmul(ps[:, 7, 0:H * TOP], v_all[:, i, :], probsT[:, i, :],
                                   start=(i == 0), stop=(i == TILES - 1))
                mm.then_inc(A["o_ps"], 1)
                pe.wait_ge(A["oT_ready"], 1)
                for g in range(2):
                    mm = pe.matmul(ps[0:HALF, 4, P * g:P * g + DIM],
                                   oT[:, 8 * g:8 * g + 8, :].rearrange("p h r -> p (h r)"), wT[:, 3, :],
                                   start=True, stop=True)
                mm.then_inc(A["ow_ps"], 1)
                pe.wait_ge(A["ow_ready"], 1)
                pe.wait_ge(A["selT_ready"], 1)
                for i in range(TILES):
                    for g in range(2):
                        mm = pe.matmul(ps[:, i // 4, P * (i % 4):P * (i % 4) + DIM], selT[:, g, P * i:P * i + P],
                                       ow[:, g, :], start=(g == 0), stop=(g == 1))
                mm.then_inc(A["y_ps"], 1)

            @block.scalar
            def _(act):
                for g in range(2):
                    act.wait_ge(A["rowmax_ready"], g + 1)
                    if g:
                        act.wait_ge(A["probsT_ps"], 1)
                    act.activation(probs[:], ps[0:HALF, 0:4, :].rearrange("p b n -> p (b n)"), ACT.Exp,
                                   scale=SCALE, bias=mrow[:], accum_out=srow[:]).then_inc(A["probs_exp"], 1)
                act.wait_ge(A["ow_ps"], 1)
                act.activation(ow[:].rearrange("p g n -> p (g n)"), ps[0:HALF, 4, 0:2 * P], ACT.Copy)\
                    .then_inc(A["ow_ready"], 1)

            @block.vector
            def _(dve):
                link = counted(dve, A["top_step"])
                link(dve.max(top[:, 0, :], qs[:]))
                link(dve.max_index(topi[:, 0, :], top[:, 0, :], qs[:]))
                link(dve.match_replace(out=qs2[:], in_to_replace=top[:, 0, :], in_values=qs[:], imm_value=LOWEST))
                link(dve.max(top[:, 1, :], qs2[:]))
                link(dve.max_index(topi[:, 1, :], top[:, 1, :], qs2[:]))
                link(dve.tensor_copy(topf[:], topi[:].rearrange("p a k -> p (a k)")))
                link(dve.tensor_reduce(st[:], qs[:], X_AXIS, ALU.add))
                link(dve.tensor_scalar(st[:], st[:], 1.0 / TOKENS, None, ALU.mult))
                link(dve.tensor_scalar(dev[:], qs[:], st[:], None, ALU.subtract))
                link(dve.tensor_tensor_reduce(qs2[:], dev[:], dev[:], 1.0, 0.0, ALU.mult, ALU.add, ur[:]))
                link(dve.tensor_scalar(ur[:], ur[:], 1.0 / (TOKENS - 1), None, ALU.mult))
                inv_sqrt(dve, link, ur[:], u[:], ut[:])
                link(dve.tensor_tensor(u[:], u[:], ur[:], ALU.mult))
                link(dve.tensor_scalar(st[:], st[:], 1e-6, None, ALU.add))
                link(dve.reciprocal(st[:], st[:]))
                link(dve.tensor_tensor(u[:], u[:], st[:], ALU.mult))
                link(dve.tensor_scalar(u[:], u[:], float(TOP), None, ALU.mult))
                link(dve.tensor_scalar(u[:], u[:], float(LEAST), float(TOP), ALU.max, ALU.min))
                link(dve.tensor_scalar(u[:], u[:], ROUND, None, ALU.add))
                link(dve.tensor_scalar(u[:], u[:], ROUND, None, ALU.subtract))
                dve.tensor_tensor(zexp[:], over_middle(topf[:, 0:TOP], H), over_inner(ident[0:H, 0:H], TOP), ALU.mult)\
                    .then_inc(A["z_ready"], 1)
                dve.wait_ge(A["idx_ps"], 1)
                dve.tensor_copy(idx[:], ps[:, 0, 0:H * TOP]).then_inc(A["idx_ready"], 1)
                dve.wait_ge(A["idx_ready"], 1)
                dve.tensor_tensor(sel[:], over_middle(idx[:], TILES), over_inner(tokid[:], H * TOP), ALU.is_equal)\
                    .then_inc(A["sel_ready"], 1)
                dve.wait_ge(A["cols_ps"], 1)
                dve.tensor_copy(idxcol[:], ps[0:HALF, 1, 0:2])
                link(dve.tensor_copy(ucol[:], ps[0:HALF, 1, 2:3]))
                dve.wait_ge(A["rank_loaded"], 16)
                link(dve.tensor_tensor(valid[:], rank[:], ucol[:], ALU.is_lt))
                for g in range(2):
                    ins = dve.tensor_scalar(selT[:, g, :], tokrow[:], idxcol[:, g:g + 1], None, ALU.is_equal)
                ins.then_inc(A["selT_ready"], 1)
                dve.wait_ge(A["q_ps"], 1)
                dve.tensor_tensor(qexp[:], heads(ps[:, 7, 0:H * TOP], H), over_inner(hm[:], TOP), ALU.mult)\
                    .then_inc(A["qexp_ready"], 1)
                for g in range(2):
                    dve.wait_ge(A["top_scores_ps"], g + 1)
                    link(dve.tensor_reduce(mrow[:], ps[0:HALF, 0:4, :].rearrange("p b n -> p (b n)"), X_AXIS, ALU.max))
                    dve.tensor_scalar(mrow[:], mrow[:], -SCALE, None, ALU.mult).then_inc(A["rowmax_ready"], 1)
                    dve.wait_ge(A["probs_exp"], g + 1)
                    link(dve.reciprocal(srow[:], srow[:]))
                    link(dve.tensor_tensor(srow[:], srow[:], valid[:], ALU.mult))
                    dve.tensor_scalar(probs[:], probs[:], srow[:], None, ALU.mult).then_inc(A["probs_ready"], 1)
                    dve.wait_ge(A["probsT_ps"], g + 1)
                    for b, n in enumerate((6, 6, 4)):
                        ins = dve.tensor_copy(probsT[:, 6 * b:6 * b + n, HALF * g:HALF * g + HALF],
                                              ps[:, 4 + b, 0:HALF * n].rearrange("p (i r) -> p i r", r=HALF))
                    ins.then_inc(A["probsT_ready"], 1)
                dve.wait_ge(A["o_ps"], 1)
                dve.tensor_tensor(oT[:], heads(ps[:, 7, 0:H * TOP], H), over_inner(hm[:], TOP), ALU.mult)\
                    .then_inc(A["oT_ready"], 1)
                link(dve.tensor_tensor(X[:], X[:], over_middle(bo[:], TILES), ALU.add))
                dve.wait_ge(A["y_ps"], 1)
                dve.tensor_tensor(X[:].rearrange("p t d -> p (t d)"), ps[:, 0:4, :].rearrange("p b n -> p (b n)"),
                                  X[:].rearrange("p t d -> p (t d)"), ALU.add)
        clear_signals(nc, A)



def local_layers(nc, W, C, X, tag):
    DEPTH, H, HD, WIN = 2, 8, 64, 64
    INNER = H * HD
    PAIRS = H // 2
    HID = int(DIM * 4 * 2 / 3)
    CUTS = [(0, 128), (128, 256), (256, HID)]
    KEYS = WIN + P
    QK_SCALE = 8.0
    ident = C["ident"]
    with ExitStack() as ctx:
        def sb(name, shape, dt=F32):
            return ctx.enter_context(nc.sbuf_tensor(f"{tag}_{name}", shape, dt))

        xl = sb("xl", [P, TILES, DIM])
        wqkv = sb("wqkv", [P, 3 * INNER])
        wo = sb("wo", [P, PAIRS, DIM])
        w1, w2 = sb("w1", [P, 2 * HID]), sb("w2", [P, 3, DIM])
        lg, lb = sb("lg", [P, 1]), sb("lb", [P, 1])
        b1 = sb("b1", [P, 2, 3])
        b2 = sb("b2", [P, DIM])
        qks = sb("qks", [P, 2, HD])
        rot_cos, rot_sin = sb("rot_cos", [P, TILES, 2, HD]), sb("rot_sin", [P, TILES, 2, HD])
        tab_cos, tab_sin = sb("tab_cos", [P, TILES, 2, HD]), sb("tab_sin", [P, TILES, 2, HD])
        bands = sb("bands", [P, 2, KEYS])
        band = sb("band", [P, KEYS])
        shift = sb("shift", [P, 2, P])
        ps = ctx.enter_context(nc.psum_tensor(tag + "_ps", [P, 8, 512], F32))

        L = signals(nc, ctx, "loaded xg_step")
        xg, xn = sb("xg", [P, GROUP, DIM]), sb("xn", [P, GROUP, DIM])
        B = group_buffers(sb)
        with nc.Block() as block:

            @block.sync
            def _(sp):
                sp.dma_start(rot_cos[:], W["rot_cos"]).then_inc(L["loaded"], 16)
                sp.dma_start(rot_sin[:], W["rot_sin"]).then_inc(L["loaded"], 16)
                sp.dma_start(bands[:], W["bands"]).then_inc(L["loaded"], 16)
                sp.dma_start(shift[:], W["shift"]).then_inc(L["loaded"], 16)
                sp.wait_ge(L["loaded"], 64)
        clear_signals(nc, L)
        with nc.Fori(0, TILES // GROUP) as t:
            with nc.Block() as block:

                @block.vector
                def _(dve):
                    link = counted(dve, L["xg_step"])
                    link(dve.tensor_copy(xg[:], X[:, bass.ds(t * GROUP, GROUP), :]))
                    link(normalize_group(dve, link, xg, xn, B))
                    dve.tensor_copy(xl[:, bass.ds(t * GROUP, GROUP), :], xn[:])
            clear_signals(nc, L)

        xt = sb("xt", [P, DIM])
        hT = sb("hT", [P, KEYS])
        xlast = sb("xlast", [P, 1])
        va, vb = sb("va", [P, INNER]), sb("vb", [WIN, INNER])
        qksq = sb("qksq", [P, 2 * H, HD])
        ss, rn, rtmp = sb("ss", [P, 2 * H]), sb("rn", [P, 2 * H]), sb("rtmp", [P, 2 * H])
        rc, rs = sb("rc", [P, 2, H, HD]), sb("rs", [P, 2, H, HD])
        qkr = sb("qkr", [P, 2 * H, HD])
        qT, kT = sb("qT", [P, PAIRS, P]), sb("kT", [P, PAIRS, KEYS])
        sm = sb("sm", [P, H, KEYS])
        nmx, den = sb("nmx", [P, H]), sb("den", [P, H])
        pTa, pTb = sb("pTa", [P, H, P]), sb("pTb", [WIN, H, P])
        o, oT = sb("o", [P, H, HD]), sb("oT", [P, PAIRS, P])
        x1 = sb("x1", [P, 3, DIM])
        h2, n2, nT = sb("h2", [P, DIM]), sb("n2", [P, DIM]), sb("nT", [P, P])
        stats, mv, rstd = sb("stats", [P, 6]), sb("mv", [P, 2]), sb("rstd", [P, 1])
        ge, hg = sb("ge", [P, 3, P]), sb("hg", [P, 3, P])
        x1b2 = sb("x1b2", [P, DIM])

        S = signals(nc, ctx, """w_loaded halos xt_ready xT_ps hT_ready qk_ps va_ps vb_ps qksq_ready v_ready qkr_ready
            qkT_ps qkT_ready scores_ps sm_ready probs_ready pT_ps pTa_ready pTb_ready o_ps o_ready oT_ps oT_ready
            y_ps x1_ready shift_ps n2_ready nT_ps nT_ready gate_ps lin_ps gelu_ready hg_ready ff_ps ffn_done
            dve_step pool_step""")

        def round_of(t, attend, feed):
            with nc.Block() as block:

                @block.tensor
                def _(pe):
                    if attend:
                        pe.wait_ge(S["xt_ready"], 1)
                        pe.transpose(ps[:, 5, 0:P], xt[:], ident).then_inc(S["xT_ps"], 1)
                    if feed:
                        pe.matmul(ps[:, 0, 0:64], shift[:, 0, :], x1[:, 1, 64:128], start=True, stop=False)
                        pe.matmul(ps[:, 0, 0:64], shift[:, 1, :], x1[:, 2, 64:128], start=False, stop=True)\
                            .then_inc(S["shift_ps"], 1)
                    if attend:
                        pe.wait_ge(S["hT_ready"], 1)
                        for b in range(2):
                            mm = pe.matmul(ps[:, 1 + b, :], hT[:, WIN:KEYS], wqkv[:, INNER * b:INNER * b + INNER],
                                           start=True, stop=True)
                        mm.then_inc(S["qk_ps"], 1)
                        pe.matmul(ps[:, 3, :], hT[:, 0:P], wqkv[:, 2 * INNER:3 * INNER], start=True, stop=True)\
                            .then_inc(S["va_ps"], 1)
                        pe.matmul(ps[0:WIN, 4, :], hT[:, P:KEYS], wqkv[:, 2 * INNER:3 * INNER], start=True, stop=True)\
                            .then_inc(S["vb_ps"], 1)
                    if feed:
                        pe.wait_ge(S["n2_ready"], 1)
                        pe.transpose(ps[:, 0, 128:256], n2[:], ident).then_inc(S["nT_ps"], 1)
                        pe.wait_ge(S["nT_ready"], 1)
                        for half, bank, sig in ((1, 7, "gate_ps"), (0, 0, "lin_ps")):
                            for c, (a, b) in enumerate(CUTS):
                                mm = pe.matmul(ps[0:b - a, bank, P * c:P * c + P],
                                               w1[:, HID * half + a:HID * half + b], nT[:], start=True, stop=True)
                            mm.then_inc(S[sig], 1)
                    if attend:
                        pe.wait_ge(S["qkr_ready"], 1)
                        for i in range(2 * PAIRS):
                            mm = pe.transpose(ps[:, 1 + i // 4, P * (i % 4):P * (i % 4) + P],
                                              qkr[:, 2 * i:2 * i + 2, :].rearrange("p h d -> p (h d)"), ident)
                        mm.then_inc(S["qkT_ps"], 1)
                        pe.wait_ge(S["qkT_ready"], 1)
                        pe.wait_ge(S["v_ready"], 2)
                        for i in range(PAIRS):
                            for s in range(2):
                                own = slice(64 * s, 64 * s + 64)
                                col = KEYS * (i % 2)
                                mm = pe.matmul(ps[:, 3 + 2 * s + i // 2, col:col + KEYS], qT[own, i, :],
                                               kT[own, i, :], start=True, stop=True)
                        mm.then_inc(S["scores_ps"], 1)
                    if feed:
                        pe.wait_ge(S["hg_ready"], 1)
                        for c, (a, b) in enumerate(CUTS):
                            mm = pe.matmul(ps[:, 7, 384:512], hg[0:b - a, c, :], w2[0:b - a, c, :],
                                           start=(c == 0), stop=(c == 2))
                        mm.then_inc(S["ff_ps"], 1)
                    if attend:
                        pe.wait_ge(S["sm_ready"], 1)
                        for h in range(H):
                            pe.wait_ge(S["probs_ready"], h + 1)
                            pe.transpose(ps[:, 1 + h // 4, P * (h % 4):P * (h % 4) + P], sm[:, h, 0:P], ident)
                            mm = pe.transpose(ps[0:WIN, 3 + h // 4, P * (h % 4):P * (h % 4) + P], sm[:, h, P:KEYS], ident)
                            if h % 4 == 3:
                                mm.then_inc(S["pT_ps"], 1)
                        pe.wait_ge(S["pTa_ready"], 1)
                        pe.wait_ge(S["pTb_ready"], 1)
                        for g in range(H):
                            head = 2 * (g % PAIRS) + g // PAIRS
                            out, own = ps[:, 5, HD * g:HD * g + HD], slice(HD * head, HD * head + HD)
                            pe.matmul(out, pTa[:, g, :], va[:, own], start=True, stop=False)
                            mm = pe.matmul(out, pTb[:, g, :], vb[:, own], start=False, stop=True)
                        mm.then_inc(S["o_ps"], 1)
                        pe.wait_ge(S["o_ready"], 1)
                        for i in range(PAIRS):
                            mm = pe.transpose(ps[:, 6, P * i:P * i + P],
                                              o[:, 2 * i:2 * i + 2, :].rearrange("p h d -> p (h d)"), ident)
                        mm.then_inc(S["oT_ps"], 1)
                        pe.wait_ge(S["oT_ready"], 1)
                        for i in range(PAIRS):
                            mm = pe.matmul(ps[:, 5, 0:DIM], oT[:, i, :], wo[:, i, :], start=(i == 0), stop=(i == PAIRS - 1))
                        mm.then_inc(S["y_ps"], 1)

                @block.gpsimd
                def _(pool):
                    link = counted(pool, S["pool_step"])
                    if attend:
                        link(pool.tensor_copy(hT[:, 0:WIN], hT[:, P:KEYS]))
                        link(pool.tensor_copy(hT[64:128, WIN:WIN + 1], xlast[64:128, :]))
                        pool.tensor_copy(kT[:, :, 0:WIN], kT[:, :, P:KEYS]).then_inc(S["halos"], 1)
                        pool.wait_ge(S["sm_ready"], 1)
                        pool.tensor_copy(band[:], bands[:, 1, :])
                        if feed:
                            pool.wait_ge(S["ffn_done"], 1)
                        pool.wait_ge(S["x1_ready"], 1)
                        link(pool.tensor_copy(x1[:, 2, :], x1[:, 1, :]))
                        pool.tensor_copy(x1[:, 1, :], x1[:, 0, :])

                @block.scalar
                def _(act):
                    if attend:
                        act.wait_ge(S["halos"], 1)
                        act.wait_ge(S["xT_ps"], 1)
                        act.activation(hT[0:64, WIN:KEYS], ps[0:64, 5, 0:P], ACT.Copy)
                        act.activation(xlast[64:128, :], ps[64:128, 5, P - 1:P], ACT.Copy)
                        act.activation(hT[64:128, WIN + 1:KEYS], ps[64:128, 5, 0:P - 1], ACT.Copy)\
                            .then_inc(S["hT_ready"], 1)
                        act.wait_ge(S["qk_ps"], 1)
                        act.activation(qksq[:].rearrange("p h d -> p (h d)"), ps[:, 1:3, :].rearrange("p b n -> p (b n)"),
                                       ACT.Square).then_inc(S["qksq_ready"], 1)
                        act.wait_ge(S["va_ps"], 1)
                        act.activation(va[:], ps[:, 3, :], ACT.Copy).then_inc(S["v_ready"], 1)
                        act.wait_ge(S["vb_ps"], 1)
                        act.activation(vb[:], ps[0:WIN, 4, :], ACT.Copy).then_inc(S["v_ready"], 1)
                    if feed:
                        act.wait_ge(S["nT_ps"], 1)
                        act.activation(nT[:], ps[:, 0, 128:256], ACT.Identity, scale=lg[:], bias=lb[:])\
                            .then_inc(S["nT_ready"], 1)
                        act.wait_ge(S["gate_ps"], 1)
                        for c, (a, b) in enumerate(CUTS):
                            ins = act.activation(ge[0:b - a, c, :], ps[0:b - a, 7, P * c:P * c + P], ACT.Gelu,
                                                 bias=b1[0:b - a, 1, c:c + 1])
                        ins.then_inc(S["gelu_ready"], 1)
                    if attend:
                        act.wait_ge(S["qkT_ps"], 1)
                        act.activation(qT[:].rearrange("p i n -> p (i n)"), ps[:, 1, :], ACT.Copy)
                        act.activation(kT[:, :, WIN:KEYS], heads(ps[:, 2, :], PAIRS), ACT.Copy)\
                            .then_inc(S["qkT_ready"], 1)
                        act.wait_ge(S["sm_ready"], 1)
                        for h in range(H):
                            act.activation(sm[:, h, :], sm[:, h, :], ACT.Exp, bias=nmx[:, h:h + 1],
                                           accum_out=den[:, h:h + 1]).then_inc(S["probs_ready"], 1)
                        act.wait_ge(S["pT_ps"], 2)
                        act.activation(pTa[:].rearrange("p h n -> p (h n)"), ps[:, 1:3, :].rearrange("p b n -> p (b n)"),
                                       ACT.Copy).then_inc(S["pTa_ready"], 1)
                        act.wait_ge(S["oT_ps"], 1)
                        act.activation(oT[:].rearrange("p i n -> p (i n)"), ps[:, 6, :], ACT.Copy)\
                            .then_inc(S["oT_ready"], 1)

                @block.vector
                def _(dve):
                    link = counted(dve, S["dve_step"])
                    if attend:
                        dve.tensor_copy(xt[:], tile_of(xl, t)).then_inc(S["xt_ready"], 1)
                    if feed:
                        dve.tensor_copy(h2[:, 0:64], x1[:, 1, 0:64])
                        dve.wait_ge(S["shift_ps"], 1)
                        link(dve.tensor_copy(h2[:, 64:128], ps[:, 0, 0:64]))
                        normalize_rows(dve, link, h2[:], n2[:], stats[:], mv[:], rstd[:]).then_inc(S["n2_ready"], 1)
                        dve.tensor_tensor(x1b2[:], x1[:, 1, :], b2[:], ALU.add)
                    if attend:
                        qk = ps[:, 1:3, :].rearrange("p a (h d) -> p a h d", h=H)
                        cos = tab_cos[:, bass.ds(t, 1), :, :].rearrange("p o a d -> p (o a) d")
                        sin = tab_sin[:, bass.ds(t, 1), :, :].rearrange("p o a d -> p (o a) d")

                        def each_head(tab, lo, hi):
                            return tab[:, :, lo:hi].unsqueeze(2).broadcast_to([P, 2, H, hi - lo])

                        dve.wait_ge(S["qksq_ready"], 1)
                        dve.tensor_tensor(rc[:], qk, each_head(cos, 0, 64), ALU.mult)
                        dve.tensor_tensor(rs[:, :, :, 0:32], qk[:, :, :, 32:64], each_head(sin, 0, 32), ALU.mult)
                        link(dve.tensor_tensor(rs[:, :, :, 32:64], qk[:, :, :, 0:32], each_head(sin, 32, 64), ALU.mult))
                        link(dve.tensor_reduce(ss[:], qksq[:], X_AXIS, ALU.add))
                        link(dve.tensor_scalar(ss[:], ss[:], 1e-24, None, ALU.max))
                        inv_sqrt(dve, link, ss[:], rn[:], rtmp[:])
                        link(dve.tensor_scalar(rn[:, 0:H], rn[:, 0:H], QK_SCALE, None, ALU.mult))
                        link(dve.tensor_tensor(rc[:].rearrange("p a h d -> p (a h d)"),
                                               rc[:].rearrange("p a h d -> p (a h d)"),
                                               rs[:].rearrange("p a h d -> p (a h d)"), ALU.add))
                        dve.tensor_tensor(qkr[:], rc[:].rearrange("p a h d -> p (a h) d"), over_inner(rn[:], HD),
                                          ALU.mult).then_inc(S["qkr_ready"], 1)
                    if feed:
                        dve.wait_ge(S["gelu_ready"], 1)
                        dve.wait_ge(S["lin_ps"], 1)
                        for c, (a, b) in enumerate(CUTS):
                            ins = dve.scalar_tensor_tensor(
                                out=hg[0:b - a, c, :], in0=ps[0:b - a, 0, P * c:P * c + P],
                                scalar=b1[0:b - a, 0, c:c + 1], in1=ge[0:b - a, c, :], op0=ALU.add, op1=ALU.mult)
                        ins.then_inc(S["hg_ready"], 1)
                    if attend:
                        dve.wait_ge(S["scores_ps"], 1)
                        scores = ps[:, 3:7, 0:2 * KEYS].rearrange("p b (s k) -> p b s k", s=2)
                        link(dve.tensor_tensor(sm[:].rearrange("p (b s) k -> p b s k", s=2), scores,
                                               band[:].unsqueeze(1).unsqueeze(1).broadcast_to([P, 4, 2, KEYS]), ALU.add))
                        link(dve.tensor_reduce(nmx[:], sm[:], X_AXIS, ALU.max))
                        dve.tensor_scalar(nmx[:], nmx[:], -1.0, None, ALU.mult).then_inc(S["sm_ready"], 1)
                    if feed:
                        dve.wait_ge(S["ff_ps"], 1)
                        dve.tensor_tensor(tile_of(xl, t - 1 if attend else TILES - 1), ps[:, 7, 384:512],
                                          x1b2[:], ALU.add).then_inc(S["ffn_done"], 1)
                    if attend:
                        dve.wait_ge(S["pT_ps"], 2)
                        dve.tensor_copy(pTb[:].rearrange("p h n -> p (h n)"),
                                        ps[0:WIN, 3:5, :].rearrange("p b n -> p (b n)")).then_inc(S["pTb_ready"], 1)
                        dve.wait_ge(S["probs_ready"], H)
                        link(dve.reciprocal(den[:], den[:]))
                        dve.wait_ge(S["o_ps"], 1)
                        dve.tensor_tensor(o[:].rearrange("p (i s) d -> p s i d", s=2),
                                          ps[:, 5, :].rearrange("p (s i d) -> p s i d", s=2, i=PAIRS),
                                          over_inner(den[:], HD).rearrange("p (s i) d -> p s i d", s=2), ALU.mult)\
                            .then_inc(S["o_ready"], 1)
                        dve.wait_ge(S["y_ps"], 1)
                        dve.tensor_tensor(x1[:, 0, :], ps[:, 5, 0:DIM], xt[:], ALU.add).then_inc(S["x1_ready"], 1)
            clear_signals(nc, S)

        with nc.Fori(0, DEPTH) as l:
            def of(name):
                a = W["L1_ffn_" + name][bass.ds(l, 1)]
                return a.rearrange("o a b -> (o a) b") if len(a.shape) == 3 else a.rearrange("o a -> (o a)")

            with nc.Block() as block:
                loads = [(wqkv[:], of("wqkv")), (wo[:], of("wo").rearrange("(c p) n -> p c n", p=P)),
                         (w1[:], of("w1")),
                         (w2[:, 0:2, :], of("w2")[0:256, :].rearrange("(c p) n -> p c n", p=P)),
                         (w2[0:HID - 256, 2, :], of("w2")[256:HID, :]),
                         (lg[:], of("ln_g").unsqueeze(1)), (lb[:], of("ln_b").unsqueeze(1)),
                         (b2[:], of("b2").partition_broadcast(P)),
                         (qks[:, 0, :], of("q_scale").partition_broadcast(P)),
                         (qks[:, 1, :], of("k_scale").partition_broadcast(P))]
                for half in range(2):
                    for c, (a, b) in enumerate(CUTS):
                        loads.append((b1[0:b - a, half, c:c + 1],
                                      of("b1")[HID * half + a:HID * half + b].unsqueeze(1)))

                @block.sync
                def _(sp):
                    for dst, src in loads:
                        sp.dma_start(dst, src).then_inc(S["w_loaded"], 16)

                @block.gpsimd
                def _(pool):
                    pool.memset(hT[:], 0.0)
                    pool.memset(kT[:], 0.0)
                    pool.memset(xlast[:], 0.0)
                    pool.memset(x1[:], 0.0)
                    pool.tensor_copy(band[:], bands[:, 0, :])

                @block.vector
                def _(dve):
                    dve.wait_ge(S["w_loaded"], 16 * len(loads))
                    for a in range(2):
                        dve.tensor_tensor(tab_cos[:, :, a, :], rot_cos[:, :, a, :],
                                          over_middle(qks[:, a, :], TILES), ALU.mult)
                        dve.tensor_tensor(tab_sin[:, :, a, 0:32], rot_sin[:, :, a, 0:32],
                                          over_middle(qks[:, a, 32:64], TILES), ALU.mult)
                        dve.tensor_tensor(tab_sin[:, :, a, 32:64], rot_sin[:, :, a, 32:64],
                                          over_middle(qks[:, a, 0:32], TILES), ALU.mult)
            clear_signals(nc, S)
            round_of(0, attend=True, feed=False)
            with nc.Fori(1, TILES) as t:
                round_of(t, attend=True, feed=True)
            round_of(TILES, attend=False, feed=True)

        with nc.Block() as block:

            @block.vector
            def _(dve):
                dve.tensor_tensor(X[:], X[:], xl[:], ALU.add)
        clear_signals(nc, L)



def grouped_attention(nc, W, C, X, tag):
    H, KV, HD = 16, 4, 64
    REP = H // KV
    HALF = TOKENS // 2
    BLK = 512
    HT = HALF // P
    SCALE = HD ** -0.5
    F32R = mybir.dt.float32r
    ident, ones = C["ident"], C["ones"]
    with ExitStack() as ctx:
        def sb(name, shape, dt=F32):
            return ctx.enter_context(nc.sbuf_tensor(f"{tag}_{name}", shape, dt))

        wq, wqr = sb("wq", [P, H, HD]), sb("wqr", [P, H, HD])
        wk, wkr = sb("wk", [P, KV, HD]), sb("wkr", [P, KV, HD])
        wv = sb("wv", [P, KV, HD])
        wo = sb("wo", [P, H, DIM])
        cos, sin = sb("cos", [HD, TOKENS]), sb("sin", [HD, TOKENS])
        bo = sb("bo", [P, DIM])
        xnT = sb("xnT", [P, TOKENS])
        khh, kll = sb("khh", [P, TOKENS], F32R), sb("kll", [P, TOKENS], F32R)
        v = sb("v", [P, TILES, HD])
        q2 = sb("q2", [P, 2, HALF], F32R)
        mrow = sb("mrow", [P, 2, HALF], F32R)
        first = sb("first", [P, P], F32R)
        xg, xn = sb("xg", [P, GROUP, DIM]), sb("xn", [P, GROUP, DIM])
        B = group_buffers(sb)
        wks, wqs = sb("wks", [P, 2, HD]), sb("wqs", [P, 2, HD])
        wos = sb("wos", [P, DIM])
        rope = sb("rope", [HD, 3, BLK])
        mpart, nm = sb("mpart", [P, HT, 4]), sb("nm", [P, HT])
        probs = sb("probs", [P, 3, HALF])
        acc = sb("acc", [P, 2, HALF])
        oT = sb("oT", [P, BLK])
        rden = sb("rden", [P, HT])
        ps = ctx.enter_context(nc.psum_tensor(tag + "_ps", [P, 8, 512], F32))

        S = signals(nc, ctx, """loaded xn_ready xnT_ps wks_ready k_ps k_done v_ps wqs_ready q_ps rope_done part_done split_done kpart_done
            max_ps max_done nm_ready row_ps row_ready wos_ready scores_ps probs_ready pv_ps oT_ready sum_step
            den_ps den_done y_ps y_done dve_step pool_step""")

        with nc.Block() as block:
            loads = [(wq[:], W["L1_attn_b_Wq"].rearrange("d (h e) -> d h e", h=H)),
                     (wk[:], W["L1_attn_b_Wkv"][:, 0:KV * HD].rearrange("d (h e) -> d h e", h=KV)),
                     (wv[:], W["L1_attn_b_Wkv"][:, KV * HD:2 * KV * HD].rearrange("d (h e) -> d h e", h=KV)),
                     (wo[0:HD], W["L1_attn_b_Wo"].rearrange("(h e) n -> e h n", h=H)),
                     (wo[HD:P], W["L1_attn_b_Wo"].rearrange("(h e) n -> e h n", h=H)),
                     (cos[:], W["rope_cos"]), (sin[:], W["rope_sin"]),
                     (bo[:], W["L1_attn_b_bo"].partition_broadcast(P))]

            @block.sync
            def _(sp):
                for dst, src in loads:
                    sp.dma_start(dst, src).then_inc(S["loaded"], 16)

            @block.gpsimd
            def _(pool):
                link = counted(pool, S["pool_step"])
                link(pool.memset(rope[:], 0.0))
                link(pool.memset(acc[:], 0.0))
                link(pool.memset(acc[0:1, 0, 0:P], 1.0))
                link(pool.tensor_copy(first[:], acc[:, 0, 0:P]))
                for half in range(2):
                    link(pool.tensor_copy(mrow[:, half, :], acc[:, 1, :]))

            @block.vector
            def _(dve):
                dve.wait_ge(S["loaded"], 16 * len(loads))
                for w, wr in ((wq, wqr), (wk, wkr)):
                    dve.tensor_scalar(wr[:, :, 0:32], w[:, :, 32:64], -1.0, None, ALU.mult)
                    dve.tensor_copy(wr[:, :, 32:64], w[:, :, 0:32])
        clear_signals(nc, S)

        with nc.Fori(0, TILES // GROUP) as t:
            with nc.Block() as block:

                @block.vector
                def _(dve):
                    link = counted(dve, S["dve_step"])
                    link(dve.tensor_copy(xg[:], X[:, bass.ds(t * GROUP, GROUP), :]))
                    normalize_group(dve, link, xg, xn, B).then_inc(S["xn_ready"], 1)
                    dve.tensor_tensor(X[:, bass.ds(t * GROUP, GROUP), :], xg[:], over_middle(bo[:], GROUP), ALU.add)

                @block.tensor
                def _(pe):
                    pe.wait_ge(S["xn_ready"], 1)
                    for i in range(GROUP):
                        mm = pe.transpose(ps[:, 0, P * i:P * i + P], xn[:, i, :], ident)
                    mm.then_inc(S["xnT_ps"], 1)

                @block.scalar
                def _(act):
                    act.wait_ge(S["xnT_ps"], 1)
                    act.activation(xnT[:, bass.ds(t * GROUP * P, GROUP * P)], ps[:, 0, :], ACT.Copy)
            clear_signals(nc, S)


        def proj(pe, n, half, b, weights):
            if b == 0:
                if weights:
                    pe.wait_ge(S["wqs_ready"], weights)
                if n:
                    pe.wait_ge(S["row_ready"], 2 * n)
            else:
                pe.wait_ge(S["rope_done"], 2 * n + 1)
            cols = slice(HALF * half + BLK * b, HALF * half + BLK * b + BLK)
            pe.matmul(ps[0:HD, 5, :], wqs[:, 0, :], xnT[:, cols], start=True, stop=True)
            pe.matmul(ps[0:HD, 6, :], wqs[:, 1, :], xnT[:, cols], start=True, stop=True).then_inc(S["q_ps"], 1)

        def rotate(dve, link, n, half, b):
            cols = slice(HALF * half + BLK * b, HALF * half + BLK * b + BLK)
            dve.wait_ge(S["q_ps"], 2 * n + b + 1)
            dve.scalar_tensor_tensor(out=rope[:, 0, :], in0=ps[0:HD, 5, :], scalar=SCALE, in1=cos[:, cols],
                                     op0=ALU.mult, op1=ALU.mult)
            link(dve.scalar_tensor_tensor(out=rope[:, 1, :], in0=ps[0:HD, 6, :], scalar=SCALE, in1=sin[:, cols],
                                          op0=ALU.mult, op1=ALU.mult))
            if b:
                dve.wait_ge(S["split_done"], 2 * n + 1)
            dve.tensor_tensor(rope[:, 2, :], rope[:, 0, :], rope[:, 1, :], ALU.add).then_inc(S["rope_done"], 1)

        def split_queries(pool, n, half, b):
            cols = slice(BLK * b, BLK * b + BLK)
            pool.wait_ge(S["rope_done"], 2 * n + b + 1)
            pool.tensor_copy(q2[0:HD, half, cols], rope[:, 2, :]).then_inc(S["part_done"], 1)
            pool.wait_ge(S["part_done"], 2 * n + b + 1)
            pool.tensor_tensor(q2[HD:P, half, cols], rope[:, 2, :], q2[0:HD, half, cols], ALU.subtract)\
                .then_inc(S["split_done"], 1)

        def rough_scores(pe, n, half, qt):
            if qt == 0:
                pe.wait_ge(S["split_done"], 2 * n + 2)
            for c in range(4):
                at = 4 * qt + c
                if at >= 2:
                    pe.wait_ge(S["max_done"], 32 * n + at - 1)
                pe.matmul(ps[:, 5 + c % 2, :], q2[:, half, P * qt:P * qt + P],
                          khh[:, BLK * c:BLK * c + BLK], start=True, stop=True)\
                    .then_inc(S["max_ps"], 1)

        def part_max(dve, n, qt):
            for c in range(4):
                dve.wait_ge(S["max_ps"], 32 * n + 4 * qt + c + 1)
                dve.tensor_reduce(mpart[:, qt, c:c + 1], ps[:, 5 + c % 2, :], X_AXIS, ALU.max)\
                    .then_inc(S["max_done"], 1)

        def negative_max(dve, link, n):
            dve.wait_ge(S["max_done"], 32 * n + 32)
            link(dve.tensor_reduce(nm[:], mpart[:], X_AXIS, ALU.max))
            dve.tensor_scalar(nm[:], nm[:], -1.0, None, ALU.mult).then_inc(S["nm_ready"], 1)

        def max_rows(pe, n):
            pe.wait_ge(S["nm_ready"], n + 1)
            for b in range(2):
                for i in range(4):
                    mm = pe.matmul(ps[0:1, 5 + b, P * i:P * i + P], nm[:, 4 * b + i:4 * b + i + 1], ident,
                                   start=True, stop=True)
                mm.then_inc(S["row_ps"], 1)

        def place_rows(act, n, half):
            for b in range(2):
                act.wait_ge(S["row_ps"], 2 * n + b + 1)
                act.activation(mrow[0:1, half, BLK * b:BLK * b + BLK], ps[0:1, 5 + b, :], ACT.Copy)\
                    .then_inc(S["row_ready"], 1)


        def out_sums(pe, p):
            pe.wait_ge(S["sum_step"], TILES * (p + 1))
            if p:
                pe.wait_ge(S["y_done"], 2)
            for i in range(HT):
                mm = pe.matmul(ps[:, 7, i:i + 1], acc[:, p, P * i:P * i + P], ones[:, 0:1], start=True, stop=True)
            mm.then_inc(S["den_ps"], 1)

        def out_block(pe, p, b):
            pe.wait_ge(S["den_done"], p + 1)
            if b:
                pe.wait_ge(S["y_done"], 2 * p + 1)
            else:
                pe.wait_ge(S["oT_ready"], p + 1)
                pe.wait_ge(S["wos_ready"], 1)
            for i in range(4):
                mm = pe.matmul(ps[:, 7, P * i:P * i + P], oT[HD * b:HD * b + HD, P * i:P * i + P],
                               wos[HD * b:HD * b + HD, :], start=True, stop=True)
            mm.then_inc(S["y_ps"], 1)

        def sums_inverse(dve, p):
            dve.wait_ge(S["den_ps"], p + 1)
            dve.reciprocal(rden[:], ps[:, 7, 0:HT]).then_inc(S["den_done"], 1)

        def add_block(dve, p, b):
            dve.wait_ge(S["den_done"], p + 1)
            dve.wait_ge(S["y_ps"], 2 * p + b + 1)
            for i in range(4):
                tile = HT * p + 4 * b + i
                ins = dve.scalar_tensor_tensor(out=X[:, tile, :], in0=ps[:, 7, P * i:P * i + P],
                                               scalar=rden[:, 4 * b + i:4 * b + i + 1], in1=X[:, tile, :],
                                               op0=ALU.mult, op1=ALU.add)
            ins.then_inc(S["y_done"], 1)


        def scores(pe, p, k):
            at = TILES * p + k
            if at >= 2:
                pe.wait_ge(S["probs_ready"], at - 1)
            for i, (keys, moving) in enumerate(((khh[:, P * k:P * k + P], q2), (kll[:, P * k:P * k + P], q2),
                                                (first[:], mrow))):
                for b in range(2):
                    mm = pe.matmul(ps[:, 2 * (k % 2) + b, :], keys, moving[:, p, BLK * b:BLK * b + BLK],
                                   start=(i == 0), stop=(i == 2))
            mm.then_inc(S["scores_ps"], 1)

        def context(pe, p, k):
            at = TILES * p + k
            pe.wait_ge(S["probs_ready"], at + 1)
            if p and k == 0:
                pe.wait_ge(S["oT_ready"], 1)
            for b in range(2):
                mm = pe.matmul(ps[HD * b:HD * b + HD, 4, :], v[:, k, :], probs[:, at % 3, BLK * b:BLK * b + BLK],
                               start=(k == 0), stop=(k == TILES - 1))
            mm.then_inc(S["pv_ps"], 1)

        def head(g, j, last):
            with nc.Block() as block:
                this_head = g * REP + j

                @block.gpsimd
                def _(pool):
                    link = counted(pool, S["pool_step"])
                    pool.tensor_copy(wos[:], tile_of(wo, this_head)).then_inc(S["wos_ready"], 1)
                    pool.wait_ge(S["wos_ready"], 1)
                    for b in range(2):
                        split_queries(pool, 0, 1, b)
                    if not last:
                        pool.wait_ge(S["split_done"], 2)
                        pool.wait_ge(S["q_ps"], 2)
                        link(pool.tensor_copy(wqs[:, 0, :], tile_of(wq, this_head + 1)))
                        pool.tensor_copy(wqs[:, 1, :], tile_of(wqr, this_head + 1)).then_inc(S["wqs_ready"], 1)
                        pool.wait_ge(S["wqs_ready"], 1)
                        pool.wait_ge(S["scores_ps"], TILES)
                        for b in range(2):
                            split_queries(pool, 1, 0, b)

                @block.tensor
                def _(pe):
                    for p in range(2):
                        prep = not (last and p == 1)
                        if p:
                            pe.wait_ge(S["row_ready"], 2)
                        scores(pe, p, 0)
                        scores(pe, p, 1)
                        for k in range(TILES):
                            context(pe, p, k)
                            if k + 2 < TILES:
                                scores(pe, p, k + 2)
                            if p and k == 1:
                                out_sums(pe, 0)
                            if p and k == 2:
                                out_block(pe, 0, 0)
                            if p and k == 3:
                                out_block(pe, 0, 1)
                            if prep and k in (2, 4):
                                proj(pe, p, 1 - p, (k - 2) // 2, weights=p)
                            if prep and 5 <= k < 5 + HT:
                                rough_scores(pe, p, 1 - p, k - 5)
                            if prep and k == 5 + HT:
                                max_rows(pe, p)
                    out_sums(pe, 1)
                    out_block(pe, 1, 0)
                    out_block(pe, 1, 1)

                @block.scalar
                def _(act):
                    for p in range(2):
                        prep = not (last and p == 1)
                        for k in range(TILES):
                            at = TILES * p + k
                            act.wait_ge(S["scores_ps"], at + 1)
                            if at >= 3:
                                act.wait_ge(S["pv_ps"], at - 2)
                                act.wait_ge(S["sum_step"], at - 2)
                            act.activation(probs[:, at % 3, :],
                                           ps[:, 2 * (k % 2):2 * (k % 2) + 2, :].rearrange("p b n -> p (b n)"),
                                           ACT.Exp).then_inc(S["probs_ready"], 1)
                            if prep and k == 7 + HT:
                                place_rows(act, p, 1 - p)
                        act.wait_ge(S["pv_ps"], TILES * (p + 1))
                        if p:
                            act.wait_ge(S["y_ps"], 2)
                        act.activation(oT[:], ps[:, 4, :], ACT.Copy).then_inc(S["oT_ready"], 1)

                @block.vector
                def _(dve):
                    link = counted(dve, S["dve_step"])
                    for p in range(2):
                        prep = not (last and p == 1)
                        for k in range(TILES):
                            at = TILES * p + k
                            dve.wait_ge(S["probs_ready"], at + 1)
                            if k == 0:
                                ins = dve.tensor_copy(acc[:, p, :], probs[:, at % 3, :])
                            else:
                                dve.wait_ge(S["sum_step"], at)
                                ins = dve.tensor_tensor(acc[:, p, :], acc[:, p, :], probs[:, at % 3, :], ALU.add)
                            ins.then_inc(S["sum_step"], 1)
                            if p and k == 1:
                                sums_inverse(dve, 0)
                            if p and k == 2:
                                add_block(dve, 0, 0)
                            if p and k == 3:
                                add_block(dve, 0, 1)
                            if prep and k in (2, 4):
                                rotate(dve, link, p, 1 - p, (k - 2) // 2)
                            if prep and 5 <= k < 5 + HT:
                                part_max(dve, p, k - 5)
                            if prep and k == 4 + HT:
                                negative_max(dve, link, p)
                    sums_inverse(dve, 1)
                    add_block(dve, 1, 0)
                    add_block(dve, 1, 1)
            clear_signals(nc, S)

        with nc.Fori(0, KV) as g:
            with nc.Block() as block:

                @block.gpsimd
                def _(pool):
                    link = counted(pool, S["pool_step"])
                    link(pool.tensor_copy(wks[:, 0, :], tile_of(wk, g)))
                    pool.tensor_copy(wks[:, 1, :], tile_of(wkr, g)).then_inc(S["wks_ready"], 1)
                    pool.wait_ge(S["wks_ready"], 1)
                    link(pool.tensor_copy(wqs[:, 0, :], tile_of(wq, g * REP)))
                    pool.tensor_copy(wqs[:, 1, :], tile_of(wqr, g * REP)).then_inc(S["wqs_ready"], 1)
                    pool.wait_ge(S["wqs_ready"], 1)
                    for b in range(2):
                        split_queries(pool, 0, 0, b)

                @block.tensor
                def _(pe):
                    pe.wait_ge(S["wks_ready"], 1)
                    for b in range(TOKENS // BLK):
                        if b >= 2:
                            pe.wait_ge(S["k_done"], b - 1)
                        for r in range(2):
                            mm = pe.matmul(ps[0:HD, 2 * (b % 2) + r, :], wks[:, r, :], xnT[:, BLK * b:BLK * b + BLK],
                                           start=True, stop=True)
                        mm.then_inc(S["k_ps"], 1)
                    for i in range(TILES):
                        mm = pe.matmul(ps[:, 4 + 3 * (i // 8), HD * (i % 8):HD * (i % 8) + HD], xnT[:, P * i:P * i + P],
                                       tile_of(wv, g), start=True, stop=True)
                    mm.then_inc(S["v_ps"], 1)
                    proj(pe, 0, 0, 0, weights=1)
                    proj(pe, 0, 0, 1, weights=1)
                    pe.wait_ge(S["k_done"], 4)
                    for qt in range(HT):
                        rough_scores(pe, 0, 0, qt)
                    max_rows(pe, 0)

                @block.scalar
                def _(act):
                    act.wait_ge(S["v_ps"], 1)
                    for i in range(2):
                        act.activation(v[:, 8 * i:8 * i + 8, :].rearrange("p t d -> p (t d)"), ps[:, 4 + 3 * i, :],
                                       ACT.Copy)
                    place_rows(act, 0, 0)

                @block.vector
                def _(dve):
                    link = counted(dve, S["dve_step"])
                    for b in range(TOKENS // BLK):
                        cols = slice(BLK * b, BLK * b + BLK)
                        dve.wait_ge(S["k_ps"], b + 1)
                        dve.tensor_tensor(rope[:, 0, :], ps[0:HD, 2 * (b % 2), :], cos[:, cols], ALU.mult)
                        link(dve.tensor_tensor(rope[:, 1, :], ps[0:HD, 2 * (b % 2) + 1, :], sin[:, cols], ALU.mult))
                        link(dve.tensor_tensor(rope[:, 2, :], rope[:, 0, :], rope[:, 1, :], ALU.add))
                        dve.tensor_copy(khh[HD:P, cols], rope[:, 2, :])
                        link(dve.tensor_copy(khh[0:HD, cols], rope[:, 2, :]))
                        dve.tensor_tensor(kll[HD:P, cols], rope[:, 2, :], khh[0:HD, cols], ALU.subtract)
                        dve.tensor_tensor(kll[0:HD, cols], rope[:, 2, :], khh[0:HD, cols], ALU.subtract)\
                            .then_inc(S["k_done"], 1)
                        dve.wait_ge(S["k_done"], b + 1)
                    rotate(dve, link, 0, 0, 0)
                    dve.wait_ge(S["rope_done"], 1)
                    rotate(dve, link, 0, 0, 1)
                    for qt in range(HT):
                        part_max(dve, 0, qt)
                    negative_max(dve, link, 0)
            clear_signals(nc, S)
            with nc.Fori(0, REP - 1) as j:
                head(g, j, last=False)
            head(g, REP - 1, last=True)



def load_all(nc, W, C_tile, X):
    with ExitStack() as ctx:
        S = signals(nc, ctx, "inputs_loaded")
        with nc.Block() as block:

            @block.sync
            def _(sp):
                sp.dma_start(X[:], W["L0_attn_a_hidden_states"].rearrange("b (t p) d -> p (b t) d", p=P))\
                    .then_inc(S["inputs_loaded"], 16)
                sp.dma_start(C_tile[:], W["f32_consts"]).then_inc(S["inputs_loaded"], 16)
                sp.wait_ge(S["inputs_loaded"], 32)
        clear_signals(nc, S)


def store_all(nc, out, X):
    with ExitStack() as ctx:
        S = signals(nc, ctx, "output_stored")
        with nc.Block() as block:

            @block.sync
            def _(sp):
                sp.dma_start(out.rearrange("b (t p) d -> p (b t) d", p=P), X[:]).then_inc(S["output_stored"], 16)
                sp.wait_ge(S["output_stored"], 16)


STAGES = {
    "delta": delta_block,
    "ternary": ternary_layer,
    "chunks": chunk_attention,
    "sparse": sparse_attention,
    "local": local_layers,
    "global": grouped_attention,
}


def build_program(nc, W, out, stages):
    with ExitStack() as ctx:
        X = ctx.enter_context(nc.sbuf_tensor("X", [P, TILES, DIM], F32))
        C_tile = ctx.enter_context(nc.sbuf_tensor("C_tile", [P, 4, P], F32))
        C = {name: C_tile[:, i, :] for i, name in enumerate(["ident", "upto", "after", "ones"])}
        load_all(nc, W, C_tile, X)
        for i, stage in enumerate(stages):
            STAGES[stage](nc, W, C, X, f"{stage}{i}")
        store_all(nc, out, X)


ORDER = ["delta", "ternary", "chunks", "ternary", "sparse", "local", "global", "local"]


def kernel(**inputs):
    import concourse.bacc as bacc
    from concourse.bass_utils import run_bass_kernel_spmd

    nc = bacc.Bacc("TRN2", target_bir_lowering=False, num_devices=1)
    arrays, W = {}, {}
    f32_consts, tri_masks = shape_constants()
    extra = {"f32_consts": f32_consts, "tri_masks": tri_masks, **table_constants()}
    for name, a in {**inputs, **extra}.items():
        a = np.ascontiguousarray(a)
        arrays[f"in_{name}"] = a
        W[name] = nc.dram_tensor(f"in_{name}", a.shape, mybir.dt.from_np(a.dtype), kind="ExternalInput").ap()
    out = nc.dram_tensor("out_x", (1, TOKENS, DIM), F32, kind="ExternalOutput").ap()
    build_program(nc, W, out, ORDER)
    r = run_bass_kernel_spmd(nc, [arrays], core_ids=[0])
    return r.results[0]["out_x"]
```

```python
from contextlib import ExitStack

import numpy as np
import concourse.bass as bass
from concourse import mybir

F32 = mybir.dt.float32

U32 = mybir.dt.uint32
I32 = mybir.dt.int32
ALU = mybir.AluOpType
ACT = mybir.ActivationFunctionType
X_AXIS = mybir.AxisListType.X

P = 128
TOKENS = 2048
TILES = TOKENS // P
DIM = 128
LN_EPS = 1e-5
SMALLEST = 1e-36



def signals(nc, ctx, names):
    return {name: ctx.enter_context(nc.semaphore(name)) for name in names.split()}


def signal_pair(nc, ctx, names):
    return [{name: ctx.enter_context(nc.semaphore(f"{name}_{parity}")) for name in names.split()}
            for parity in ("even", "odd")]


def zero_other_signals(block, other):
    @block.sync
    def _(sp):
        for sem in other.values():
            sp.sem_clear(sem)


def clear_signals(nc, S):
    engines = (nc.sync, nc.gpsimd, nc.scalar, nc.tensor, nc.vector)
    for i, sem in enumerate(S.values()):
        engines[i % len(engines)].sem_clear(sem)
    nc.all_engine_barrier()


def counted(eng, sem):
    count = [0]

    def link(ins):
        count[0] += 1
        ins.then_inc(sem, 1)
        eng.wait_ge(sem, count[0])

    return link


def over_inner(ap, n):
    return ap.unsqueeze(2).broadcast_to([ap.shape[0], ap.shape[1], n])


def over_middle(ap, n):
    return ap.unsqueeze(1).broadcast_to([ap.shape[0], n, ap.shape[1]])


def heads(ap, n):
    return ap.rearrange("p (h d) -> p h d", h=n)


def tile_of(ap3, t):
    return ap3[:, bass.ds(t, 1), :].rearrange("p a d -> p (a d)")


def inv_sqrt(dve, link, x, y, tmp, tmp2):
    link(dve.tensor_scalar(y.bitcast(U32), x.bitcast(U32), 1, None, ALU.logical_shift_right))
    link(dve.tensor_scalar(y.bitcast(I32), y.bitcast(I32), -1.0, float(0x5F3759DF), ALU.mult, ALU.add))
    link(dve.tensor_tensor(tmp, y, y, ALU.mult))
    link(dve.tensor_tensor(tmp, tmp, x, ALU.mult))
    link(dve.tensor_scalar(tmp2, tmp, 0.375, -1.25, ALU.mult, ALU.add))
    link(dve.tensor_tensor(tmp, tmp2, tmp, ALU.mult))
    link(dve.scalar_tensor_tensor(out=y, in0=tmp, scalar=1.875, in1=y, op0=ALU.add, op1=ALU.mult))
    link(dve.tensor_tensor(tmp, y, y, ALU.mult))
    link(dve.scalar_tensor_tensor(out=tmp, in0=tmp, scalar=-0.5, in1=x, op0=ALU.mult, op1=ALU.mult))
    link(dve.scalar_tensor_tensor(out=y, in0=tmp, scalar=1.5, in1=y, op0=ALU.add, op1=ALU.mult))


def normalize_rows(dve, link, x, out, stats, mv, rstd):
    link(dve.bn_stats(stats, x))
    link(dve.bn_aggr(mv, stats))
    link(dve.tensor_scalar(mv[:, 1:2], mv[:, 1:2], LN_EPS, None, ALU.add))
    inv_sqrt(dve, link, mv[:, 1:2], rstd, stats[:, 0:1], stats[:, 1:2])
    return dve.tensor_scalar(out, x, mv[:, 0:1], rstd, ALU.subtract, ALU.mult)



def shape_constants():
    j, t = np.arange(P)[:, None], np.arange(P)[None, :]
    f32 = {
        "ident": j == t,
        "upto": j <= t,
        "after": j > t,
        "ones": np.ones((P, P)),
    }
    levels = []
    for l in range(7):
        a, b = j >> l, t >> l
        levels.append((b % 2 == 1) & (a == b - 1))
    masks = np.stack(levels, 1)
    return (np.concatenate([v.astype(np.float32) for v in f32.values()], 1),
            np.ascontiguousarray(masks.astype(np.uint32)))



def delta_block(nc, W, C, X, tag):
    HK, HV, D, TAPS, NEXP, INTER = 4, 8, 128, 4, 8, 64
    REP = HV // HK
    QK, VAL = 2 * HK * D, HV * D
    CONV = QK + VAL
    EPS = 1e-6
    LEVELS = 7
    ident, upto, after, ones = C["ident"], C["upto"], C["after"], C["ones"]

    with ExitStack() as ctx:
        def sb(name, shape, dt=F32):
            return ctx.enter_context(nc.sbuf_tensor(f"{tag}_{name}", shape, dt))

        wconv = sb("wconv", [P, TAPS, CONV])
        wz = sb("wz", [P, VAL])
        wba = sb("wba", [P, 2 * HV])
        wout = sb("wout", [P, HV, DIM])
        wrouter = sb("wrouter", [P, NEXP])
        wgate = sb("wgate", [P, NEXP, INTER])
        wup = sb("wup", [P, NEXP, INTER])
        wdown = sb("wdown", [P, 4, DIM])
        ln1 = sb("ln1", [P, 1])
        ln2 = sb("ln2", [P, 1])
        dtb = sb("dtb", [P, HV])
        nega = sb("nega", [P, HV])
        gnw = sb("gnw", [P, D])
        tri = sb("tri", [P, LEVELS, P], U32)
        iota8 = sb("iota8", [P, NEXP])
        state = sb("state", [P, HV, D])
        x1T = sb("x1T", [P, TAPS - 1 + P])
        ps = ctx.enter_context(nc.psum_tensor(tag + "_ps", [P, 8, 512], F32))

        with ExitStack() as c2:
            cw = c2.enter_context(nc.sbuf_tensor(tag + "_cw", [P, CONV, TAPS], F32))
            wqkvz = c2.enter_context(nc.sbuf_tensor(tag + "_wqkvz", [P, CONV], F32))
            S = signals(nc, c2, "weights_loaded alog_exp dve_step pool_step")
            with nc.Block() as block:
                loads = [
                    (cw[:], W["L0_attn_a_conv_w"].partition_broadcast(P)),
                    (wqkvz[:], W["L0_attn_a_W_qkvz"][:, 0:CONV]),
                    (wz[:], W["L0_attn_a_W_qkvz"][:, CONV:CONV + VAL]),
                    (wba[:], W["L0_attn_a_W_ba"]),
                    (wout[:], W["L0_attn_a_W_out"].rearrange("(h d) n -> d h n", h=HV)),
                    (wrouter[:], W["L0_attn_a_W_router"]),
                    (wgate[:], W["L0_attn_a_W_gate_e"].rearrange("e h i -> h e i")),
                    (wup[:], W["L0_attn_a_W_up_e"].rearrange("e h i -> h e i")),
                    (wdown[:], W["L0_attn_a_W_down_e"].rearrange("(c e) i h -> (e i) c h", e=2)),
                    (ln1[:], W["L0_attn_a_w_ln1"].unsqueeze(1)),
                    (ln2[:], W["L0_attn_a_w_ln2"].unsqueeze(1)),
                    (dtb[:], W["L0_attn_a_dt_bias"].partition_broadcast(P)),
                    (nega[:], W["L0_attn_a_A_log"].partition_broadcast(P)),
                    (gnw[:], W["L0_attn_a_gate_norm_w"].partition_broadcast(P)),
                    (tri[:], W["tri_masks"]),
                ]

                @block.sync
                def _(sp):
                    for dst, src in loads:
                        sp.dma_start(dst, src).then_inc(S["weights_loaded"], 16)

                @block.gpsimd
                def _(pool):
                    pool.memset(x1T[:], 0.0)
                    pool.memset(state[:], 0.0)
                    pool.iota(iota8[:], [[1, NEXP]], base=0, channel_multiplier=0,
                              allow_small_or_imprecise_dtypes=True)

                @block.scalar
                def _(act):
                    act.wait_ge(S["weights_loaded"], 16 * len(loads))
                    act.activation(nega[:], nega[:], ACT.Exp).then_inc(S["alog_exp"], 1)

                @block.vector
                def _(dve):
                    dve.wait_ge(S["weights_loaded"], 16 * len(loads))
                    for j in range(TAPS):
                        dve.tensor_tensor(wconv[:, j, :], wqkvz[:], cw[:, :, j], ALU.mult)
                    dve.tensor_scalar(ln1[:], ln1[:], 1.0, None, ALU.add)
                    dve.tensor_scalar(ln2[:], ln2[:], 1.0, None, ALU.add)
                    dve.wait_ge(S["alog_exp"], 1)
                    dve.tensor_scalar(nega[:], nega[:], -1.0, None, ALU.mult)
            clear_signals(nc, S)

        stats, mv, rstd = sb("stats", [P, 6]), sb("mv", [P, 2]), sb("rstd", [P, 1])
        h0 = sb("h0", [P, 2, DIM])
        sq = sb("sq", [P, HV, D])
        ms = sb("ms", [P, 1])
        x1 = sb("x1", [P, DIM])
        ya, ny, eb, ea, la, nbeta, g = (sb(n, [P, HV]) for n in "ya ny eb ea la nbeta g".split())
        beta = sb("beta", [P, 2, HV])
        eg = sb("eg", [P, 2, 3, HV])
        qk = sb("qk", [P, 2 * HK, D])
        val, zs = sb("val", [P, 2, HV, D]), sb("zs", [P, 2, HV, D])
        qkss, rn, rtmp = sb("qkss", [P, 2 * HK]), sb("rn", [P, 8]), sb("rtmp", [P, 2, 8])
        qn, kn = sb("qn", [P, HK, D]), sb("kn", [P, 2, HK, D])
        qkT = sb("qkT", [P, 2, 2 * HK, P])
        gm = sb("gm", [P, HV, P])
        et, etm = sb("et", [P, HV, P]), sb("etm", [P, HV, P])
        etb = gm
        probsT = sb("probsT", [P, 2, HV, P])
        NT, T, NTp = sb("NT", [P, HV, P]), sb("T", [P, HV, P]), sb("NTp", [P, HV, P])
        Y = sb("Y", [P, 2, HV, P])
        R, U, UD, qs = (sb(n, [P, HV, D]) for n in "R U UD qs".split())
        core, coreT = sb("core", [P, HV, D]), sb("coreT", [P, HV, P])
        oss = sb("oss", [P, HV])
        h1, x2, x2T = sb("h1", [P, DIM]), sb("x2", [P, DIM]), sb("x2T", [P, P])
        rl, el, esum = sb("rl", [P, NEXP]), sb("el", [P, NEXP]), sb("esum", [P, 1])
        lmax, nmax = sb("lmax", [P, 8]), sb("nmax", [P, 1])
        eidx, eidf = sb("eidx", [P, 8], U32), sb("eidf", [P, 8])
        pick = sb("pick", [P, 3, NEXP])
        route = sb("route", [P, NEXP])
        sg, hid = sb("sg", [P, NEXP, INTER]), sb("hid", [P, NEXP, INTER])
        hidT = sb("hidT", [P, 4, P])

        def banks(a, n=1):
            return ps[:, a:a + n, :].rearrange("p b n -> p (b n)")

        def bank_heads(a, n):
            return heads(banks(a, n), 4 * n)

        def half(s):
            return slice(4 * s, 4 * s + 4)

        def flat(a):
            return a.rearrange("p h d -> p (h d)")

        SIGNALS = signal_pair(nc, ctx, """x1_ready x1T_ps halo x1T_ready ba_ps qk_ps v_ps z_ps v_silu z_silu qk_silu
            gate_in gate_exp gate_ln g_ready gm_ready gsum_ps decay_ps decay_exp eg_ready qkn_ready qkT_ps qkT_ready
            gram_ps et_masked probs_ready Y_ready T_ps T_ready NTp_ps NTp_ready delta_ps
            kS_ps R_ready W_ps U_ready qS_ps qs_ready intra_ps core_summed state_ps state_ready core_ready
            coreT_ps coreT_ready out_ps x2_ready x2T_ps x2T_ready router_ps logits_read gateup_ps nmax_ready
            el_ready sg_ready hid_ready hidT_ps hidT_ready down_ps dve_step pool_step""")

        def round_of(t, new, solve, recur):
            old = 1 - new
            S = SIGNALS[new]
            with nc.Block() as block:
                zero_other_signals(block, SIGNALS[old])

                @block.tensor
                def _(pe):
                    def conv(bank, column):
                        for j in range(TAPS):
                            mm = pe.matmul(banks(bank), x1T[:, j:j + P], wconv[:, j, column:column + 512],
                                           start=(j == 0), stop=(j == TAPS - 1))
                        return mm

                    def turn_Y(s):
                        for h in range(4 * s, 4 * s + 4):
                            mm = pe.transpose(bank_heads(0, 2)[:, h, :], Y[:, new, h, :], ident)
                        mm.then_inc(S["T_ps"], 1)

                    def double_blocks(l):
                        for s in range(2):
                            pe.wait_ge(S["T_ready"], 2 * (l - 1) + s + 1)
                            for h in range(4 * s, 4 * s + 4):
                                mm = pe.matmul(bank_heads(0, 2)[:, h, :], NT[:, h, :], T[:, h, :],
                                               start=True, stop=True)
                            mm.then_inc(S["NTp_ps"], 1)
                        for s in range(2):
                            pe.wait_ge(S["NTp_ready"], 2 * (l - 1) + s + 1)
                            if l == 1 and s == 0:
                                pe.wait_ge(S["probs_ready"], 1)
                            for h in range(4 * s, 4 * s + 4):
                                mm = pe.matmul(bank_heads(2, 2)[:, h, :], NTp[:, h, :], Y[:, new, h, :],
                                               start=True, stop=True)
                            mm.then_inc(S["delta_ps"], 1)

                    def turn_level(l):
                        for s in range(2):
                            pe.wait_ge(S["Y_ready"], 2 * l + s + 1)
                            turn_Y(s)

                    if recur:
                        for first, bank, sig in ((HK, 4, "kS_ps"), (0, 6, "qS_ps")):
                            for h in range(HK):
                                pair = slice(REP * h, REP * h + REP)
                                mm = pe.matmul(bank_heads(bank, 2)[:, pair, :], qkT[:, old, first + h, :],
                                               state[:, pair, :], start=True, stop=True)
                            mm.then_inc(S[sig], 1)
                    if solve:
                        pe.wait_ge(S["x1_ready"], 1)
                        pe.transpose(banks(0)[:, 0:P], x1[:], ident).then_inc(S["x1T_ps"], 1)
                        pe.wait_ge(S["x1T_ready"], 1)
                        pe.matmul(banks(3)[:, 0:2 * HV], x1T[:, 3:3 + P], wba[:], start=True, stop=True)\
                            .then_inc(S["ba_ps"], 1)
                        conv(0, 0)
                        conv(1, 512).then_inc(S["qk_ps"], 1)
                    if recur:
                        pe.wait_ge(S["R_ready"], 1)
                        for h in range(HV):
                            mm = pe.matmul(bank_heads(4, 2)[:, h, :], Y[:, old, h, :], R[:, h, :], start=True, stop=True)
                        mm.then_inc(S["W_ps"], 1)
                    if solve:
                        conv(2, 1024)
                    if recur:
                        pe.wait_ge(S["U_ready"], 1)
                        pe.wait_ge(S["qs_ready"], 1)
                        for h in range(HV):
                            mm = pe.matmul(bank_heads(6, 2)[:, h, :], probsT[:, old, h, :], U[:, h, :],
                                           start=True, stop=True)
                        mm.then_inc(S["intra_ps"], 1)
                        for h in range(HK):
                            pair = slice(REP * h, REP * h + REP)
                            mm = pe.matmul(bank_heads(4, 2)[:, pair, :], kn[:, old, h, :], UD[:, pair, :],
                                           start=True, stop=True)
                        mm.then_inc(S["state_ps"], 1)
                    if solve:
                        pe.wait_ge(S["gate_in"], 1)
                        pe.wait_ge(S["gate_exp"], 1)
                        conv(3, 1536).then_inc(S["v_ps"], 1)
                        pe.wait_ge(S["qk_silu"], 1)
                        for b in range(2):
                            mm = pe.matmul(banks(b), x1T[:, 3:3 + P], wz[:, b * 512:b * 512 + 512],
                                           start=True, stop=True)
                        mm.then_inc(S["z_ps"], 1)
                        pe.wait_ge(S["qkn_ready"], 1)
                        pe.wait_ge(S["v_silu"], 1)
                        for h in range(HK):
                            pe.transpose(bank_heads(2, 2)[:, h, :], qn[:, h, :], ident)
                            mm = pe.transpose(bank_heads(2, 2)[:, HK + h, :], kn[:, new, h, :], ident)
                        mm.then_inc(S["qkT_ps"], 1)
                        pe.wait_ge(S["gm_ready"], 1)
                        pe.wait_ge(S["z_silu"], 1)
                        for h in range(HV):
                            mm = pe.matmul(bank_heads(0, 2)[:, h, :], gm[:, h, :], upto, start=True, stop=True)
                        mm.then_inc(S["decay_ps"], 1)
                        pe.wait_ge(S["qkT_ready"], 1)
                        for h in range(HK):
                            kT = qkT[:, new, HK + h, :]
                            pe.matmul(bank_heads(2, 1)[:, h, :], kT, kT, start=True, stop=True)
                            mm = pe.matmul(bank_heads(3, 1)[:, h, :], kT, qkT[:, new, h, :], start=True, stop=True)
                        mm.then_inc(S["gram_ps"], 1)
                        pe.wait_ge(S["decay_exp"], 1)
                        pe.matmul(banks(0)[:, 0:8], upto, g[:], start=True, stop=True)
                        pe.matmul(banks(0)[:, 8:16], after, g[:], start=True, stop=True)
                        pe.matmul(banks(0)[:, 16:24], ones, g[:], start=True, stop=True).then_inc(S["gsum_ps"], 1)
                    if recur:
                        pe.wait_ge(S["core_ready"], 1)
                        for h in range(HV):
                            mm = pe.transpose(bank_heads(6, 2)[:, h, :], core[:, h, :], ident)
                        mm.then_inc(S["coreT_ps"], 1)
                        pe.wait_ge(S["coreT_ready"], 1)
                        pe.wait_ge(S["state_ready"], 1)
                        for h in range(HV):
                            mm = pe.matmul(banks(4)[:, 0:DIM], coreT[:, h, :], wout[:, h, :],
                                           start=(h == 0), stop=(h == HV - 1))
                        mm.then_inc(S["out_ps"], 1)
                    if solve:
                        pe.wait_ge(S["eg_ready"], 1)
                        turn_level(0)
                        double_blocks(1)
                        turn_level(1)
                    if recur:
                        pe.wait_ge(S["x2_ready"], 1)
                        pe.transpose(banks(5)[:, 0:P], x2[:], ident).then_inc(S["x2T_ps"], 1)
                    if solve:
                        double_blocks(2)
                        turn_level(2)
                    if recur:
                        pe.wait_ge(S["x2T_ready"], 1)
                        pe.matmul(banks(5)[:, 0:NEXP], x2T[:], wrouter[:], start=True, stop=True)\
                            .then_inc(S["router_ps"], 1)
                        pe.matmul(banks(6), x2T[:], wgate[:].rearrange("p e i -> p (e i)"), start=True, stop=True)
                        pe.matmul(banks(7), x2T[:], wup[:].rearrange("p e i -> p (e i)"), start=True, stop=True)\
                            .then_inc(S["gateup_ps"], 1)
                    if solve:
                        double_blocks(3)
                        turn_level(3)
                        double_blocks(4)
                        turn_level(4)
                    if recur:
                        pe.wait_ge(S["hid_ready"], 1)
                        for c in range(4):
                            mm = pe.transpose(bank_heads(4, 1)[:, c, :],
                                              hid[:, 2 * c:2 * c + 2, :].rearrange("p e i -> p (e i)"), ident)
                        mm.then_inc(S["hidT_ps"], 1)
                    if solve:
                        double_blocks(5)
                        turn_level(5)
                    if recur:
                        pe.wait_ge(S["hidT_ready"], 1)
                        pe.wait_ge(S["logits_read"], 1)
                        for c in range(4):
                            mm = pe.matmul(banks(5)[:, 0:DIM], hidT[:, c, :], wdown[:, c, :], start=(c == 0), stop=(c == 3))
                        mm.then_inc(S["down_ps"], 1)
                    if solve:
                        double_blocks(6)

                @block.scalar
                def _(act):
                    def copy_T(s):
                        act.wait_ge(S["T_ps"], copy_T.done + 1)
                        copy_T.done += 1
                        act.activation(flat(T[:, half(s), :]), banks(s), ACT.Copy).then_inc(S["T_ready"], 1)

                    copy_T.done = 0

                    def copy_NTp(l, s):
                        act.wait_ge(S["NTp_ps"], 2 * (l - 1) + s + 1)
                        act.activation(flat(NTp[:, half(s), :]), banks(s), ACT.Copy).then_inc(S["NTp_ready"], 1)

                    if solve:
                        act.activation(x1T[:, 0:3], x1T[:, P:P + 3], ACT.Copy).then_inc(S["halo"], 1)
                        act.wait_ge(S["halo"], 1)
                        act.wait_ge(S["x1T_ps"], 1)
                        act.activation(x1T[:, 3:3 + P], banks(0)[:, 0:P], ACT.Copy, scale=ln1[:])\
                            .then_inc(S["x1T_ready"], 1)
                        act.wait_ge(S["gate_in"], 1)
                        act.activation(ea[:], ny[:], ACT.Exp)
                        act.activation(eb[:], banks(3)[:, 0:HV], ACT.Exp, scale=-1.0).then_inc(S["gate_exp"], 1)
                        act.wait_ge(S["gate_exp"], 1)
                        act.activation(la[:], ea[:], ACT.Ln, bias=1.0).then_inc(S["gate_ln"], 1)
                        act.wait_ge(S["qk_ps"], 1)
                        act.activation(flat(qk[:]), banks(0, 2), ACT.Silu).then_inc(S["qk_silu"], 1)
                        act.wait_ge(S["v_ps"], 1)
                        act.activation(flat(val[:, new]), banks(2, 2), ACT.Silu).then_inc(S["v_silu"], 1)
                        act.wait_ge(S["z_ps"], 1)
                        act.activation(flat(zs[:, new]), banks(0, 2), ACT.Silu).then_inc(S["z_silu"], 1)
                        act.wait_ge(S["qkT_ps"], 1)
                        act.activation(flat(qkT[:, new]), banks(2, 2), ACT.Copy).then_inc(S["qkT_ready"], 1)
                        act.wait_ge(S["decay_ps"], 1)
                        act.activation(flat(et[:]), banks(0, 2), ACT.Exp).then_inc(S["decay_exp"], 1)
                        act.wait_ge(S["gsum_ps"], 1)
                        act.activation(eg[:, new].rearrange("p a h -> p (a h)"), banks(0)[:, 0:24], ACT.Exp)\
                            .then_inc(S["eg_ready"], 1)
                    if recur:
                        act.wait_ge(S["coreT_ps"], 1)
                        act.activation(flat(coreT[:]), banks(6, 2), ACT.Copy).then_inc(S["coreT_ready"], 1)
                    if solve:
                        copy_T(0)
                        copy_T(1)
                        copy_NTp(1, 0)
                        copy_NTp(1, 1)
                        copy_T(0)
                        copy_T(1)
                    if recur:
                        act.wait_ge(S["x2T_ps"], 1)
                        act.activation(x2T[:], banks(5)[:, 0:P], ACT.Copy, scale=ln2[:]).then_inc(S["x2T_ready"], 1)
                    if solve:
                        copy_NTp(2, 0)
                        copy_NTp(2, 1)
                        copy_T(0)
                        copy_T(1)
                        copy_NTp(3, 0)
                        copy_NTp(3, 1)
                    if recur:
                        act.wait_ge(S["nmax_ready"], 1)
                        act.activation(el[:], rl[:], ACT.Exp, bias=nmax[:], accum_out=esum[:]).then_inc(S["el_ready"], 1)
                    if solve:
                        copy_T(0)
                        copy_T(1)
                        copy_NTp(4, 0)
                        copy_NTp(4, 1)
                    if recur:
                        act.wait_ge(S["gateup_ps"], 1)
                        act.activation(flat(sg[:]), banks(6), ACT.Silu).then_inc(S["sg_ready"], 1)
                    if solve:
                        copy_T(0)
                        copy_T(1)
                    if recur:
                        act.wait_ge(S["hidT_ps"], 1)
                        act.activation(flat(hidT[:]), banks(4), ACT.Copy).then_inc(S["hidT_ready"], 1)
                    if solve:
                        copy_NTp(5, 0)
                        copy_NTp(5, 1)
                        copy_T(0)
                        copy_T(1)
                        copy_NTp(6, 0)
                        copy_NTp(6, 1)

                @block.gpsimd
                def _(pool):
                    if recur:
                        pool.wait_ge(S["qS_ps"], 1)
                        pool.tensor_tensor(state[:], state[:], over_inner(eg[:, old, 2, :], D), ALU.mult)\
                            .then_inc(S["pool_step"], 1)
                    if solve:
                        pool.wait_ge(S["g_ready"], 1)
                        pool.tensor_tensor(gm[:], over_middle(after, HV), over_inner(g[:], P), ALU.mult)\
                            .then_inc(S["gm_ready"], 1)
                        pool.wait_ge(S["decay_exp"], 1)
                        pool.tensor_tensor(etm[:], et[:], over_middle(upto, HV), ALU.mult).then_inc(S["et_masked"], 1)
                        pool.wait_ge(S["z_silu"], 1)
                        pool.tensor_tensor(zs[:, new], zs[:, new], over_middle(gnw[:], HV), ALU.mult)

                @block.vector
                def _(dve):
                    link = counted(dve, S["dve_step"])

                    def root_mean_square(x, out):
                        link(dve.tensor_tensor_reduce(sq[:, 0, :], x, x, 1.0, 0.0, ALU.mult, ALU.add, ms[:]))
                        link(dve.tensor_scalar(ms[:], ms[:], 1.0 / DIM, EPS, ALU.mult, ALU.add))
                        inv_sqrt(dve, link, ms[:], rstd[:], stats[:, 0:1], stats[:, 1:2])
                        return dve.tensor_scalar(out, x, rstd[:], None, ALU.mult)

                    def update_Y(l):
                        for s in range(2):
                            dve.wait_ge(S["delta_ps"], 2 * (l - 1) + s + 1)
                            dve.copy_predicated(Y[:, new, half(s), :], over_middle(tri[:, l, :], 4),
                                                bank_heads(2 + s, 1)).then_inc(S["Y_ready"], 1)

                    if solve:
                        link(normalize_rows(dve, link, tile_of(X, t), h0[:, new, :], stats[:], mv[:], rstd[:]))
                        root_mean_square(h0[:, new, :], x1[:]).then_inc(S["x1_ready"], 1)
                    if recur:
                        dve.wait_ge(S["kS_ps"], 1)
                        link(dve.tensor_tensor(R[:], bank_heads(4, 2), over_inner(eg[:, old, 0, :], D), ALU.mult))
                        dve.tensor_tensor(R[:], val[:, old], R[:], ALU.subtract).then_inc(S["R_ready"], 1)
                    if solve:
                        dve.wait_ge(S["ba_ps"], 1)
                        link(dve.tensor_tensor(ya[:], banks(3)[:, HV:2 * HV], dtb[:], ALU.add))
                        dve.scalar_tensor_tensor(out=ny[:], in0=ya[:], scalar=-1.0, in1=ya[:],
                                                 op0=ALU.mult, op1=ALU.min).then_inc(S["gate_in"], 1)
                    if recur:
                        dve.wait_ge(S["qS_ps"], 1)
                        dve.tensor_tensor(qs[:], bank_heads(6, 2), over_inner(eg[:, old, 0, :], D), ALU.mult)\
                            .then_inc(S["qs_ready"], 1)
                    if solve:
                        dve.wait_ge(S["gate_ln"], 1)
                        link(dve.scalar_tensor_tensor(out=la[:], in0=ya[:], scalar=0.0, in1=la[:],
                                                      op0=ALU.max, op1=ALU.add))
                        dve.tensor_tensor(g[:], la[:], nega[:], ALU.mult).then_inc(S["g_ready"], 1)
                        link(dve.tensor_scalar(eb[:], eb[:], 1.0, None, ALU.add))
                        link(dve.reciprocal(beta[:, new, :], eb[:]))
                        link(dve.tensor_scalar(nbeta[:], beta[:, new, :], -1.0, None, ALU.mult))
                    if recur:
                        dve.wait_ge(S["W_ps"], 1)
                        link(dve.tensor_tensor(U[:], bank_heads(4, 2), over_inner(beta[:, old, :], D), ALU.mult))
                        dve.tensor_tensor(UD[:], U[:], over_inner(eg[:, old, 1, :], D), ALU.mult)\
                            .then_inc(S["U_ready"], 1)
                    if solve:
                        dve.wait_ge(S["qk_silu"], 1)
                        link(dve.tensor_tensor(sq[:], qk[:], qk[:], ALU.mult))
                        link(dve.tensor_reduce(qkss[:], sq[:], X_AXIS, ALU.add))
                        link(dve.tensor_scalar(qkss[:], qkss[:], EPS, None, ALU.add))
                        inv_sqrt(dve, link, qkss[:], rn[:], rtmp[:, 0, :], rtmp[:, 1, :])
                        link(dve.tensor_scalar(rn[:, 0:HK], rn[:, 0:HK], D ** -0.5, None, ALU.mult))
                        dve.tensor_tensor(qn[:], qk[:, 0:HK, :], over_inner(rn[:, 0:HK], D), ALU.mult)
                        dve.tensor_tensor(kn[:, new], qk[:, HK:2 * HK, :], over_inner(rn[:, HK:2 * HK], D), ALU.mult)\
                            .then_inc(S["qkn_ready"], 1)
                    if recur:
                        dve.wait_ge(S["intra_ps"], 1)
                        link(dve.tensor_tensor(core[:], bank_heads(6, 2), qs[:], ALU.add))
                        link(dve.tensor_tensor(sq[:], core[:], core[:], ALU.mult))
                        link(dve.tensor_reduce(oss[:], sq[:], X_AXIS, ALU.add))
                        link(dve.tensor_scalar(oss[:], oss[:], 1.0 / D, EPS, ALU.mult, ALU.add))
                        if solve:
                            dve.wait_ge(S["qkn_ready"], 1)
                        inv_sqrt(dve, link, oss[:], rn[:], rtmp[:, 0, :], rtmp[:, 1, :])
                        link(dve.tensor_tensor(core[:], core[:], over_inner(rn[:], D), ALU.mult))
                        dve.tensor_tensor(core[:], core[:], zs[:, old], ALU.mult).then_inc(S["core_ready"], 1)
                        dve.wait_ge(S["state_ps"], 1)
                        dve.wait_ge(S["pool_step"], 1)
                        dve.tensor_tensor(state[:], bank_heads(4, 2), state[:], ALU.add)\
                            .then_inc(S["state_ready"], 1)
                    if solve:
                        dve.wait_ge(S["decay_exp"], 1)
                        link(dve.tensor_tensor(etb[:], et[:], over_inner(nbeta[:], P), ALU.mult))
                        dve.wait_ge(S["gram_ps"], 1)
                        for r in range(REP):
                            link(dve.tensor_tensor(NT[:, r::REP, :], bank_heads(2, 1), etb[:, r::REP, :], ALU.mult))
                        for s in range(2):
                            link(dve.tensor_copy(Y[:, new, half(s), :], over_middle(ident, 4)))
                            dve.copy_predicated(Y[:, new, half(s), :], over_middle(tri[:, 0, :], 4),
                                                NT[:, half(s), :]).then_inc(S["Y_ready"], 1)
                        dve.wait_ge(S["et_masked"], 1)
                        for r in range(REP):
                            ins = dve.tensor_tensor(probsT[:, new, r::REP, :], bank_heads(3, 1), etm[:, r::REP, :],
                                                    ALU.mult)
                        ins.then_inc(S["probs_ready"], 1)
                    if recur:
                        dve.wait_ge(S["out_ps"], 1)
                        link(dve.tensor_tensor(h1[:], banks(4)[:, 0:DIM], h0[:, old, :], ALU.add))
                        root_mean_square(h1[:], x2[:]).then_inc(S["x2_ready"], 1)
                    if solve:
                        update_Y(1)
                        update_Y(2)
                    if recur:
                        dve.wait_ge(S["router_ps"], 1)
                        dve.tensor_copy(rl[:], banks(5)[:, 0:NEXP]).then_inc(S["logits_read"], 1)
                        dve.wait_ge(S["logits_read"], 1)
                        link(dve.max(lmax[:], rl[:]))
                        dve.tensor_scalar(nmax[:], lmax[:, 0:1], -1.0, None, ALU.mult).then_inc(S["nmax_ready"], 1)
                    if solve:
                        update_Y(3)
                    if recur:
                        link(dve.max_index(eidx[:], lmax[:], rl[:]))
                        link(dve.tensor_copy(eidf[:], eidx[:]))
                        dve.tensor_scalar(pick[:, 0, :], iota8[:], eidf[:, 0:1], None, ALU.is_equal)
                        link(dve.tensor_scalar(pick[:, 1, :], iota8[:], eidf[:, 1:2], None, ALU.is_equal))
                        link(dve.tensor_tensor(pick[:, 0, :], pick[:, 0, :], pick[:, 1, :], ALU.add))
                        dve.wait_ge(S["el_ready"], 1)
                        link(dve.tensor_tensor_reduce(pick[:, 2, :], el[:], pick[:, 0, :], 1.0, 0.0,
                                                      ALU.mult, ALU.add, ms[:]))
                        link(dve.reciprocal(ms[:], ms[:]))
                        link(dve.tensor_scalar(route[:], pick[:, 2, :], ms[:], None, ALU.mult))
                    if solve:
                        update_Y(4)
                    if recur:
                        dve.wait_ge(S["sg_ready"], 1)
                        link(dve.tensor_tensor(hid[:], heads(banks(7), NEXP), sg[:], ALU.mult))
                        dve.tensor_tensor(hid[:], hid[:], over_inner(route[:], INTER), ALU.mult)\
                            .then_inc(S["hid_ready"], 1)
                    if solve:
                        update_Y(5)
                    if recur:
                        dve.wait_ge(S["down_ps"], 1)
                        link(dve.tensor_tensor(h1[:], banks(5)[:, 0:DIM], h1[:], ALU.add))
                        dve.tensor_tensor(tile_of(X, t - 1), h1[:], tile_of(X, t - 1), ALU.add)
                    if solve:
                        update_Y(6)

        round_of(0, 0, solve=True, recur=False)
        with nc.Fori(1, TILES // 2) as i:
            for odd in range(2):
                round_of(i * 2 - 1 + odd, 1 - odd, solve=True, recur=True)
        round_of(TILES - 1, 1, solve=True, recur=True)
        round_of(TILES, 0, solve=False, recur=True)
        for S in SIGNALS:
            clear_signals(nc, S)



GROUP = 4


def norm_buffers(sb, n):
    return {"stats": sb("gstats", [P, n, 6]), "mv": sb("gmv", [P, n, 2]),
            "var": sb("gvar", [P, n]), "rstd": sb("grstd", [P, n]), "tmp": sb("gtmp", [P, 2, n])}


def normalize_tiles(dve, link, x, out, B, n, ready, group):
    for i in range(n):
        ins = dve.bn_stats(B["stats"][:, i, :], x[:, i, :])
    link(ins)
    for i in range(n):
        ins = dve.bn_aggr(B["mv"][:, i, :], B["stats"][:, i, :])
    link(ins)
    link(dve.tensor_scalar(B["var"][:], B["mv"][:, :, 1], LN_EPS, None, ALU.add))
    inv_sqrt(dve, link, B["var"][:], B["rstd"][:], B["tmp"][:, 0, :], B["tmp"][:, 1, :])
    for i in range(n):
        ins = dve.tensor_scalar(out[:, i, :], x[:, i, :], B["mv"][:, i, 0:1], B["rstd"][:, i:i + 1],
                                ALU.subtract, ALU.mult)
        if i % group == group - 1:
            ins.then_inc(ready, 1)



def ternary_layer(nc, W, C, X, tag):
    ident, ones = C["ident"], C["ones"]
    with ExitStack() as ctx:
        def sb(name, shape, dt=F32):
            return ctx.enter_context(nc.sbuf_tensor(f"{tag}_{name}", shape, dt))

        w, wabs, wpos, wneg = (sb(n, [P, DIM]) for n in ("w", "wabs", "wpos", "wneg"))
        wT = sb("wT", [P, DIM])
        rowsum, delta, ndelta, alpha = (sb(n, [P, 1]) for n in ("rowsum", "delta", "ndelta", "alpha"))
        bias = sb("bias", [P, DIM])
        xn, xnT = sb("xn", [P, TILES, DIM]), sb("xnT", [P, TILES, P])
        B = norm_buffers(sb, TILES)
        ps = ctx.enter_context(nc.psum_tensor(tag + "_ps", [P, 8, GROUP, 128], F32))

        S = signals(nc, ctx, "loaded rowsum_ready total_ps w_ready wT_ps xn_ready xnT_ps xnT_ready y_ps dve_step")
        with nc.Block() as block:

            @block.sync
            def _(sp):
                sp.dma_start(w[:], W["L0_ffn_weight"]).then_inc(S["loaded"], 16)
                sp.dma_start(alpha[:], W["L0_ffn_alpha"].partition_broadcast(P)).then_inc(S["loaded"], 16)
                sp.dma_start(bias[:], W["L0_ffn_bias"].partition_broadcast(P)).then_inc(S["loaded"], 16)

            @block.vector
            def _(dve):
                link = counted(dve, S["dve_step"])
                dve.wait_ge(S["loaded"], 48)
                link(dve.scalar_tensor_tensor(out=wabs[:], in0=w[:], scalar=-1.0, in1=w[:], op0=ALU.mult, op1=ALU.max))
                dve.tensor_reduce(rowsum[:], wabs[:], X_AXIS, ALU.add).then_inc(S["rowsum_ready"], 1)
                dve.wait_ge(S["total_ps"], 1)
                link(dve.tensor_scalar(delta[:], ps[:, 0, 0, 0:1], 1.0 / (DIM * DIM), 0.7, ALU.mult, ALU.mult))
                link(dve.tensor_scalar(ndelta[:], delta[:], -1.0, None, ALU.mult))
                link(dve.tensor_scalar(wpos[:], w[:], delta[:], None, ALU.is_gt))
                link(dve.tensor_scalar(wneg[:], w[:], ndelta[:], None, ALU.is_lt))
                link(dve.tensor_tensor(wpos[:], wpos[:], wneg[:], ALU.subtract))
                dve.tensor_scalar(wpos[:], wpos[:], alpha[:], None, ALU.mult).then_inc(S["w_ready"], 1)
                dve.wait_ge(S["wT_ps"], 1)
                dve.tensor_copy(wT[:], ps[:, 1, 0, :])

            @block.tensor
            def _(pe):
                pe.wait_ge(S["rowsum_ready"], 1)
                pe.matmul(ps[:, 0, 0, 0:1], ones, rowsum[:], start=True, stop=True).then_inc(S["total_ps"], 1)
                pe.wait_ge(S["w_ready"], 1)
                pe.transpose(ps[:, 1, 0, :], wpos[:], ident).then_inc(S["wT_ps"], 1)
        clear_signals(nc, S)

        with nc.Block() as block:

            @block.tensor
            def _(pe):
                for g in range(TILES // GROUP):
                    pe.wait_ge(S["xn_ready"], g + 1)
                    for i in range(GROUP):
                        mm = pe.transpose(ps[:, g, i, :], xn[:, g * GROUP + i, :], ident)
                    mm.then_inc(S["xnT_ps"], 1)
                for g in range(TILES // GROUP):
                    pe.wait_ge(S["xnT_ready"], g + 1)
                    for i in range(GROUP):
                        mm = pe.matmul(ps[:, 4 + g, i, :], xnT[:, g * GROUP + i, :], wT[:], start=True, stop=True)
                    mm.then_inc(S["y_ps"], 1)

            @block.scalar
            def _(act):
                for g in range(TILES // GROUP):
                    act.wait_ge(S["xnT_ps"], g + 1)
                    act.activation(xnT[:, g * GROUP:g * GROUP + GROUP, :], ps[:, g], ACT.Copy)\
                        .then_inc(S["xnT_ready"], 1)

            @block.vector
            def _(dve):
                link = counted(dve, S["dve_step"])
                normalize_tiles(dve, link, X, xn, B, TILES, S["xn_ready"], GROUP)
                dve.wait_ge(S["xn_ready"], TILES // GROUP)
                link(dve.tensor_tensor(X[:], X[:], over_middle(bias[:], TILES), ALU.add))
                for g in range(TILES // GROUP):
                    dve.wait_ge(S["y_ps"], g + 1)
                    group = X[:, g * GROUP:g * GROUP + GROUP, :]
                    dve.tensor_tensor(group, ps[:, 4 + g], group, ALU.add)
        clear_signals(nc, S)



def chunk_attention(nc, W, C, X, tag):
    H, HD, CH = 16, 8, 32
    QUADS = P // CH
    NCH = TOKENS // CH
    SCALE = float(1.0 / np.sqrt(np.float32(HD)))
    ident = C["ident"]
    with ExitStack() as ctx:
        def sb(name, shape, dt=F32):
            return ctx.enter_context(nc.sbuf_tensor(f"{tag}_{name}", shape, dt))

        wl = sb("wl", [P, 4, DIM])
        wg = sb("wg", [P, 4, DIM])
        hm = sb("hm", [P, H])
        mean4 = sb("mean4", [P, QUADS])
        spread = sb("spread", [NCH, TOKENS])
        sumT = sb("sumT", [P, NCH])
        ps = ctx.enter_context(nc.psum_tensor(tag + "_ps", [P, 8, 512], F32))

        xl, xlT = sb("xl", [P, 2, DIM]), sb("xlT", [P, P])
        stats, mv, rstd = sb("stats", [P, 6]), sb("mv", [P, 2]), sb("rstd", [P, 1])
        qT, v = sb("qT", [P, P]), sb("v", [P, 2, DIM])
        kexp = sb("kexp", [P, H, P])
        mx, den = sb("mx", [P, H]), sb("den", [P, H])
        e, eT = sb("e", [P, H, CH]), sb("eT", [P, 2, H, CH])
        ctxm = sb("ctxm", [P, QUADS, H, CH])
        ctxT = sb("ctxT", [P, P])
        chunk = sb("chunk", [P, DIM])
        L = signals(nc, ctx, "loaded")
        SIGNALS = signal_pair(nc, ctx, """xl_ready xlT_ps xlT_ready qkv_ps qTv_ready kexp_ready scores_ps shifted_ready
            exp_ready ctx_ps ctxT_ready y_ps chunk_ready sum_ps dve_step""")
        with nc.Block() as block:

            @block.sync
            def _(sp):
                for i, n in enumerate(("Wq", "Wk", "Wv", "Wo")):
                    sp.dma_start(wl[:, i, :], W[f"L0_attn_b_{n}_l"]).then_inc(L["loaded"], 16)
                    sp.dma_start(wg[:, i, :], W[f"L0_attn_b_{n}_g"]).then_inc(L["loaded"], 16)
                sp.dma_start(hm[:], W["head8_mask"]).then_inc(L["loaded"], 16)
                sp.dma_start(mean4[:], W["mean4"]).then_inc(L["loaded"], 16)
                sp.dma_start(spread[:], W["spread"]).then_inc(L["loaded"], 16)
                sp.wait_ge(L["loaded"], 11 * 16)
        clear_signals(nc, L)

        def round_of(t, new, score, mix):
            old = 1 - new
            S = SIGNALS[new]
            with nc.Block() as block:
                zero_other_signals(block, SIGNALS[old])

                @block.tensor
                def _(pe):
                    def context(quads):
                        for j in quads:
                            own = slice(CH * j, CH * j + CH)
                            mm = pe.matmul(ps[:, 2 + j, :], v[own, old, :], eT[own, old].rearrange("p h q -> p (h q)"),
                                           start=True, stop=True)
                        mm.then_inc(S["ctx_ps"], 1)

                    if mix:
                        context(range(0, 2))
                    if score:
                        pe.wait_ge(S["xl_ready"], 1)
                        pe.transpose(ps[:, 0, 0:P], xl[:, new, :], ident).then_inc(S["xlT_ps"], 1)
                        pe.wait_ge(S["xlT_ready"], 1)
                        pe.matmul(ps[:, 0, 128:256], wl[:, 0, :], xlT[:], start=True, stop=True)
                        pe.matmul(ps[:, 7, 128:256], wl[:, 1, :], xlT[:], start=True, stop=True)
                        pe.matmul(ps[:, 0, 384:512], xlT[:], wl[:, 2, :], start=True, stop=True)\
                            .then_inc(S["qkv_ps"], 1)
                    if mix:
                        context(range(2, QUADS))
                    if score:
                        pe.wait_ge(S["qTv_ready"], 1)
                        pe.wait_ge(S["kexp_ready"], 1)
                        for j in range(QUADS):
                            own = slice(CH * j, CH * j + CH)
                            mm = pe.matmul(ps[own, 1, :], qT[:, own], kexp[:, :, own], start=True, stop=True)
                        mm.then_inc(S["scores_ps"], 1)
                    if mix:
                        pe.wait_ge(S["ctxT_ready"], 1)
                        pe.matmul(ps[:, 6, 0:DIM], ctxT[:], wl[:, 3, :], start=True, stop=True).then_inc(S["y_ps"], 1)
                        pe.wait_ge(S["chunk_ready"], 1)
                        pe.matmul(ps[:, 6, 256:256 + QUADS], chunk[:], mean4[:], start=True, stop=True)\
                            .then_inc(S["sum_ps"], 1)

                @block.scalar
                def _(act):
                    if score:
                        act.wait_ge(S["xlT_ps"], 1)
                        act.activation(xlT[:], ps[:, 0, 0:P], ACT.Copy).then_inc(S["xlT_ready"], 1)
                        act.wait_ge(S["qkv_ps"], 1)
                        act.activation(qT[:], ps[:, 0, 128:256], ACT.Copy, scale=SCALE)
                        act.activation(v[:, new, :], ps[:, 0, 384:512], ACT.Copy).then_inc(S["qTv_ready"], 1)
                        act.wait_ge(S["shifted_ready"], 1)
                        act.activation(e[:], e[:], ACT.Exp).then_inc(S["exp_ready"], 1)

                @block.vector
                def _(dve):
                    link = counted(dve, S["dve_step"])
                    if score:
                        normalize_rows(dve, link, tile_of(X, t), xl[:, new, :], stats[:], mv[:], rstd[:])\
                            .then_inc(S["xl_ready"], 1)
                        dve.wait_ge(S["qkv_ps"], 1)
                        dve.tensor_tensor(kexp[:], over_middle(ps[:, 7, 128:256], H), over_inner(hm[:], P), ALU.mult)\
                            .then_inc(S["kexp_ready"], 1)
                    if mix:
                        dve.wait_ge(S["ctx_ps"], 2)
                        own_head = hm[:].unsqueeze(1).unsqueeze(3).broadcast_to([P, QUADS, H, CH])
                        link(dve.tensor_tensor(ctxm[:], ps[:, 2:6, :].rearrange("p j (h q) -> p j h q", h=H),
                                               own_head, ALU.mult))
                        dve.tensor_reduce(ctxT[:].rearrange("p (j q) -> p j q", j=QUADS),
                                          ctxm[:].rearrange("p j h q -> p j q h"), X_AXIS, ALU.add)\
                            .then_inc(S["ctxT_ready"], 1)
                    if score:
                        dve.wait_ge(S["scores_ps"], 1)
                        scores = heads(ps[:, 1, :], H)
                        link(dve.tensor_reduce(mx[:], scores, X_AXIS, ALU.max))
                        dve.tensor_tensor(e[:], scores, over_inner(mx[:], CH), ALU.subtract)\
                            .then_inc(S["shifted_ready"], 1)
                    if mix:
                        dve.wait_ge(S["y_ps"], 1)
                        dve.tensor_tensor(chunk[:], ps[:, 6, 0:DIM], xl[:, old, :], ALU.add).then_inc(S["chunk_ready"], 1)
                        dve.wait_ge(S["chunk_ready"], 1)
                        dve.tensor_tensor(tile_of(X, t - 1), chunk[:], tile_of(X, t - 1), ALU.add)
                    if score:
                        dve.wait_ge(S["exp_ready"], 1)
                        link(dve.tensor_reduce(den[:], e[:], X_AXIS, ALU.add))
                        link(dve.reciprocal(den[:], den[:]))
                        link(dve.tensor_tensor(e[:], e[:], over_inner(den[:], CH), ALU.mult))
                        dve.transpose(eT[:, new].rearrange("p h q -> p (h q)"), e[:].rearrange("p h k -> p (h k)"))
                    if mix:
                        dve.wait_ge(S["sum_ps"], 1)
                        dve.tensor_copy(sumT[:, bass.ds((t - 1) * QUADS, QUADS)], ps[:, 6, 256:256 + QUADS])

        round_of(0, 0, score=True, mix=False)
        with nc.Fori(1, TILES // 2) as i:
            for odd in range(2):
                round_of(i * 2 - 1 + odd, 1 - odd, score=True, mix=True)
        round_of(TILES - 1, 1, score=True, mix=True)
        round_of(TILES, 0, score=False, mix=True)
        for S in SIGNALS:
            clear_signals(nc, S)

        summ, gqT, gv = sb("summ", [NCH, DIM]), sb("gqT", [P, NCH]), sb("gv", [NCH, DIM])
        gk = sb("gk", [P, H, NCH])
        ge, geT = sb("ge", [NCH, H, NCH]), sb("geT", [NCH, H, NCH])
        gm = sb("gm", [P, H, NCH])
        gctxT = sb("gctxT", [P, NCH])
        gout = sb("gout", [NCH, DIM])
        S2 = signals(nc, ctx, """proj_ps g_evac gk_ready gscores_ps gshifted gexp gnorm geT_ps geT_ready gctx_ps
            gctxT_ready gout_ps gout_ready spread_ps g_step""")
        with nc.Block() as block:

            @block.tensor
            def _(pe):
                pe.transpose(ps[0:NCH, 0, 0:P], sumT[:], ident)
                pe.matmul(ps[:, 0, 128:192], wg[:, 0, :], sumT[:], start=True, stop=True)
                pe.matmul(ps[:, 7, 128:192], wg[:, 1, :], sumT[:], start=True, stop=True)
                pe.matmul(ps[0:NCH, 0, 256:384], sumT[:], wg[:, 2, :], start=True, stop=True).then_inc(S2["proj_ps"], 1)
                pe.wait_ge(S2["g_evac"], 1)
                pe.wait_ge(S2["gk_ready"], 1)
                gkf = gk[:].rearrange("p h k -> p (h k)")
                for b in range(2):
                    mm = pe.matmul(ps[0:NCH, 1 + b, :], gqT[:], gkf[:, 512 * b:512 * b + 512], start=True, stop=True)
                mm.then_inc(S2["gscores_ps"], 1)
                pe.wait_ge(S2["gnorm"], 1)
                for h in range(H):
                    mm = pe.transpose(ps[0:NCH, 3 + h // 8, NCH * (h % 8):NCH * (h % 8) + NCH], ge[:, h, :],
                                      ident[0:NCH, 0:NCH])
                mm.then_inc(S2["geT_ps"], 1)
                pe.wait_ge(S2["geT_ready"], 1)
                geTf = geT[:].rearrange("p h q -> p (h q)")
                for b in range(2):
                    mm = pe.matmul(ps[:, 5 + b, :], gv[:], geTf[:, 512 * b:512 * b + 512], start=True, stop=True)
                mm.then_inc(S2["gctx_ps"], 1)
                pe.wait_ge(S2["gctxT_ready"], 1)
                pe.matmul(ps[0:NCH, 7, 0:DIM], gctxT[:], wg[:, 3, :], start=True, stop=True).then_inc(S2["gout_ps"], 1)
                pe.wait_ge(S2["gout_ready"], 1)
                for i in range(TILES):
                    mm = pe.matmul(ps[:, i // 4, 128 * (i % 4):128 * (i % 4) + DIM], spread[:, P * i:P * i + P],
                                   gout[:], start=True, stop=True)
                mm.then_inc(S2["spread_ps"], 1)

            @block.scalar
            def _(act):
                act.wait_ge(S2["proj_ps"], 1)
                act.activation(summ[:], ps[0:NCH, 0, 0:P], ACT.Copy)
                act.activation(gqT[:], ps[:, 0, 128:192], ACT.Copy, scale=SCALE)
                act.activation(gv[:], ps[0:NCH, 0, 256:384], ACT.Copy).then_inc(S2["g_evac"], 1)
                act.wait_ge(S2["gshifted"], 1)
                act.activation(ge[:], ge[:], ACT.Exp).then_inc(S2["gexp"], 1)
                act.wait_ge(S2["geT_ps"], 1)
                act.activation(geT[:].rearrange("p h q -> p (h q)"), ps[0:NCH, 3:5, :].rearrange("p b n -> p (b n)"),
                               ACT.Copy).then_inc(S2["geT_ready"], 1)

            @block.vector
            def _(dve):
                link = counted(dve, S2["g_step"])
                dve.wait_ge(S2["proj_ps"], 1)
                dve.tensor_tensor(gk[:], over_middle(ps[:, 7, 128:192], H), over_inner(hm[:], NCH), ALU.mult)\
                    .then_inc(S2["gk_ready"], 1)
                dve.wait_ge(S2["gscores_ps"], 1)
                scores = heads(ps[0:NCH, 1:3, :].rearrange("p b n -> p (b n)"), H)
                link(dve.tensor_reduce(mx[0:NCH], scores, X_AXIS, ALU.max))
                dve.tensor_tensor(ge[:], scores, over_inner(mx[0:NCH], NCH), ALU.subtract).then_inc(S2["gshifted"], 1)
                dve.wait_ge(S2["gexp"], 1)
                link(dve.tensor_reduce(den[0:NCH], ge[:], X_AXIS, ALU.add))
                link(dve.reciprocal(den[0:NCH], den[0:NCH]))
                dve.tensor_tensor(ge[:], ge[:], over_inner(den[0:NCH], NCH), ALU.mult).then_inc(S2["gnorm"], 1)
                dve.wait_ge(S2["gctx_ps"], 1)
                link(dve.tensor_tensor(gm[:], heads(ps[:, 5:7, :].rearrange("p b n -> p (b n)"), H),
                                       over_inner(hm[:], NCH), ALU.mult))
                dve.tensor_reduce(gctxT[:], gm[:].rearrange("p h q -> p q h"), X_AXIS, ALU.add)\
                    .then_inc(S2["gctxT_ready"], 1)
                dve.wait_ge(S2["gout_ps"], 1)
                dve.wait_ge(S2["g_evac"], 1)
                dve.tensor_tensor(gout[:], ps[0:NCH, 7, 0:DIM], summ[:], ALU.add).then_inc(S2["gout_ready"], 1)
                dve.wait_ge(S2["spread_ps"], 1)
                dve.tensor_tensor(X[:].rearrange("p t d -> p (t d)"), ps[:, 0:4, :].rearrange("p b n -> p (b n)"),
                                  X[:].rearrange("p t d -> p (t d)"), ALU.add)
        clear_signals(nc, S2)



def rotary_tables():
    half = np.arange(0, 64, 2, dtype=np.float32)
    inv_freq = (np.float32(1.0) / np.power(np.float32(10000.0), half / np.float32(64))).astype(np.float32)
    t = np.arange(TOKENS, dtype=np.float32)
    freqs = np.tile(t[:, None] * inv_freq[None, :], (1, 2)).astype(np.float32)
    base = ((half + np.float32(0.4 * 64)) / np.float32(1.4 * 64)).astype(np.float32)
    power = ((t - TOKENS // 2) / np.float32(32.0)).astype(np.float32)
    scale = np.tile(np.power(base[None, :], power[:, None]), (1, 2)).astype(np.float32)
    cos, sin = np.cos(freqs).astype(np.float32), np.sin(freqs).astype(np.float32)
    sin = np.concatenate([-sin[:, :32], sin[:, 32:]], 1)
    both = [np.stack([a * scale, a / scale], 1) for a in (cos, sin)]
    return [np.ascontiguousarray(a.reshape(TILES, P, 2, 64).transpose(1, 0, 2, 3).astype(np.float32)) for a in both]


def rope_tables():
    d = np.arange(0, 64, 2, dtype=np.float32) / np.float32(64)
    inv_freq = (np.float32(1.0) / np.power(np.float32(10000.0), d)).astype(np.float32)
    freqs = (np.arange(TOKENS, dtype=np.float32)[:, None] * inv_freq[None, :]).astype(np.float32)
    freqs = np.concatenate([freqs, freqs], 1).T
    return np.cos(freqs).astype(np.float32).copy(), np.sin(freqs).astype(np.float32).copy()


def band_masks():
    q, c = np.arange(P)[:, None], np.arange(P + 64)[None, :]
    near = (c - q >= 0) & (c - q <= 64)
    return np.stack([np.where(m, 0, -1e30) for m in (near & (c >= 64), near)], 1).astype(np.float32)


def shift_matrices():
    s = np.zeros((P, 2, P), np.float32)
    s[np.arange(P - 1), 0, np.arange(1, P)] = 1
    s[P - 1, 1, 0] = 1
    return s


def table_constants():
    rot_cos, rot_sin = rotary_tables()
    f = np.arange(P)
    c = np.arange(TOKENS // 32)
    rope_cos, rope_sin = rope_tables()
    return {
        "rope_cos": rope_cos,
        "rope_sin": rope_sin,
        "rot_cos": rot_cos,
        "rot_sin": rot_sin,
        "bands": band_masks(),
        "shift": shift_matrices(),
        "token_ids": (f[:, None] + P * np.arange(TILES)[None, :]).astype(np.float32),
        "rank_ids": (np.arange(80)[:, None] % 10).astype(np.float32),
        "head8_mask": (f[:, None] // 8 == np.arange(16)[None, :]).astype(np.float32),
        "mean4": np.where(f[:, None] // 32 == np.arange(4)[None, :], 1 / 32, 0).astype(np.float32),
        "spread": (c[:, None] == np.arange(TOKENS)[None, :] // 32).astype(np.float32),
    }



def sparse_attention(nc, W, C, X, tag):
    H, HD, TOP, LEAST = 16, 8, 10, 3
    HALF = H // 2 * TOP
    SCALE = float(1.0 / np.sqrt(np.float32(HD)))
    ROUND = float(3 << 22)
    LOWEST = -3.0e38
    GT = GROUP * P
    ident, ones = C["ident"], C["ones"]
    with ExitStack() as ctx:
        def sb(name, shape, dt=F32):
            return ctx.enter_context(nc.sbuf_tensor(f"{tag}_{name}", shape, dt))

        w = sb("w", [P, 4, DIM])
        wT = sb("wT", [P, 4, DIM])
        bq, bv, bo = sb("bq", [P, DIM]), sb("bv", [P, DIM]), sb("bo", [P, DIM])
        bk = sb("bk", [P, 1])
        hm, tokid = sb("hm", [P, H]), sb("tokid", [P, TILES])
        q_all, v_all = sb("q_all", [P, TILES, DIM]), sb("v_all", [P, TILES, DIM])
        kT_all = sb("kT_all", [P, TOKENS])
        qs = sb("qs", [H, TOKENS])
        tokrow = sb("tokrow", [HALF, TOKENS])
        ps = ctx.enter_context(nc.psum_tensor(tag + "_ps", [P, 8, 512], F32))

        xg, xn, xnT = sb("xg", [P, GROUP, DIM]), sb("xn", [P, GROUP, DIM]), sb("xnT", [P, GT])
        B = norm_buffers(sb, GROUP)
        qg = sb("qg", [P, GROUP, DIM])
        NH = GROUP * H
        e8, t8, lp = sb("e8", [P, NH, HD]), sb("t8", [P, NH, HD]), sb("lp", [P, NH, HD])
        m8, s8, l2, r8, r8b, ent, var8 = (sb(n, [P, NH]) for n in "m8 s8 l2 r8 r8b ent var8".split())
        score = sb("score", [P, GROUP, H])
        tiny = sb("tiny", [P, 1])

        S = signals(nc, ctx, """loaded wT_ps wT_ready xn_ready xnT_ps xnT_ready qv_ps kT_ps kT_done shifted8 exp8
            prob_ready log_ready score_ready scoreT_ps dve_step pool_step""")
        with nc.Block() as block:

            @block.sync
            def _(sp):
                for i, n in enumerate("qkvo"):
                    sp.dma_start(w[:, i, :], W["L1_attn_a_W" + n]).then_inc(S["loaded"], 16)
                for dst, n in ((bq, "q"), (bv, "v"), (bo, "o")):
                    sp.dma_start(dst[:], W["L1_attn_a_b" + n].partition_broadcast(P)).then_inc(S["loaded"], 16)
                sp.dma_start(bk[:], W["L1_attn_a_bk"].unsqueeze(1)).then_inc(S["loaded"], 16)
                sp.dma_start(hm[:], W["head8_mask"]).then_inc(S["loaded"], 16)
                sp.dma_start(tokid[:], W["token_ids"]).then_inc(S["loaded"], 16)
                sp.wait_ge(S["loaded"], 10 * 16)

            @block.gpsimd
            def _(pool):
                pool.iota(tokrow[:], [[1, TOKENS]], base=0, channel_multiplier=0,
                          allow_small_or_imprecise_dtypes=True)
                pool.memset(tiny[:], 1e-9)

            @block.tensor
            def _(pe):
                pe.wait_ge(S["loaded"], 10 * 16)
                for i in range(4):
                    mm = pe.transpose(ps[:, 0, P * i:P * i + P], w[:, i, :], ident)
                mm.then_inc(S["wT_ps"], 1)

            @block.scalar
            def _(act):
                act.wait_ge(S["wT_ps"], 1)
                act.activation(wT[:].rearrange("p a n -> p (a n)"), ps[:, 0, :], ACT.Copy)
        clear_signals(nc, S)

        with nc.Fori(0, TILES // GROUP) as t:
            with nc.Block() as block:

                @block.tensor
                def _(pe):
                    pe.wait_ge(S["xn_ready"], 1)
                    for i in range(GROUP):
                        mm = pe.transpose(ps[:, 0, P * i:P * i + P], xn[:, i, :], ident)
                    mm.then_inc(S["xnT_ps"], 1)
                    pe.wait_ge(S["xnT_ready"], 1)
                    for i in range(GROUP):
                        pe.matmul(ps[:, 1, P * i:P * i + P], xnT[:, P * i:P * i + P], wT[:, 0, :], start=True, stop=True)
                        mm = pe.matmul(ps[:, 2, P * i:P * i + P], xnT[:, P * i:P * i + P], wT[:, 2, :],
                                       start=True, stop=True)
                    mm.then_inc(S["qv_ps"], 1)
                    pe.matmul(ps[:, 3, :], wT[:, 1, :], xnT[:], start=True, stop=True).then_inc(S["kT_ps"], 1)
                    pe.wait_ge(S["score_ready"], 1)
                    for i in range(GROUP):
                        mm = pe.transpose(ps[0:H, 4, P * i:P * i + P], score[:, i, :], ident)
                    mm.then_inc(S["scoreT_ps"], 1)

                @block.scalar
                def _(act):
                    act.wait_ge(S["xnT_ps"], 1)
                    act.activation(xnT[:], ps[:, 0, :], ACT.Copy).then_inc(S["xnT_ready"], 1)
                    act.wait_ge(S["kT_ps"], 1)
                    act.activation(kT_all[:, bass.ds(t * GT, GT)], ps[:, 3, :], ACT.Identity, bias=bk[:])
                    act.wait_ge(S["shifted8"], 1)
                    act.activation(e8[:], e8[:], ACT.Exp).then_inc(S["exp8"], 1)
                    act.wait_ge(S["prob_ready"], 1)
                    act.activation(lp[:], e8[:], ACT.Ln, bias=tiny[:]).then_inc(S["log_ready"], 1)

                @block.vector
                def _(dve):
                    link = counted(dve, S["dve_step"])
                    link(dve.tensor_copy(xg[:], X[:, bass.ds(t * GROUP, GROUP), :]))
                    normalize_tiles(dve, link, xg, xn, B, GROUP, S["xn_ready"], GROUP)
                    dve.wait_ge(S["qv_ps"], 1)
                    psq = ps[:, 1, :].rearrange("p (g d) -> p g d", g=GROUP)
                    psv = ps[:, 2, :].rearrange("p (g d) -> p g d", g=GROUP)
                    link(dve.tensor_tensor(qg[:], psq, over_middle(bq[:], GROUP), ALU.add))
                    dve.tensor_tensor(v_all[:, bass.ds(t * GROUP, GROUP), :], psv, over_middle(bv[:], GROUP), ALU.add)
                    dve.tensor_copy(q_all[:, bass.ds(t * GROUP, GROUP), :], qg[:])
                    q8 = qg[:].rearrange("p g (h e) -> p (g h) e", e=HD)
                    link(dve.tensor_reduce(m8[:], q8, X_AXIS, ALU.max))
                    dve.tensor_tensor(e8[:], q8, over_inner(m8[:], HD), ALU.subtract).then_inc(S["shifted8"], 1)
                    link(dve.tensor_tensor(t8[:], q8, q8, ALU.mult))
                    link(dve.tensor_reduce(s8[:], t8[:], X_AXIS, ALU.add))
                    link(dve.tensor_scalar(s8[:], s8[:], SMALLEST, None, ALU.max))
                    inv_sqrt(dve, link, s8[:], l2[:], r8[:], r8b[:])
                    link(dve.tensor_tensor(l2[:], l2[:], s8[:], ALU.mult))
                    link(dve.tensor_reduce(s8[:], q8, X_AXIS, ALU.add))
                    link(dve.tensor_scalar(s8[:], s8[:], 1.0 / HD, None, ALU.mult))
                    link(dve.tensor_tensor(t8[:], q8, over_inner(s8[:], HD), ALU.subtract))
                    link(dve.tensor_tensor(t8[:], t8[:], t8[:], ALU.mult))
                    link(dve.tensor_reduce(var8[:], t8[:], X_AXIS, ALU.add))
                    dve.wait_ge(S["exp8"], 1)
                    link(dve.tensor_reduce(s8[:], e8[:], X_AXIS, ALU.add))
                    link(dve.reciprocal(s8[:], s8[:]))
                    dve.tensor_tensor(e8[:], e8[:], over_inner(s8[:], HD), ALU.mult).then_inc(S["prob_ready"], 1)
                    dve.wait_ge(S["log_ready"], 1)
                    link(dve.tensor_tensor(t8[:], e8[:], lp[:], ALU.mult))
                    link(dve.tensor_reduce(ent[:], t8[:], X_AXIS, ALU.add))
                    link(dve.tensor_scalar(ent[:], ent[:], -0.3, None, ALU.mult))
                    link(dve.scalar_tensor_tensor(out=ent[:], in0=l2[:], scalar=0.5, in1=ent[:],
                                                  op0=ALU.mult, op1=ALU.add))
                    dve.scalar_tensor_tensor(out=score[:].rearrange("p g h -> p (g h)"), in0=var8[:],
                                             scalar=0.2 / (HD - 1), in1=ent[:], op0=ALU.mult, op1=ALU.add)\
                        .then_inc(S["score_ready"], 1)
                    dve.wait_ge(S["scoreT_ps"], 1)
                    dve.tensor_copy(qs[:, bass.ds(t * GT, GT)], ps[0:H, 4, :])
            clear_signals(nc, S)

        qs2, dev = sb("qs2", [H, TOKENS]), sb("dev", [H, TOKENS])
        top = sb("top", [H, 2, 8])
        topi, topf = sb("topi", [H, 2, 8], U32), sb("topf", [H, 16])
        st, u, ut, ut2, ur = (sb(n, [H, 1]) for n in ("st", "u", "ut", "ut2", "ur"))
        zexp = sb("zexp", [H, H, TOP])
        idx = sb("idx", [P, H * TOP])
        idxcol, ucol, valid = sb("idxcol", [HALF, 2]), sb("ucol", [HALF, 1]), sb("valid", [HALF, 1])
        rank = sb("rank", [HALF, 1])
        sel = sb("sel", [P, TILES, H * TOP])
        qexp = sb("qexp", [P, H, TOP])
        mrow, srow = sb("mrow", [HALF, 1]), sb("srow", [HALF, 1])
        probs = sb("probs", [HALF, TOKENS])
        probsT = sb("probsT", [P, TILES, H * TOP])
        oT = sb("oT", [P, H, TOP])
        ow = sb("ow", [HALF, 2, DIM])
        selT = sb("selT", [HALF, 2, TOKENS])
        A = signals(nc, ctx, """rank_loaded stats_ready z_ready idx_ps idx_ready cols_ps sel_ready q_ps qexp_ready
            top_scores_ps rowmax_ready probs_exp probs_ready probsT_ps probsT_ready o_ps oT_ready ow_ps ow_ready
            selT_ready y_ps top_step""")
        with nc.Block() as block:

            @block.sync
            def _(sp):
                sp.dma_start(rank[:], W["rank_ids"]).then_inc(A["rank_loaded"], 16)
                sp.wait_ge(A["rank_loaded"], 16)

            @block.tensor
            def _(pe):
                pe.wait_ge(A["z_ready"], 1)
                pe.matmul(ps[:, 0, 0:H * TOP], ones[0:H, :], zexp[:].rearrange("p h r -> p (h r)"),
                          start=True, stop=True).then_inc(A["idx_ps"], 1)
                pe.wait_ge(A["idx_ready"], 1)
                for g in range(2):
                    pe.matmul(ps[0:HALF, 1, g:g + 1], idx[0:1, HALF * g:HALF * g + HALF], ones[0:1, 0:1],
                              start=True, stop=True)
                pe.matmul(ps[0:HALF, 1, 2:3], ones[0:1, 0:HALF], u[0:1, :], start=True, stop=True)\
                    .then_inc(A["cols_ps"], 1)
                pe.wait_ge(A["sel_ready"], 1)
                for i in range(TILES):
                    mm = pe.matmul(ps[:, 7, 0:H * TOP], q_all[:, i, :], sel[:, i, :],
                                   start=(i == 0), stop=(i == TILES - 1))
                mm.then_inc(A["q_ps"], 1)
                pe.wait_ge(A["qexp_ready"], 1)
                for g in range(2):
                    if g:
                        pe.wait_ge(A["probs_exp"], 1)
                    for b in range(4):
                        mm = pe.matmul(ps[0:HALF, b, :], qexp[:, 8 * g:8 * g + 8, :].rearrange("p h r -> p (h r)"),
                                       kT_all[:, 512 * b:512 * b + 512], start=True, stop=True)
                    mm.then_inc(A["top_scores_ps"], 1)
                    pe.wait_ge(A["probs_ready"], g + 1)
                    if g:
                        pe.wait_ge(A["probsT_ready"], 1)
                    for i in range(TILES):
                        mm = pe.transpose(ps[:, 4 + i // 6, HALF * (i % 6):HALF * (i % 6) + HALF],
                                          probs[:, P * i:P * i + P], ident[0:HALF, 0:HALF])
                    mm.then_inc(A["probsT_ps"], 1)
                pe.wait_ge(A["probsT_ready"], 2)
                for i in range(TILES):
                    mm = pe.matmul(ps[:, 7, 0:H * TOP], v_all[:, i, :], probsT[:, i, :],
                                   start=(i == 0), stop=(i == TILES - 1))
                mm.then_inc(A["o_ps"], 1)
                pe.wait_ge(A["oT_ready"], 1)
                for g in range(2):
                    mm = pe.matmul(ps[0:HALF, 4, P * g:P * g + DIM],
                                   oT[:, 8 * g:8 * g + 8, :].rearrange("p h r -> p (h r)"), wT[:, 3, :],
                                   start=True, stop=True)
                mm.then_inc(A["ow_ps"], 1)
                pe.wait_ge(A["ow_ready"], 1)
                pe.wait_ge(A["selT_ready"], 1)
                for i in range(TILES):
                    for g in range(2):
                        mm = pe.matmul(ps[:, i // 4, P * (i % 4):P * (i % 4) + DIM], selT[:, g, P * i:P * i + P],
                                       ow[:, g, :], start=(g == 0), stop=(g == 1))
                mm.then_inc(A["y_ps"], 1)

            @block.scalar
            def _(act):
                for g in range(2):
                    act.wait_ge(A["rowmax_ready"], g + 1)
                    if g:
                        act.wait_ge(A["probsT_ps"], 1)
                    act.activation(probs[:], ps[0:HALF, 0:4, :].rearrange("p b n -> p (b n)"), ACT.Exp,
                                   scale=SCALE, bias=mrow[:], accum_out=srow[:]).then_inc(A["probs_exp"], 1)
                act.wait_ge(A["ow_ps"], 1)
                act.activation(ow[:].rearrange("p g n -> p (g n)"), ps[0:HALF, 4, 0:2 * P], ACT.Copy)\
                    .then_inc(A["ow_ready"], 1)

            @block.vector
            def _(dve):
                link = counted(dve, A["top_step"])
                link(dve.max(top[:, 0, :], qs[:]))
                link(dve.max_index(topi[:, 0, :], top[:, 0, :], qs[:]))
                link(dve.match_replace(out=qs2[:], in_to_replace=top[:, 0, :], in_values=qs[:], imm_value=LOWEST))
                link(dve.max(top[:, 1, :], qs2[:]))
                link(dve.max_index(topi[:, 1, :], top[:, 1, :], qs2[:]))
                link(dve.tensor_copy(topf[:], topi[:].rearrange("p a k -> p (a k)")))
                link(dve.tensor_reduce(st[:], qs[:], X_AXIS, ALU.add))
                link(dve.tensor_scalar(st[:], st[:], 1.0 / TOKENS, None, ALU.mult))
                link(dve.tensor_scalar(dev[:], qs[:], st[:], None, ALU.subtract))
                link(dve.tensor_tensor_reduce(qs2[:], dev[:], dev[:], 1.0, 0.0, ALU.mult, ALU.add, ur[:]))
                link(dve.tensor_scalar(ur[:], ur[:], 1.0 / (TOKENS - 1), None, ALU.mult))
                link(dve.tensor_scalar(ur[:], ur[:], SMALLEST, None, ALU.max))
                inv_sqrt(dve, link, ur[:], u[:], ut[:], ut2[:])
                link(dve.tensor_tensor(u[:], u[:], ur[:], ALU.mult))
                link(dve.tensor_scalar(st[:], st[:], 1e-6, None, ALU.add))
                link(dve.reciprocal(st[:], st[:]))
                link(dve.tensor_tensor(u[:], u[:], st[:], ALU.mult))
                link(dve.tensor_scalar(u[:], u[:], float(TOP), None, ALU.mult))
                link(dve.tensor_scalar(u[:], u[:], float(LEAST), float(TOP), ALU.max, ALU.min))
                link(dve.tensor_scalar(u[:], u[:], ROUND, None, ALU.add))
                link(dve.tensor_scalar(u[:], u[:], ROUND, None, ALU.subtract))
                dve.tensor_tensor(zexp[:], over_middle(topf[:, 0:TOP], H), over_inner(ident[0:H, 0:H], TOP), ALU.mult)\
                    .then_inc(A["z_ready"], 1)
                dve.wait_ge(A["idx_ps"], 1)
                dve.tensor_copy(idx[:], ps[:, 0, 0:H * TOP]).then_inc(A["idx_ready"], 1)
                dve.wait_ge(A["idx_ready"], 1)
                dve.tensor_tensor(sel[:], over_middle(idx[:], TILES), over_inner(tokid[:], H * TOP), ALU.is_equal)\
                    .then_inc(A["sel_ready"], 1)
                dve.wait_ge(A["cols_ps"], 1)
                dve.tensor_copy(idxcol[:], ps[0:HALF, 1, 0:2])
                link(dve.tensor_copy(ucol[:], ps[0:HALF, 1, 2:3]))
                dve.wait_ge(A["rank_loaded"], 16)
                link(dve.tensor_tensor(valid[:], rank[:], ucol[:], ALU.is_lt))
                for g in range(2):
                    ins = dve.tensor_scalar(selT[:, g, :], tokrow[:], idxcol[:, g:g + 1], None, ALU.is_equal)
                ins.then_inc(A["selT_ready"], 1)
                dve.wait_ge(A["q_ps"], 1)
                dve.tensor_tensor(qexp[:], heads(ps[:, 7, 0:H * TOP], H), over_inner(hm[:], TOP), ALU.mult)\
                    .then_inc(A["qexp_ready"], 1)
                for g in range(2):
                    dve.wait_ge(A["top_scores_ps"], g + 1)
                    link(dve.tensor_reduce(mrow[:], ps[0:HALF, 0:4, :].rearrange("p b n -> p (b n)"), X_AXIS, ALU.max))
                    dve.tensor_scalar(mrow[:], mrow[:], -SCALE, None, ALU.mult).then_inc(A["rowmax_ready"], 1)
                    dve.wait_ge(A["probs_exp"], g + 1)
                    link(dve.reciprocal(srow[:], srow[:]))
                    link(dve.tensor_tensor(srow[:], srow[:], valid[:], ALU.mult))
                    dve.tensor_scalar(probs[:], probs[:], srow[:], None, ALU.mult).then_inc(A["probs_ready"], 1)
                    dve.wait_ge(A["probsT_ps"], g + 1)
                    for b, n in enumerate((6, 6, 4)):
                        ins = dve.tensor_copy(probsT[:, 6 * b:6 * b + n, HALF * g:HALF * g + HALF],
                                              ps[:, 4 + b, 0:HALF * n].rearrange("p (i r) -> p i r", r=HALF))
                    ins.then_inc(A["probsT_ready"], 1)
                dve.wait_ge(A["o_ps"], 1)
                dve.tensor_tensor(oT[:], heads(ps[:, 7, 0:H * TOP], H), over_inner(hm[:], TOP), ALU.mult)\
                    .then_inc(A["oT_ready"], 1)
                link(dve.tensor_tensor(X[:], X[:], over_middle(bo[:], TILES), ALU.add))
                dve.wait_ge(A["y_ps"], 1)
                dve.tensor_tensor(X[:].rearrange("p t d -> p (t d)"), ps[:, 0:4, :].rearrange("p b n -> p (b n)"),
                                  X[:].rearrange("p t d -> p (t d)"), ALU.add)
        clear_signals(nc, A)



def local_layers(nc, W, C, X, tag):
    DEPTH, H, HD, WIN = 2, 8, 64, 64
    INNER = H * HD
    PAIRS = H // 2
    HID = int(DIM * 4 * 2 / 3)
    CUTS = [(0, 128), (128, 256), (256, HID)]
    KEYS = WIN + P
    QK_SCALE = 8.0
    ident = C["ident"]
    with ExitStack() as ctx:
        def sb(name, shape, dt=F32):
            return ctx.enter_context(nc.sbuf_tensor(f"{tag}_{name}", shape, dt))

        xl = sb("xl", [P, TILES, DIM])
        wqkv = sb("wqkv", [P, 3 * INNER])
        wo = sb("wo", [P, PAIRS, DIM])
        w1, w2 = sb("w1", [P, 2 * HID]), sb("w2", [P, 3, DIM])
        lg, lb = sb("lg", [P, 1]), sb("lb", [P, 1])
        b1 = sb("b1", [P, 2, 3])
        b2 = sb("b2", [P, DIM])
        qks = sb("qks", [P, 2, HD])
        rot_cos, rot_sin = sb("rot_cos", [P, TILES, 2, HD]), sb("rot_sin", [P, TILES, 2, HD])
        tab_cos, tab_sin = sb("tab_cos", [P, TILES, 2, HD]), sb("tab_sin", [P, TILES, 2, HD])
        bands = sb("bands", [P, 2, KEYS])
        shift = sb("shift", [P, 2, P])
        ps = ctx.enter_context(nc.psum_tensor(tag + "_ps", [P, 8, 512], F32))

        L = signals(nc, ctx, "loaded xl_ready xl_step w_loaded scales_loaded")
        B = norm_buffers(sb, TILES)
        with nc.Block() as block:

            @block.sync
            def _(sp):
                sp.dma_start(rot_cos[:], W["rot_cos"]).then_inc(L["loaded"], 16)
                sp.dma_start(rot_sin[:], W["rot_sin"]).then_inc(L["loaded"], 16)
                sp.dma_start(bands[:], W["bands"]).then_inc(L["loaded"], 16)
                sp.dma_start(shift[:], W["shift"]).then_inc(L["loaded"], 16)
                sp.wait_ge(L["loaded"], 64)

            @block.vector
            def _(dve):
                link = counted(dve, L["xl_step"])
                normalize_tiles(dve, link, X, xl, B, TILES, L["xl_ready"], TILES)
        clear_signals(nc, L)

        xt = sb("xt", [P, DIM])
        hT = sb("hT", [P, 2, KEYS])
        xlast = sb("xlast", [P, 1])
        va, vb = sb("va", [P, 2, INNER]), sb("vb", [WIN, 2, INNER])
        qksq = sb("qksq", [P, 2 * H, HD])
        ss, rn, rtmp = sb("ss", [P, 2 * H]), sb("rn", [P, 2 * H]), sb("rtmp", [P, 2, 2 * H])
        rc, rs = sb("rc", [P, 2, H, HD]), sb("rs", [P, 2, H, HD])
        qkr = sb("qkr", [P, 2 * H, HD])
        qT, kT = sb("qT", [P, 2, PAIRS, P]), sb("kT", [P, 2, PAIRS, KEYS])
        sm = sb("sm", [P, H, KEYS])
        nmx, den = sb("nmx", [P, H]), sb("den", [P, H])
        pTa, pTb = sb("pTa", [P, H, P]), sb("pTb", [WIN, H, P])
        o, oT = sb("o", [P, H, HD]), sb("oT", [P, PAIRS, P])
        x1 = sb("x1", [P, 2, DIM])
        xprev = sb("xprev", [P, 64])
        h2, n2, nT = sb("h2", [P, DIM]), sb("n2", [P, DIM]), sb("nT", [P, P])
        stats, mv, rstd = sb("stats", [P, 6]), sb("mv", [P, 2]), sb("rstd", [P, 1])
        ge, hg = sb("ge", [P, 3, P]), sb("hg", [P, 3, P])
        x1b2 = sb("x1b2", [P, DIM])

        SIGNALS = signal_pair(nc, ctx, """hT_halo xt_ready xT_ps hT_ready qk_ps va_ps vb_ps qksq_ready
            va_ready qkr_ready qkT_ps scores_ps sm_ready probs_ready pTa_ps pTa_ready pTb_ready o_ps
            o_ready oT_ps oT_ready y_ps shift_ps n2_ready nT_ps nT_ready gate_ps gelu_ready lin_ps hg_ready ff_ps
            dve_step pool_step""")

        def round_of(t, par, project, attend, feed, mask=1):
            new, old = par, 1 - par
            S = SIGNALS[new]
            with nc.Block() as block:
                zero_other_signals(block, SIGNALS[old])

                @block.tensor
                def _(pe):
                    if feed:
                        pe.matmul(ps[:, 3, 0:64], shift[:, 0, :], x1[:, new, 64:128], start=True, stop=False)
                        pe.matmul(ps[:, 3, 0:64], shift[:, 1, :], xprev[:], start=False, stop=True)\
                            .then_inc(S["shift_ps"], 1)
                    if project:
                        pe.wait_ge(S["xt_ready"], 1)
                        pe.transpose(ps[:, 2, 0:P], xt[:], ident).then_inc(S["xT_ps"], 1)
                    if attend:
                        for i in range(PAIRS):
                            for s in range(2):
                                own = slice(64 * s, 64 * s + 64)
                                col = KEYS * (i % 2)
                                mm = pe.matmul(ps[:, 4 + 2 * s + i // 2, col:col + KEYS], qT[own, old, i, :],
                                               kT[own, old, i, :], start=True, stop=True)
                        mm.then_inc(S["scores_ps"], 1)
                    if feed:
                        pe.wait_ge(S["n2_ready"], 1)
                        pe.transpose(ps[:, 3, 128:256], n2[:], ident).then_inc(S["nT_ps"], 1)
                    if project:
                        pe.wait_ge(S["hT_ready"], 1)
                        for b in range(2):
                            mm = pe.matmul(ps[:, b, :], hT[:, new, WIN:KEYS], wqkv[:, INNER * b:INNER * b + INNER],
                                           start=True, stop=True)
                        mm.then_inc(S["qk_ps"], 1)
                    if project:
                        pe.matmul(ps[:, 2, :], hT[:, new, 0:P], wqkv[:, 2 * INNER:3 * INNER], start=True, stop=True)\
                            .then_inc(S["va_ps"], 1)
                    if feed:
                        pe.wait_ge(S["nT_ready"], 1)
                        for c, (a, b) in enumerate(CUTS):
                            mm = pe.matmul(ps[0:b - a, 3, P * c:P * c + P], w1[:, HID + a:HID + b], nT[:],
                                           start=True, stop=True)
                        mm.then_inc(S["gate_ps"], 1)
                    if attend:
                        for g in range(H):
                            pe.wait_ge(S["probs_ready"], g + 1)
                            pe.transpose(ps[:, 4 + g // 4, P * (g % 4):P * (g % 4) + P], sm[:, g, 0:P], ident)
                            mm = pe.transpose(ps[0:WIN, 6 + g // 4, P * (g % 4):P * (g % 4) + P], sm[:, g, P:KEYS], ident)
                        mm.then_inc(S["pTa_ps"], 1)
                    if project:
                        pe.wait_ge(S["va_ready"], 1)
                        pe.matmul(ps[0:WIN, 2, :], hT[:, new, P:KEYS], wqkv[:, 2 * INNER:3 * INNER],
                                  start=True, stop=True).then_inc(S["vb_ps"], 1)
                    if attend:
                        pe.wait_ge(S["pTa_ready"], 1)
                        pe.wait_ge(S["pTb_ready"], 1)
                        for g in range(H):
                            head = 2 * (g % PAIRS) + g // PAIRS
                            out, own = ps[:, 4, HD * g:HD * g + HD], slice(HD * head, HD * head + HD)
                            pe.matmul(out, pTa[:, g, :], va[:, old, own], start=True, stop=False)
                            mm = pe.matmul(out, pTb[:, g, :], vb[:, old, own], start=False, stop=True)
                        mm.then_inc(S["o_ps"], 1)
                    if project:
                        pe.wait_ge(S["qkr_ready"], 1)
                        for i in range(2 * PAIRS):
                            mm = pe.transpose(ps[:, i // 4, P * (i % 4):P * (i % 4) + P],
                                              qkr[:, 2 * i:2 * i + 2, :].rearrange("p h d -> p (h d)"), ident)
                        mm.then_inc(S["qkT_ps"], 1)
                    if feed:
                        pe.wait_ge(S["gelu_ready"], 1)
                        for c, (a, b) in enumerate(CUTS):
                            mm = pe.matmul(ps[0:b - a, 3, P * c:P * c + P], w1[:, a:b], nT[:], start=True, stop=True)
                        mm.then_inc(S["lin_ps"], 1)
                    if attend:
                        pe.wait_ge(S["o_ready"], 1)
                        for i in range(PAIRS):
                            mm = pe.transpose(ps[:, 5, P * i:P * i + P],
                                              o[:, 2 * i:2 * i + 2, :].rearrange("p h d -> p (h d)"), ident)
                        mm.then_inc(S["oT_ps"], 1)
                        pe.wait_ge(S["oT_ready"], 1)
                        for i in range(PAIRS):
                            mm = pe.matmul(ps[:, 6, 0:DIM], oT[:, i, :], wo[:, i, :], start=(i == 0), stop=(i == PAIRS - 1))
                        mm.then_inc(S["y_ps"], 1)
                    if feed:
                        pe.wait_ge(S["hg_ready"], 1)
                        for c, (a, b) in enumerate(CUTS):
                            mm = pe.matmul(ps[:, 3, 384:512], hg[0:b - a, c, :], w2[0:b - a, c, :],
                                           start=(c == 0), stop=(c == 2))
                        mm.then_inc(S["ff_ps"], 1)

                @block.gpsimd
                def _(pool):
                    link = counted(pool, S["pool_step"])
                    if project:
                        link(pool.tensor_copy(hT[:, new, 0:WIN], hT[:, old, P:KEYS]))
                        pool.tensor_copy(hT[64:128, new, WIN:WIN + 1], xlast[64:128, :]).then_inc(S["hT_halo"], 1)
                        pool.wait_ge(S["hT_halo"], 1)
                        link(pool.tensor_copy(kT[:, new, :, 0:WIN], kT[:, old, :, P:KEYS]))
                    if feed:
                        pool.wait_ge(S["shift_ps"], 1)
                        pool.tensor_copy(xprev[:], x1[:, new, 64:128])

                @block.scalar
                def _(act):
                    if project:
                        act.wait_ge(S["xT_ps"], 1)
                        act.activation(hT[0:64, new, WIN:KEYS], ps[0:64, 2, 0:P], ACT.Copy)
                        act.wait_ge(S["hT_halo"], 1)
                        act.activation(xlast[64:128, :], ps[64:128, 2, P - 1:P], ACT.Copy)
                        act.activation(hT[64:128, new, WIN + 1:KEYS], ps[64:128, 2, 0:P - 1], ACT.Copy)\
                            .then_inc(S["hT_ready"], 1)
                    if feed:
                        act.wait_ge(S["nT_ps"], 1)
                        act.activation(nT[:], ps[:, 3, 128:256], ACT.Identity, scale=lg[:], bias=lb[:])\
                            .then_inc(S["nT_ready"], 1)
                    if project:
                        act.wait_ge(S["qk_ps"], 1)
                        act.activation(qksq[:].rearrange("p h d -> p (h d)"), ps[:, 0:2, :].rearrange("p b n -> p (b n)"),
                                       ACT.Square).then_inc(S["qksq_ready"], 1)
                    if attend:
                        act.wait_ge(S["sm_ready"], 1)
                        for g in range(H):
                            act.activation(sm[:, g, :], sm[:, g, :], ACT.Exp, bias=nmx[:, g:g + 1],
                                           accum_out=den[:, g:g + 1]).then_inc(S["probs_ready"], 1)
                    if project:
                        act.wait_ge(S["va_ps"], 1)
                        act.activation(va[:, new, :], ps[:, 2, :], ACT.Copy).then_inc(S["va_ready"], 1)
                    if attend:
                        act.wait_ge(S["pTa_ps"], 1)
                        act.activation(pTa[:].rearrange("p h n -> p (h n)"), ps[:, 4:6, :].rearrange("p b n -> p (b n)"),
                                       ACT.Copy).then_inc(S["pTa_ready"], 1)
                        act.activation(pTb[:].rearrange("p h n -> p (h n)"),
                                       ps[0:WIN, 6:8, :].rearrange("p b n -> p (b n)"), ACT.Copy)\
                            .then_inc(S["pTb_ready"], 1)
                    if feed:
                        act.wait_ge(S["gate_ps"], 1)
                        for c, (a, b) in enumerate(CUTS):
                            ins = act.activation(ge[0:b - a, c, :], ps[0:b - a, 3, P * c:P * c + P], ACT.Gelu,
                                                 bias=b1[0:b - a, 1, c:c + 1])
                        ins.then_inc(S["gelu_ready"], 1)
                    if project:
                        act.wait_ge(S["vb_ps"], 1)
                        act.activation(vb[:, new, :], ps[0:WIN, 2, :], ACT.Copy)
                        act.wait_ge(S["qkT_ps"], 1)
                        act.activation(qT[:, new].rearrange("p i n -> p (i n)"), ps[:, 0, :], ACT.Copy)
                        act.activation(kT[:, new, :, WIN:KEYS], heads(ps[:, 1, :], PAIRS), ACT.Copy)
                    if attend:
                        act.wait_ge(S["oT_ps"], 1)
                        act.activation(oT[:].rearrange("p i n -> p (i n)"), ps[:, 5, :], ACT.Copy)\
                            .then_inc(S["oT_ready"], 1)

                @block.vector
                def _(dve):
                    link = counted(dve, S["dve_step"])
                    if project:
                        dve.tensor_copy(xt[:], tile_of(xl, t)).then_inc(S["xt_ready"], 1)
                    if feed:
                        dve.tensor_copy(h2[:, 0:64], x1[:, new, 0:64])
                        dve.wait_ge(S["shift_ps"], 1)
                        link(dve.tensor_copy(h2[:, 64:128], ps[:, 3, 0:64]))
                        normalize_rows(dve, link, h2[:], n2[:], stats[:], mv[:], rstd[:]).then_inc(S["n2_ready"], 1)
                        dve.tensor_tensor(x1b2[:], x1[:, new, :], b2[:], ALU.add)
                    if attend:
                        dve.wait_ge(S["scores_ps"], 1)
                        scores = ps[:, 4:8, 0:2 * KEYS].rearrange("p b (s k) -> p b s k", s=2)
                        band = bands[:, mask, :].unsqueeze(1).unsqueeze(1).broadcast_to([P, 4, 2, KEYS])
                        link(dve.tensor_tensor(sm[:].rearrange("p (b s) k -> p b s k", s=2), scores, band, ALU.add))
                        link(dve.tensor_reduce(nmx[:], sm[:], X_AXIS, ALU.max))
                        dve.tensor_scalar(nmx[:], nmx[:], -1.0, None, ALU.mult).then_inc(S["sm_ready"], 1)
                    if project:
                        qk = ps[:, 0:2, :].rearrange("p a (h d) -> p a h d", h=H)
                        cos = tab_cos[:, bass.ds(t, 1), :, :].rearrange("p o a d -> p (o a) d")
                        sin = tab_sin[:, bass.ds(t, 1), :, :].rearrange("p o a d -> p (o a) d")

                        def each_head(tab, lo, hi):
                            return tab[:, :, lo:hi].unsqueeze(2).broadcast_to([P, 2, H, hi - lo])

                        dve.wait_ge(S["qksq_ready"], 1)
                        dve.tensor_tensor(rc[:], qk, each_head(cos, 0, 64), ALU.mult)
                        dve.tensor_tensor(rs[:, :, :, 0:32], qk[:, :, :, 32:64], each_head(sin, 0, 32), ALU.mult)
                        link(dve.tensor_tensor(rs[:, :, :, 32:64], qk[:, :, :, 0:32], each_head(sin, 32, 64), ALU.mult))
                    if project:
                        link(dve.tensor_reduce(ss[:], qksq[:], X_AXIS, ALU.add))
                        link(dve.tensor_scalar(ss[:], ss[:], 1e-24, None, ALU.max))
                        inv_sqrt(dve, link, ss[:], rn[:], rtmp[:, 0, :], rtmp[:, 1, :])
                        link(dve.tensor_scalar(rn[:, 0:H], rn[:, 0:H], QK_SCALE, None, ALU.mult))
                        link(dve.tensor_tensor(rc[:].rearrange("p a h d -> p (a h d)"),
                                               rc[:].rearrange("p a h d -> p (a h d)"),
                                               rs[:].rearrange("p a h d -> p (a h d)"), ALU.add))
                        dve.tensor_tensor(qkr[:], rc[:].rearrange("p a h d -> p (a h) d"), over_inner(rn[:], HD),
                                          ALU.mult).then_inc(S["qkr_ready"], 1)
                    if attend:
                        dve.wait_ge(S["probs_ready"], H)
                        link(dve.reciprocal(den[:], den[:]))
                        dve.wait_ge(S["o_ps"], 1)
                        dve.tensor_tensor(o[:].rearrange("p (i s) d -> p s i d", s=2),
                                          ps[:, 4, :].rearrange("p (s i d) -> p s i d", s=2, i=PAIRS),
                                          over_inner(den[:], HD).rearrange("p (s i) d -> p s i d", s=2), ALU.mult)\
                            .then_inc(S["o_ready"], 1)
                    if feed:
                        dve.wait_ge(S["lin_ps"], 1)
                        for c, (a, b) in enumerate(CUTS):
                            ins = dve.scalar_tensor_tensor(
                                out=hg[0:b - a, c, :], in0=ps[0:b - a, 3, P * c:P * c + P],
                                scalar=b1[0:b - a, 0, c:c + 1], in1=ge[0:b - a, c, :], op0=ALU.add, op1=ALU.mult)
                        ins.then_inc(S["hg_ready"], 1)
                    if attend:
                        dve.wait_ge(S["y_ps"], 1)
                        dve.tensor_tensor(x1[:, old, :], ps[:, 6, 0:DIM], tile_of(xl, t - 1), ALU.add)
                    if feed:
                        dve.wait_ge(S["ff_ps"], 1)
                        dve.tensor_tensor(tile_of(xl, t - 2), ps[:, 3, 384:512], x1b2[:], ALU.add)

        with nc.Fori(0, DEPTH) as l:
            def of(name):
                a = W["L1_ffn_" + name][bass.ds(l, 1)]
                return a.rearrange("o a b -> (o a) b") if len(a.shape) == 3 else a.rearrange("o a -> (o a)")

            with nc.Block() as block:
                loads = [(wqkv[:], of("wqkv")), (wo[:], of("wo").rearrange("(c p) n -> p c n", p=P)),
                         (w1[:], of("w1")),
                         (w2[:, 0:2, :], of("w2")[0:256, :].rearrange("(c p) n -> p c n", p=P)),
                         (w2[0:HID - 256, 2, :], of("w2")[256:HID, :]),
                         (lg[:], of("ln_g").unsqueeze(1)), (lb[:], of("ln_b").unsqueeze(1)),
                         (b2[:], of("b2").partition_broadcast(P))]
                scales = [(qks[:, 0, :], of("q_scale").partition_broadcast(P)),
                          (qks[:, 1, :], of("k_scale").partition_broadcast(P))]
                for half in range(2):
                    for c, (a, b) in enumerate(CUTS):
                        loads.append((b1[0:b - a, half, c:c + 1],
                                      of("b1")[HID * half + a:HID * half + b].unsqueeze(1)))

                @block.sync
                def _(sp):
                    for dst, src in scales:
                        sp.dma_start(dst, src).then_inc(L["scales_loaded"], 16)
                    for dst, src in loads:
                        sp.dma_start(dst, src).then_inc(L["w_loaded"], 16)
                    sp.wait_ge(L["w_loaded"], 16 * len(loads))

                @block.gpsimd
                def _(pool):
                    pool.memset(hT[:], 0.0)
                    pool.memset(kT[:], 0.0)
                    pool.memset(xlast[:], 0.0)
                    pool.memset(xprev[:], 0.0)

                @block.vector
                def _(dve):
                    dve.wait_ge(L["scales_loaded"], 16 * len(scales))
                    for a in range(2):
                        dve.tensor_tensor(tab_cos[:, :, a, :], rot_cos[:, :, a, :],
                                          over_middle(qks[:, a, :], TILES), ALU.mult)
                        dve.tensor_tensor(tab_sin[:, :, a, 0:32], rot_sin[:, :, a, 0:32],
                                          over_middle(qks[:, a, 32:64], TILES), ALU.mult)
                        dve.tensor_tensor(tab_sin[:, :, a, 32:64], rot_sin[:, :, a, 32:64],
                                          over_middle(qks[:, a, 0:32], TILES), ALU.mult)
            clear_signals(nc, L)
            round_of(0, 0, project=True, attend=False, feed=False)
            round_of(1, 1, project=True, attend=True, feed=False, mask=0)
            with nc.Fori(1, TILES // 2) as i:
                for par in range(2):
                    round_of(i * 2 + par, par, project=True, attend=True, feed=True)
            round_of(TILES, 0, project=False, attend=True, feed=True)
            round_of(TILES + 1, 1, project=False, attend=False, feed=True)
            for S in SIGNALS:
                clear_signals(nc, S)

        with nc.Block() as block:

            @block.vector
            def _(dve):
                dve.tensor_tensor(X[:], X[:], xl[:], ALU.add)
        clear_signals(nc, L)



def grouped_attention(nc, W, C, X, tag):
    H, KV, HD = 16, 4, 64
    REP = H // KV
    HALF = TOKENS // 2
    BLK = 512
    HT = HALF // P
    SCALE = HD ** -0.5
    F32R = mybir.dt.float32r
    ident, ones = C["ident"], C["ones"]
    with ExitStack() as ctx:
        def sb(name, shape, dt=F32):
            return ctx.enter_context(nc.sbuf_tensor(f"{tag}_{name}", shape, dt))

        wq, wqr = sb("wq", [P, H, HD]), sb("wqr", [P, H, HD])
        wk, wkr = sb("wk", [P, KV, HD]), sb("wkr", [P, KV, HD])
        wv = sb("wv", [P, KV, HD])
        wo = sb("wo", [P, H, DIM])
        cos, sin = sb("cos", [HD, TOKENS]), sb("sin", [HD, TOKENS])
        bo = sb("bo", [P, DIM])
        xnT = sb("xnT", [P, TOKENS])
        khh, kll = sb("khh", [P, TOKENS], F32R), sb("kll", [P, TOKENS], F32R)
        v = sb("v", [P, TILES, HD])
        q2 = sb("q2", [P, 2, HALF], F32R)
        mrow = sb("mrow", [P, 2, HALF], F32R)
        first = sb("first", [P, P], F32R)
        xn = sb("xn", [P, TILES, DIM])
        B = norm_buffers(sb, TILES)
        wks, wqs = sb("wks", [P, 2, HD]), sb("wqs", [P, 2, HD])
        wos = sb("wos", [P, DIM])
        rope = sb("rope", [HD, 6, BLK])
        mpart, nm = sb("mpart", [P, HT, 4]), sb("nm", [P, HT])
        probs = sb("probs", [P, 3, HALF])
        acc, acc_odd = sb("acc", [P, 2, HALF]), sb("acc_odd", [P, 2, HALF])
        oT = sb("oT", [P, BLK])
        rden = sb("rden", [P, HT])
        ps = ctx.enter_context(nc.psum_tensor(tag + "_ps", [P, 8, 512], F32))

        S = signals(nc, ctx, """loaded xn_ready xnT_ps wks_ready k_ps k_rounded rounded_copy rest_copy v_ps wqs_ready q_ps rope_done split_done kpart_done
            max_ps max_done nm_ready row_ps row_ready wos_ready scores_ps probs_ready pv_ps oT_ready sum_step odd_step v_ready
            den_ps den_done y_ps y_done dve_step pool_step""")

        with nc.Block() as block:
            loads = [(wq[:], W["L1_attn_b_Wq"].rearrange("d (h e) -> d h e", h=H)),
                     (wk[:], W["L1_attn_b_Wkv"][:, 0:KV * HD].rearrange("d (h e) -> d h e", h=KV)),
                     (wv[:], W["L1_attn_b_Wkv"][:, KV * HD:2 * KV * HD].rearrange("d (h e) -> d h e", h=KV)),
                     (wo[0:HD], W["L1_attn_b_Wo"].rearrange("(h e) n -> e h n", h=H)),
                     (wo[HD:P], W["L1_attn_b_Wo"].rearrange("(h e) n -> e h n", h=H)),
                     (cos[:], W["rope_cos"]), (sin[:], W["rope_sin"]),
                     (bo[:], W["L1_attn_b_bo"].partition_broadcast(P))]

            @block.sync
            def _(sp):
                for dst, src in loads:
                    sp.dma_start(dst, src).then_inc(S["loaded"], 16)

            @block.gpsimd
            def _(pool):
                link = counted(pool, S["pool_step"])
                link(pool.memset(rope[:], 0.0))
                link(pool.memset(acc[:], 0.0))
                link(pool.memset(acc[0:1, 0, 0:P], 1.0))
                link(pool.tensor_copy(first[:], acc[:, 0, 0:P]))
                for half in range(2):
                    link(pool.tensor_copy(mrow[:, half, :], acc[:, 1, :]))
                link(pool.memset(oT[:], 0.0))
                link(pool.memset(wos[:], 0.0))
                link(pool.memset(acc_odd[:], 1.0))

            @block.vector
            def _(dve):
                dve.wait_ge(S["loaded"], 16 * len(loads))
                for w, wr in ((wq, wqr), (wk, wkr)):
                    dve.tensor_scalar(wr[:, :, 0:32], w[:, :, 32:64], -1.0, None, ALU.mult)
                    dve.tensor_copy(wr[:, :, 32:64], w[:, :, 0:32])
        clear_signals(nc, S)

        with nc.Block() as block:

            @block.vector
            def _(dve):
                link = counted(dve, S["dve_step"])
                normalize_tiles(dve, link, X, xn, B, TILES, S["xn_ready"], GROUP)
                dve.wait_ge(S["xn_ready"], TILES // GROUP)
                dve.tensor_tensor(X[:], X[:], over_middle(bo[:], TILES), ALU.add)

            @block.tensor
            def _(pe):
                for g in range(TILES // GROUP):
                    pe.wait_ge(S["xn_ready"], g + 1)
                    for i in range(GROUP):
                        mm = pe.transpose(ps[:, g, P * i:P * i + P], xn[:, g * GROUP + i, :], ident)
                    mm.then_inc(S["xnT_ps"], 1)

            @block.scalar
            def _(act):
                for g in range(TILES // GROUP):
                    act.wait_ge(S["xnT_ps"], g + 1)
                    act.activation(xnT[:, g * GROUP * P:(g + 1) * GROUP * P], ps[:, g, :], ACT.Copy)
        clear_signals(nc, S)


        def proj(pe, n, half, b, weights):
            if b == 0:
                if weights:
                    pe.wait_ge(S["wqs_ready"], weights)
                if n:
                    pe.wait_ge(S["row_ready"], 2 * n)
            else:
                pe.wait_ge(S["rope_done"], 2 * n + 1)
            cols = slice(HALF * half + BLK * b, HALF * half + BLK * b + BLK)
            pe.matmul(ps[0:HD, 5, :], wqs[:, 0, :], xnT[:, cols], start=True, stop=True)
            pe.matmul(ps[0:HD, 6, :], wqs[:, 1, :], xnT[:, cols], start=True, stop=True).then_inc(S["q_ps"], 1)

        def rotate(dve, link, n, half, b):
            cols = slice(HALF * half + BLK * b, HALF * half + BLK * b + BLK)
            dve.wait_ge(S["q_ps"], 2 * n + b + 1)
            dve.scalar_tensor_tensor(out=rope[:, 0, :], in0=ps[0:HD, 5, :], scalar=SCALE, in1=cos[:, cols],
                                     op0=ALU.mult, op1=ALU.mult)
            link(dve.scalar_tensor_tensor(out=rope[:, 1, :], in0=ps[0:HD, 6, :], scalar=SCALE, in1=sin[:, cols],
                                          op0=ALU.mult, op1=ALU.mult))
            if n:
                dve.wait_ge(S["split_done"], b + 1)
            dve.tensor_tensor(rope[:, 2 + b, :], rope[:, 0, :], rope[:, 1, :], ALU.add)
            dve.tensor_tensor(q2[0:HD, half, BLK * b:BLK * b + BLK], rope[:, 0, :], rope[:, 1, :], ALU.add)\
                .then_inc(S["rope_done"], 1)

        def split_queries(pool, n, half, b):
            cols = slice(BLK * b, BLK * b + BLK)
            pool.wait_ge(S["rope_done"], 2 * n + b + 1)
            if b:
                pool.wait_ge(S["split_done"], 2 * n + 1)
            pool.tensor_tensor(q2[HD:P, half, cols], rope[:, 2 + b, :], q2[0:HD, half, cols], ALU.subtract)\
                .then_inc(S["split_done"], 1)

        def rough_scores(pe, n, half, qt, chunks, last_bank_free):
            if qt == 0 and chunks[0] == 0:
                pe.wait_ge(S["split_done"], 2 * n + 2)
                pe.wait_ge(*last_bank_free)
            for c in chunks:
                at = 4 * qt + c
                if at >= 3:
                    pe.wait_ge(S["max_done"], 32 * n + at - 2)
                pe.matmul(ps[:, 5 + at % 3, :], q2[:, half, P * qt:P * qt + P],
                          khh[:, BLK * c:BLK * c + BLK], start=True, stop=True)\
                    .then_inc(S["max_ps"], 1)

        def part_max(dve, n, qt):
            for c in range(4):
                at = 4 * qt + c
                dve.wait_ge(S["max_ps"], 32 * n + at + 1)
                dve.tensor_reduce(mpart[:, qt, c:c + 1], ps[:, 5 + at % 3, :], X_AXIS, ALU.max)\
                    .then_inc(S["max_done"], 1)

        def negative_max(dve, link, n):
            dve.wait_ge(S["max_done"], 32 * n + 32)
            link(dve.tensor_reduce(nm[:], mpart[:], X_AXIS, ALU.max))
            dve.tensor_scalar(nm[:], nm[:], -1.0, None, ALU.mult).then_inc(S["nm_ready"], 1)

        def max_rows(pe, n):
            pe.wait_ge(S["nm_ready"], n + 1)
            for b in range(2):
                for i in range(4):
                    mm = pe.matmul(ps[0:1, 5 + b, P * i:P * i + P], nm[:, 4 * b + i:4 * b + i + 1], ident,
                                   start=True, stop=True)
                mm.then_inc(S["row_ps"], 1)

        def place_rows(act, n, half):
            for b in range(2):
                act.wait_ge(S["row_ps"], 2 * n + b + 1)
                act.activation(mrow[0:1, half, BLK * b:BLK * b + BLK], ps[0:1, 5 + b, :], ACT.Copy)\
                    .then_inc(S["row_ready"], 1)


        def out_sums(pe, p):
            if p:
                pe.wait_ge(S["sum_step"], TILES // 2)
                pe.wait_ge(S["odd_step"], TILES // 2)
                pe.wait_ge(S["y_done"], 2)
            for i in range(HT):
                for a, sums in enumerate((acc, acc_odd)):
                    mm = pe.matmul(ps[:, 7, i:i + 1], sums[:, 1 - p, P * i:P * i + P], ones[:, 0:1],
                                   start=(a == 0), stop=(a == 1))
            mm.then_inc(S["den_ps"], 1)

        def out_block(pe, p, b):
            pe.wait_ge(S["den_done"], p + 1)
            if b:
                pe.wait_ge(S["y_done"], 2 * p + 1)
            elif p:
                pe.wait_ge(S["oT_ready"], 1)
                pe.wait_ge(S["wos_ready"], 1)
            for i in range(4):
                mm = pe.matmul(ps[:, 7, P * i:P * i + P], oT[HD * b:HD * b + HD, P * i:P * i + P],
                               wos[HD * b:HD * b + HD, :], start=True, stop=True)
            mm.then_inc(S["y_ps"], 1)

        def sums_inverse(dve, p):
            dve.wait_ge(S["den_ps"], p + 1)
            dve.reciprocal(rden[:], ps[:, 7, 0:HT]).then_inc(S["den_done"], 1)

        def add_block(dve, p, b):
            dve.wait_ge(S["den_done"], p + 1)
            dve.wait_ge(S["y_ps"], 2 * p + b + 1)
            for i in range(4):
                tile = HT * (1 - p) + 4 * b + i
                ins = dve.scalar_tensor_tensor(out=X[:, tile, :], in0=ps[:, 7, P * i:P * i + P],
                                               scalar=rden[:, 4 * b + i:4 * b + i + 1], in1=X[:, tile, :],
                                               op0=ALU.mult, op1=ALU.add)
            ins.then_inc(S["y_done"], 1)


        def scores(pe, at):
            p, k = at // TILES, at % TILES
            if at >= 2:
                pe.wait_ge(S["probs_ready"], at - 1)
            for i, (keys, moving) in enumerate(((khh[:, P * k:P * k + P], q2), (kll[:, P * k:P * k + P], q2),
                                                (first[:], mrow))):
                if i == 2 and at == TILES:
                    pe.wait_ge(S["row_ready"], 2)
                for b in range(2):
                    mm = pe.matmul(ps[:, 2 * (k % 2) + b, :], keys, moving[:, p, BLK * b:BLK * b + BLK],
                                   start=(i == 0), stop=(i == 2))
            mm.then_inc(S["scores_ps"], 1)

        def context(pe, at):
            k = at % TILES
            pe.wait_ge(S["probs_ready"], at + 1)
            if at == TILES:
                pe.wait_ge(S["oT_ready"], 1)
            for b in range(2):
                mm = pe.matmul(ps[HD * b:HD * b + HD, 4, :], v[:, k, :], probs[:, at % 3, BLK * b:BLK * b + BLK],
                               start=(k == 0), stop=(k == TILES - 1))
            mm.then_inc(S["pv_ps"], 1)

        def add_probs(eng, step, sums, at):
            p, k = at // TILES, at % TILES
            eng.wait_ge(S["probs_ready"], at + 1)
            if k < 2:
                ins = eng.tensor_copy(sums[:, p, :], probs[:, at % 3, :])
            else:
                eng.wait_ge(S[step], at // 2)
                ins = eng.tensor_tensor(sums[:, p, :], sums[:, p, :], probs[:, at % 3, :], ALU.add)
            ins.then_inc(S[step], 1)

        ROUGH = 5

        def head(g, j, last):
            with nc.Block() as block:
                this_head = g * REP + j

                @block.gpsimd
                def _(pool):
                    link = counted(pool, S["pool_step"])
                    before = None
                    for p in range(2):
                        prep = not (last and p == 1)
                        if p:
                            pool.wait_ge(S["den_ps"], 1)
                        for k in range(1, TILES, 2):
                            at = TILES * p + k
                            if before:
                                pool.wait_ge(*before)
                            add_probs(pool, "odd_step", acc_odd, at)
                            before = (S["odd_step"], at // 2 + 1)
                            if prep and k in (1, 3):
                                pool.wait_ge(*before)
                                split_queries(pool, p, 1 - p, (k - 1) // 2)
                                before = (S["split_done"], 2 * p + (k - 1) // 2 + 1)
                            if p == 0 and k == 5:
                                pool.wait_ge(*before)
                                pool.wait_ge(S["y_ps"], 2)
                                pool.tensor_copy(wos[:], tile_of(wo, this_head)).then_inc(S["wos_ready"], 1)
                                before = (S["wos_ready"], 1)
                            if p == 0 and k == 7 and not last:
                                pool.wait_ge(*before)
                                pool.wait_ge(S["q_ps"], 2)
                                link(pool.tensor_copy(wqs[:, 0, :], tile_of(wq, this_head + 1)))
                                pool.tensor_copy(wqs[:, 1, :], tile_of(wqr, this_head + 1)).then_inc(S["wqs_ready"], 1)
                                before = (S["wqs_ready"], 1)

                @block.tensor
                def _(pe):
                    scores(pe, 0)
                    scores(pe, 1)
                    out_sums(pe, 0)
                    for at in range(2 * TILES):
                        p, k = at // TILES, at % TILES
                        prep = not (last and p == 1)
                        rough = prep and ROUGH <= k < ROUGH + HT
                        if p and k == 1:
                            out_sums(pe, 1)
                        if k in (1 + p, 2 + p):
                            out_block(pe, p, k - 1 - p)
                        if rough:
                            rough_scores(pe, p, 1 - p, k - ROUGH, (0, 1), (S["y_done"], 2 * p + 2))
                        context(pe, at)
                        if rough:
                            rough_scores(pe, p, 1 - p, k - ROUGH, (2, 3), None)
                        if at + 2 < 2 * TILES:
                            scores(pe, at + 2)
                        if prep and k in (0, 2):
                            proj(pe, p, 1 - p, k // 2, weights=p)
                        if prep and k == ROUGH + HT:
                            max_rows(pe, p)

                @block.scalar
                def _(act):
                    for p in range(2):
                        prep = not (last and p == 1)
                        for k in range(TILES):
                            at = TILES * p + k
                            act.wait_ge(S["scores_ps"], at + 1)
                            if at >= 3:
                                act.wait_ge(S["pv_ps"], at - 2)
                                act.wait_ge(S["odd_step" if (at - 3) % 2 else "sum_step"], (at - 3) // 2 + 1)
                            act.activation(probs[:, at % 3, :],
                                           ps[:, 2 * (k % 2):2 * (k % 2) + 2, :].rearrange("p b n -> p (b n)"),
                                           ACT.Exp).then_inc(S["probs_ready"], 1)
                            if prep and k == ROUGH + HT + 1:
                                place_rows(act, p, 1 - p)
                        act.wait_ge(S["pv_ps"], TILES * (p + 1))
                        act.wait_ge(S["y_ps"], 2 * p + 2)
                        act.activation(oT[:], ps[:, 4, :], ACT.Copy).then_inc(S["oT_ready"], 1)

                @block.vector
                def _(dve):
                    link = counted(dve, S["dve_step"])
                    sums_inverse(dve, 0)
                    for at in range(2 * TILES):
                        p, k = at // TILES, at % TILES
                        prep = not (last and p == 1)
                        if k % 2 == 0:
                            add_probs(dve, "sum_step", acc, at)
                        if p and k == 1:
                            sums_inverse(dve, 1)
                        if k in (1 + p, 2 + p):
                            add_block(dve, p, k - 1 - p)
                        if prep and k in (0, 2):
                            rotate(dve, link, p, 1 - p, k // 2)
                        if prep and ROUGH <= k < ROUGH + HT:
                            part_max(dve, p, k - ROUGH)
                        if prep and k == ROUGH + HT - 1:
                            negative_max(dve, link, p)
            clear_signals(nc, S)

        with nc.Fori(0, KV) as g:
            with nc.Block() as block:

                @block.gpsimd
                def _(pool):
                    link = counted(pool, S["pool_step"])
                    link(pool.tensor_copy(wqs[:, 0, :], tile_of(wq, g * REP)))
                    pool.tensor_copy(wqs[:, 1, :], tile_of(wqr, g * REP)).then_inc(S["wqs_ready"], 1)
                    pool.wait_ge(S["wqs_ready"], 1)
                    link(pool.tensor_copy(wks[:, 0, :], tile_of(wk, g)))
                    pool.tensor_copy(wks[:, 1, :], tile_of(wkr, g)).then_inc(S["wks_ready"], 1)
                    pool.wait_ge(S["wks_ready"], 1)
                    for b in range(2):
                        split_queries(pool, 0, 0, b)
                    pool.wait_ge(S["split_done"], 2)
                    for b in range(TOKENS // BLK):
                        cols = slice(BLK * b, BLK * b + BLK)
                        pool.wait_ge(S["k_rounded"], b + 1)
                        if b:
                            pool.wait_ge(S["rest_copy"], b)
                        pool.tensor_tensor(kll[HD:P, cols], rope[:, 4 + b % 2, :], khh[0:HD, cols], ALU.subtract)\
                            .then_inc(S["rest_copy"], 1)

                @block.tensor
                def _(pe):
                    proj(pe, 0, 0, 0, weights=1)
                    pe.wait_ge(S["wks_ready"], 1)
                    for b in range(TOKENS // BLK):
                        if b >= 2:
                            pe.wait_ge(S["k_rounded"], b - 1)
                        for r in range(2):
                            mm = pe.matmul(ps[0:HD, 2 * (b % 2) + r, :], wks[:, r, :], xnT[:, BLK * b:BLK * b + BLK],
                                           start=True, stop=True)
                        mm.then_inc(S["k_ps"], 1)
                        if b == 1:
                            proj(pe, 0, 0, 1, weights=1)
                    for i in range(TILES):
                        mm = pe.matmul(ps[:, 4 + 3 * (i // 8), HD * (i % 8):HD * (i % 8) + HD], xnT[:, P * i:P * i + P],
                                       tile_of(wv, g), start=True, stop=True)
                    mm.then_inc(S["v_ps"], 1)
                    pe.wait_ge(S["k_rounded"], TOKENS // BLK)
                    pe.wait_ge(S["rounded_copy"], TOKENS // BLK)
                    for qt in range(HT):
                        rough_scores(pe, 0, 0, qt, range(4), (S["v_ready"], 1))
                    max_rows(pe, 0)

                @block.scalar
                def _(act):
                    for b in range(TOKENS // BLK):
                        cols = slice(BLK * b, BLK * b + BLK)
                        act.wait_ge(S["k_rounded"], b + 1)
                        act.activation(khh[HD:P, cols], khh[0:HD, cols], ACT.Copy).then_inc(S["rounded_copy"], 1)
                    act.wait_ge(S["v_ps"], 1)
                    for i in range(2):
                        ins = act.activation(v[:, 8 * i:8 * i + 8, :].rearrange("p t d -> p (t d)"), ps[:, 4 + 3 * i, :],
                                             ACT.Copy)
                    ins.then_inc(S["v_ready"], 1)
                    place_rows(act, 0, 0)

                @block.vector
                def _(dve):
                    link = counted(dve, S["dve_step"])
                    rotate(dve, link, 0, 0, 0)
                    for b in range(TOKENS // BLK):
                        if b == 2:
                            rotate(dve, link, 0, 0, 1)
                        cols = slice(BLK * b, BLK * b + BLK)
                        dve.wait_ge(S["rope_done"], 1 + b // 2)
                        dve.wait_ge(S["k_ps"], b + 1)
                        dve.tensor_tensor(rope[:, 0, :], ps[0:HD, 2 * (b % 2), :], cos[:, cols], ALU.mult)
                        link(dve.tensor_tensor(rope[:, 1, :], ps[0:HD, 2 * (b % 2) + 1, :], sin[:, cols], ALU.mult))
                        if b >= 2:
                            dve.wait_ge(S["rest_copy"], b - 1)
                        dve.tensor_tensor(rope[:, 4 + b % 2, :], rope[:, 0, :], rope[:, 1, :], ALU.add)
                        dve.tensor_tensor(khh[0:HD, cols], rope[:, 0, :], rope[:, 1, :], ALU.add)\
                            .then_inc(S["k_rounded"], 1)
                        dve.wait_ge(S["k_rounded"], b + 1)
                        link(dve.tensor_tensor(kll[0:HD, cols], rope[:, 4 + b % 2, :], khh[0:HD, cols], ALU.subtract))
                    dve.wait_ge(S["rest_copy"], TOKENS // BLK)
                    for qt in range(HT):
                        part_max(dve, 0, qt)
                    negative_max(dve, link, 0)
            clear_signals(nc, S)
            with nc.Fori(0, REP - 1) as j:
                head(g, j, last=False)
            head(g, REP - 1, last=True)

        with nc.Block() as block:

            @block.tensor
            def _(pe):
                out_sums(pe, 0)
                out_block(pe, 0, 0)
                out_block(pe, 0, 1)

            @block.vector
            def _(dve):
                sums_inverse(dve, 0)
                add_block(dve, 0, 0)
                add_block(dve, 0, 1)
        clear_signals(nc, S)



def load_all(nc, W, C_tile, X):
    with ExitStack() as ctx:
        S = signals(nc, ctx, "inputs_loaded")
        with nc.Block() as block:

            @block.sync
            def _(sp):
                sp.dma_start(X[:], W["L0_attn_a_hidden_states"].rearrange("b (t p) d -> p (b t) d", p=P))\
                    .then_inc(S["inputs_loaded"], 16)
                sp.dma_start(C_tile[:], W["f32_consts"]).then_inc(S["inputs_loaded"], 16)
                sp.wait_ge(S["inputs_loaded"], 32)
        clear_signals(nc, S)


def store_all(nc, out, X):
    with ExitStack() as ctx:
        S = signals(nc, ctx, "output_stored")
        with nc.Block() as block:

            @block.sync
            def _(sp):
                sp.dma_start(out.rearrange("b (t p) d -> p (b t) d", p=P), X[:]).then_inc(S["output_stored"], 16)
                sp.wait_ge(S["output_stored"], 16)


STAGES = {
    "delta": delta_block,
    "ternary": ternary_layer,
    "chunks": chunk_attention,
    "sparse": sparse_attention,
    "local": local_layers,
    "global": grouped_attention,
}


def build_program(nc, W, out, stages):
    with ExitStack() as ctx:
        X = ctx.enter_context(nc.sbuf_tensor("X", [P, TILES, DIM], F32))
        C_tile = ctx.enter_context(nc.sbuf_tensor("C_tile", [P, 4, P], F32))
        C = {name: C_tile[:, i, :] for i, name in enumerate(["ident", "upto", "after", "ones"])}
        load_all(nc, W, C_tile, X)
        for i, stage in enumerate(stages):
            STAGES[stage](nc, W, C, X, f"{stage}{i}")
        store_all(nc, out, X)


ORDER = ["delta", "ternary", "chunks", "ternary", "sparse", "local", "global", "local"]


def kernel(**inputs):
    import concourse.bacc as bacc
    from concourse.bass_utils import run_bass_kernel_spmd

    nc = bacc.Bacc("TRN2", target_bir_lowering=False, num_devices=1)
    arrays, W = {}, {}
    f32_consts, tri_masks = shape_constants()
    extra = {"f32_consts": f32_consts, "tri_masks": tri_masks, **table_constants()}
    for name, a in {**inputs, **extra}.items():
        a = np.ascontiguousarray(a)
        arrays[f"in_{name}"] = a
        W[name] = nc.dram_tensor(f"in_{name}", a.shape, mybir.dt.from_np(a.dtype), kind="ExternalInput").ap()
    out = nc.dram_tensor("out_x", (1, TOKENS, DIM), F32, kind="ExternalOutput").ap()
    build_program(nc, W, out, ORDER)
    r = run_bass_kernel_spmd(nc, [arrays], core_ids=[0])
    return r.results[0]["out_x"]
```
